# Optimizing a Trainium2 kernel written in Bass

```python
import numpy as np
import jax
import jax.numpy as jnp

def _softmax(x, axis=-1):
    return jax.nn.softmax(x, axis=axis)

def _gelu(x):
    return jax.nn.gelu(x, approximate=True)

def _silu(x):
    return jax.nn.silu(x)

def _sigmoid(x):
    return jax.nn.sigmoid(x)

def _layernorm(x, axis=-1, eps=1e-05):
    m = jnp.mean(x, axis=axis, keepdims=True)
    v = jnp.var(x, axis=axis, keepdims=True)
    return (x - m) / jnp.sqrt(v + eps)

def _scatter_add(tgt, idx, src, axis=0):
    return tgt.at[idx].add(src)

def _segment_sum(src, seg, n):
    return jax.ops.segment_sum(src, seg, n)
kernel_name = 'mk_lm_tower_d2_tok_ids1024_r4_c57035'

def setup_inputs(seed: int=0):
    np.random.seed(seed)
    _w = jnp.asarray

    def _rec_inputs():
        import jax
        import jax.numpy as jnp
        _rk = jax.random.key(seed)
        x = jax.random.randint(jax.random.fold_in(_rk, 1), (32, 128), 0, 2048, jnp.int32)
        return x
    x = _rec_inputs()

    def _L0_tok_setup():
        import jax, jax.numpy as jnp
        import numpy as np
        CODEBOOK_SIZE = 2048
        CODEBOOK_DIM = 256
        HIDDEN_DIM = 1024
        OUT_DIM = 256
        B, M = (32, 144)
        key = jax.random.key(seed)
        k_idx, k_cb, k_w1, k_w2 = jax.random.split(key, 4)
        index = jax.random.randint(k_idx, (B, M), 0, CODEBOOK_SIZE, dtype=jnp.int32)
        codebook = CODEBOOK_DIM ** 0.5 * jax.random.normal(k_cb, (CODEBOOK_SIZE, CODEBOOK_DIM), dtype=jnp.float32)
        s1 = 1.0 / np.sqrt(CODEBOOK_DIM)
        s2 = 1.0 / np.sqrt(HIDDEN_DIM)
        W1 = s1 * jax.random.normal(k_w1, (CODEBOOK_DIM, HIDDEN_DIM), dtype=jnp.float32)
        b1 = jnp.zeros((HIDDEN_DIM,), dtype=jnp.float32)
        W2 = s2 * jax.random.normal(k_w2, (HIDDEN_DIM, OUT_DIM), dtype=jnp.float32)
        b2 = jnp.zeros((OUT_DIM,), dtype=jnp.float32)
        return {'index': index, 'codebook': codebook, 'W1': W1, 'b1': b1, 'W2': W2, 'b2': b2}
    _L0_tok_all = _L0_tok_setup()
    _L0_tok_in = {k: v for k, v in _L0_tok_all.items() if k in ('codebook', 'W1', 'b1', 'W2', 'b2')}
    del _L0_tok_all

    def _L0_attn_setup():
        import jax, jax.numpy as jnp
        import numpy as np
        B, N, D, H = (4, 512, 256, 16)
        DH = D // H
        EPS = 1e-05
        key = jax.random.key(seed)
        k1, k2, k3, k4 = jax.random.split(key, 4)
        return {'x': jax.random.normal(k1, (B, N, D), dtype=jnp.float32), 'g_ln': jnp.ones((D,), dtype=jnp.float32), 'Wq': jax.random.normal(k2, (D, D), dtype=jnp.float32) * 0.02, 'Wkv': jax.random.normal(k3, (D, 2 * D), dtype=jnp.float32) * 0.02, 'Wo': jax.random.normal(k4, (D, D), dtype=jnp.float32) * 0.02}
    _L0_attn_all = _L0_attn_setup()
    _L0_attn_in = {k: v for k, v in _L0_attn_all.items() if k in ('g_ln', 'Wq', 'Wkv', 'Wo')}
    del _L0_attn_all

    def _L0_ffn_setup():
        import jax, jax.numpy as jnp
        import numpy as np
        DIM = 256
        INTER = 256
        N_EXPERTS = 8
        TOPK = 2
        N_SHARED = 2
        key = jax.random.key(seed)
        ks = jax.random.split(key, 10)
        s = 0.02
        return {'x': jax.random.normal(ks[0], (4, 512, DIM), dtype=jnp.float32), 'gate_w': jax.random.normal(ks[1], (N_EXPERTS, DIM), dtype=jnp.float32) * s, 'gate_bias': jax.random.normal(ks[2], (N_EXPERTS,), dtype=jnp.float32) * s, 'w1': jax.random.normal(ks[3], (N_EXPERTS, INTER, DIM), dtype=jnp.float32) * s, 'w3': jax.random.normal(ks[4], (N_EXPERTS, INTER, DIM), dtype=jnp.float32) * s, 'w2': jax.random.normal(ks[5], (N_EXPERTS, DIM, INTER), dtype=jnp.float32) * s, 'sw1': jax.random.normal(ks[6], (N_SHARED * INTER, DIM), dtype=jnp.float32) * s, 'sw3': jax.random.normal(ks[7], (N_SHARED * INTER, DIM), dtype=jnp.float32) * s, 'sw2': jax.random.normal(ks[8], (DIM, N_SHARED * INTER), dtype=jnp.float32) * s}
    _L0_ffn_all = _L0_ffn_setup()
    _L0_ffn_in = {k: v for k, v in _L0_ffn_all.items() if k in ('gate_w', 'gate_bias', 'w1', 'w3', 'w2', 'sw1', 'sw3', 'sw2')}
    del _L0_ffn_all

    def _L1_attn_setup():
        import jax, jax.numpy as jnp
        import numpy as np
        import math
        N_EMBD = 256
        N_HEAD = 16
        HEAD_DIM = N_EMBD // N_HEAD
        B, T = (2, 512)
        LORA_RANK = 16
        LORA_SCALE = 32.0 / 16.0
        QMIN, QMAX = (0.0, 255.0)

        def round_ste(x):
            return x + jax.lax.stop_gradient(jnp.round(x) - x)

        def fake_quant(x, scale, zero_point):
            q = jnp.clip(round_ste(x / scale + zero_point), QMIN, QMAX)
            return (q - zero_point) * scale

        def lora_linear(x, w, b, la, lb):
            return x @ w + b + LORA_SCALE * (x @ la @ lb)
        key = jax.random.key(seed)
        ks = jax.random.split(key, 10)
        std = 0.02
        hidden_states = jax.random.normal(ks[0], (B, T, N_EMBD), dtype=jnp.float32)
        w_attn = jax.random.normal(ks[1], (N_EMBD, 3 * N_EMBD), dtype=jnp.float32) * std
        b_attn = jnp.zeros((3 * N_EMBD,), dtype=jnp.float32)
        la_attn = jax.random.normal(ks[2], (N_EMBD, LORA_RANK), dtype=jnp.float32) * std
        lb_attn = jnp.zeros((LORA_RANK, 3 * N_EMBD), dtype=jnp.float32)
        w_proj = jax.random.normal(ks[3], (N_EMBD, N_EMBD), dtype=jnp.float32) * std
        b_proj = jnp.zeros((N_EMBD,), dtype=jnp.float32)
        la_proj = jax.random.normal(ks[4], (N_EMBD, LORA_RANK), dtype=jnp.float32) * std
        lb_proj = jnp.zeros((LORA_RANK, N_EMBD), dtype=jnp.float32)
        kv_scale = jnp.asarray(0.05, dtype=jnp.float32)
        kv_zero_point = jnp.asarray(128.0, dtype=jnp.float32)
        return {'hidden_states': hidden_states, 'w_attn': w_attn, 'b_attn': b_attn, 'la_attn': la_attn, 'lb_attn': lb_attn, 'w_proj': w_proj, 'b_proj': b_proj, 'la_proj': la_proj, 'lb_proj': lb_proj, 'kv_scale': kv_scale, 'kv_zero_point': kv_zero_point}
    _L1_attn_all = _L1_attn_setup()
    _L1_attn_in = {k: v for k, v in _L1_attn_all.items() if k in ('w_attn', 'b_attn', 'la_attn', 'lb_attn', 'w_proj', 'b_proj', 'la_proj', 'lb_proj', 'kv_scale', 'kv_zero_point')}
    del _L1_attn_all

    def _L1_ffn_setup():
        import jax, jax.numpy as jnp
        import numpy as np
        HIDDEN = 256
        INNER = 1024

        def _weight_quant(w):
            scale = 1.0 / jnp.clip(jnp.mean(jnp.abs(w)), 1e-05)
            wq = jnp.clip(jnp.round(w * scale), -1.0, 1.0) / scale
            return w + jax.lax.stop_gradient(wq - w)

        def _act_quant(x):
            scale = 127.0 / jnp.clip(jnp.max(jnp.abs(x), axis=-1, keepdims=True), 1e-05)
            xq = jnp.clip(jnp.round(x * scale), -128.0, 127.0) / scale
            return x + jax.lax.stop_gradient(xq - x)

        def _bitlinear(x, w):
            return jnp.einsum('bsi,oi->bso', _act_quant(x), _weight_quant(w))
        key = jax.random.key(seed)
        k0, k1, k2, k3 = jax.random.split(key, 4)
        x = jax.random.normal(k0, (4, 512, HIDDEN), dtype=jnp.float32)
        w_gate = jax.random.normal(k1, (INNER, HIDDEN), dtype=jnp.float32) / np.sqrt(HIDDEN)
        w_up = jax.random.normal(k2, (INNER, HIDDEN), dtype=jnp.float32) / np.sqrt(HIDDEN)
        w_down = jax.random.normal(k3, (HIDDEN, INNER), dtype=jnp.float32) / np.sqrt(INNER)
        return {'x': x, 'w_gate': w_gate, 'w_up': w_up, 'w_down': w_down}
    _L1_ffn_all = _L1_ffn_setup()
    _L1_ffn_in = {k: v for k, v in _L1_ffn_all.items() if k in ('w_gate', 'w_up', 'w_down')}
    del _L1_ffn_all
    return {'x': x, 'L0_tok_codebook': _L0_tok_in['codebook'], 'L0_tok_W1': _L0_tok_in['W1'], 'L0_tok_b1': _L0_tok_in['b1'], 'L0_tok_W2': _L0_tok_in['W2'], 'L0_tok_b2': _L0_tok_in['b2'], 'L0_attn_g_ln': _L0_attn_in['g_ln'], 'L0_attn_Wq': _L0_attn_in['Wq'], 'L0_attn_Wkv': _L0_attn_in['Wkv'], 'L0_attn_Wo': _L0_attn_in['Wo'], 'L0_ffn_gate_w': _L0_ffn_in['gate_w'], 'L0_ffn_gate_bias': _L0_ffn_in['gate_bias'], 'L0_ffn_w1': _L0_ffn_in['w1'], 'L0_ffn_w3': _L0_ffn_in['w3'], 'L0_ffn_w2': _L0_ffn_in['w2'], 'L0_ffn_sw1': _L0_ffn_in['sw1'], 'L0_ffn_sw3': _L0_ffn_in['sw3'], 'L0_ffn_sw2': _L0_ffn_in['sw2'], 'L1_attn_w_attn': _L1_attn_in['w_attn'], 'L1_attn_b_attn': _L1_attn_in['b_attn'], 'L1_attn_la_attn': _L1_attn_in['la_attn'], 'L1_attn_lb_attn': _L1_attn_in['lb_attn'], 'L1_attn_w_proj': _L1_attn_in['w_proj'], 'L1_attn_b_proj': _L1_attn_in['b_proj'], 'L1_attn_la_proj': _L1_attn_in['la_proj'], 'L1_attn_lb_proj': _L1_attn_in['lb_proj'], 'L1_attn_kv_scale': _L1_attn_in['kv_scale'], 'L1_attn_kv_zero_point': _L1_attn_in['kv_zero_point'], 'L1_ffn_w_gate': _L1_ffn_in['w_gate'], 'L1_ffn_w_up': _L1_ffn_in['w_up'], 'L1_ffn_w_down': _L1_ffn_in['w_down']}

def reference(x, L0_tok_codebook, L0_tok_W1, L0_tok_b1, L0_tok_W2, L0_tok_b2, L0_attn_g_ln, L0_attn_Wq, L0_attn_Wkv, L0_attn_Wo, L0_ffn_gate_w, L0_ffn_gate_bias, L0_ffn_w1, L0_ffn_w3, L0_ffn_w2, L0_ffn_sw1, L0_ffn_sw3, L0_ffn_sw2, L1_attn_w_attn, L1_attn_b_attn, L1_attn_la_attn, L1_attn_lb_attn, L1_attn_w_proj, L1_attn_b_proj, L1_attn_la_proj, L1_attn_lb_proj, L1_attn_kv_scale, L1_attn_kv_zero_point, L1_ffn_w_gate, L1_ffn_w_up, L1_ffn_w_down):
    import jax
    import jax.numpy as jnp

    def _L0_tok_ref(index, codebook, W1, b1, W2, b2):
        import jax, jax.numpy as jnp
        import numpy as np
        CODEBOOK_SIZE = 2048
        CODEBOOK_DIM = 256
        HIDDEN_DIM = 1024
        OUT_DIM = 256
        B, M = (32, 144)
        quantized = jnp.take(codebook, index, axis=0)
        h = jax.nn.gelu(jnp.einsum('bmd,dh->bmh', quantized, W1) + b1)
        rec = jnp.einsum('bmh,ho->bmo', h, W2) + b2
        return rec

    def _L0_attn_ref(x, g_ln, Wq, Wkv, Wo):
        import jax, jax.numpy as jnp
        import numpy as np
        B, N, D, H = (4, 512, 256, 16)
        DH = D // H
        EPS = 1e-05
        mu = jnp.mean(x, axis=-1, keepdims=True)
        var = jnp.mean(jnp.square(x - mu), axis=-1, keepdims=True)
        xn = (x - mu) * jax.lax.rsqrt(var + EPS) * g_ln
        b, n, d = xn.shape
        q = (xn @ Wq).reshape(b, n, H, DH).transpose(0, 2, 1, 3)
        kv = xn @ Wkv
        k, v = jnp.split(kv, 2, axis=-1)
        k = k.reshape(b, n, H, DH).transpose(0, 2, 1, 3)
        v = v.reshape(b, n, H, DH).transpose(0, 2, 1, 3)
        scale = DH ** (-0.5)
        dots = jnp.einsum('bhid,bhjd->bhij', q, k) * scale
        mask_value = -jnp.finfo(dots.dtype).max
        causal = jnp.triu(jnp.ones((n, n), dtype=bool), k=1)
        dots = jnp.where(causal, mask_value, dots)
        attn = jax.nn.softmax(dots.astype(jnp.float32), axis=-1).astype(dots.dtype)
        out = jnp.einsum('bhij,bhjd->bhid', attn, v)
        out = out.transpose(0, 2, 1, 3).reshape(b, n, d)
        return out @ Wo

    def _L0_ffn_ref(x, gate_w, gate_bias, w1, w3, w2, sw1, sw3, sw2):
        import jax, jax.numpy as jnp
        import numpy as np
        DIM = 256
        INTER = 256
        N_EXPERTS = 8
        TOPK = 2
        N_SHARED = 2
        shape = x.shape
        xt = x.reshape(-1, shape[-1])
        scores = jax.nn.softmax((xt @ gate_w.T).astype(jnp.float32), axis=-1)
        _, idx = jax.lax.top_k(scores + gate_bias, TOPK)
        weights = jnp.take_along_axis(scores, idx, axis=1).astype(x.dtype)
        y = jnp.zeros_like(xt)
        for e in range(N_EXPERTS):
            gate_e = jnp.sum(jnp.where(idx == e, weights, 0.0), axis=1)
            h = jax.nn.silu(xt @ w1[e].T) * (xt @ w3[e].T)
            y = y + gate_e[:, None] * (h @ w2[e].T)
        z = jax.nn.silu(xt @ sw1.T) * (xt @ sw3.T) @ sw2.T
        return (y + z).reshape(shape)

    def _L1_attn_ref(hidden_states, w_attn, b_attn, la_attn, lb_attn, w_proj, b_proj, la_proj, lb_proj, kv_scale, kv_zero_point):
        import jax, jax.numpy as jnp
        import numpy as np
        import math
        N_EMBD = 256
        N_HEAD = 16
        HEAD_DIM = N_EMBD // N_HEAD
        B, T = (2, 512)
        LORA_RANK = 16
        LORA_SCALE = 32.0 / 16.0
        QMIN, QMAX = (0.0, 255.0)

        def round_ste(x):
            return x + jax.lax.stop_gradient(jnp.round(x) - x)

        def fake_quant(x, scale, zero_point):
            q = jnp.clip(round_ste(x / scale + zero_point), QMIN, QMAX)
            return (q - zero_point) * scale

        def lora_linear(x, w, b, la, lb):
            return x @ w + b + LORA_SCALE * (x @ la @ lb)
        Bn, Tn, C = hidden_states.shape
        qkv = lora_linear(hidden_states, w_attn, b_attn, la_attn, lb_attn)
        q, k, v = jnp.split(qkv, 3, axis=2)

        def to_heads(x):
            return x.reshape(Bn, Tn, N_HEAD, HEAD_DIM).transpose(0, 2, 1, 3)
        q, k, v = (to_heads(q), to_heads(k), to_heads(v))
        k = fake_quant(k, kv_scale, kv_zero_point)
        v = fake_quant(v, kv_scale, kv_zero_point)
        scores = jnp.einsum('bhqd,bhkd->bhqk', q, k) / math.sqrt(HEAD_DIM)
        causal = jnp.tril(jnp.ones((Tn, Tn), dtype=bool))
        scores = jnp.where(causal, scores, -jnp.inf)
        attn = jax.nn.softmax(scores, axis=-1)
        out = jnp.einsum('bhqk,bhkd->bhqd', attn, v)
        out = out.transpose(0, 2, 1, 3).reshape(Bn, Tn, C)
        return lora_linear(out, w_proj, b_proj, la_proj, lb_proj)

    def _L1_ffn_ref(x, w_gate, w_up, w_down):
        import jax, jax.numpy as jnp
        import numpy as np
        HIDDEN = 256
        INNER = 1024

        def _weight_quant(w):
            scale = 1.0 / jnp.clip(jnp.mean(jnp.abs(w)), 1e-05)
            wq = jnp.clip(jnp.round(w * scale), -1.0, 1.0) / scale
            return w + jax.lax.stop_gradient(wq - w)

        def _act_quant(x):
            scale = 127.0 / jnp.clip(jnp.max(jnp.abs(x), axis=-1, keepdims=True), 1e-05)
            xq = jnp.clip(jnp.round(x * scale), -128.0, 127.0) / scale
            return x + jax.lax.stop_gradient(xq - x)

        def _bitlinear(x, w):
            return jnp.einsum('bsi,oi->bso', _act_quant(x), _weight_quant(w))
        gate = jax.nn.silu(_bitlinear(x, w_gate))
        up = _bitlinear(x, w_up)
        return _bitlinear(gate * up, w_down)
    h = _L0_tok_ref(x, L0_tok_codebook, L0_tok_W1, L0_tok_b1, L0_tok_W2, L0_tok_b2)
    h = h + _L0_attn_ref(_layernorm(h, axis=-1), L0_attn_g_ln, L0_attn_Wq, L0_attn_Wkv, L0_attn_Wo)
    h = h + _L0_ffn_ref(_layernorm(h, axis=-1), L0_ffn_gate_w, L0_ffn_gate_bias, L0_ffn_w1, L0_ffn_w3, L0_ffn_w2, L0_ffn_sw1, L0_ffn_sw3, L0_ffn_sw2)
    h = h + _L1_attn_ref(_layernorm(h, axis=-1), L1_attn_w_attn, L1_attn_b_attn, L1_attn_la_attn, L1_attn_lb_attn, L1_attn_w_proj, L1_attn_b_proj, L1_attn_la_proj, L1_attn_lb_proj, L1_attn_kv_scale, L1_attn_kv_zero_point)
    h = h + _L1_ffn_ref(_layernorm(h, axis=-1), L1_ffn_w_gate, L1_ffn_w_up, L1_ffn_w_down)
    return h

_drawn_inputs = setup_inputs


def setup_inputs(seed=0):
    import zlib

    import numpy as np

    out = dict(_drawn_inputs(seed))
    spreads = {'L0_tok_b1': (0.0, 0.8),
     'L0_tok_b2': (0.0, 0.8),
     'L0_attn_g_ln': (1.0, 0.6),
     'L1_attn_b_attn': (0.0, 0.8),
     'L1_attn_lb_attn': (0.0, 0.8),
     'L1_attn_b_proj': (0.0, 0.8),
     'L1_attn_lb_proj': (0.0, 0.8)}
    factors = {'L0_attn_Wq': 8.0,
     'L0_attn_Wkv': 8.0,
     'L0_attn_Wo': 8.0,
     'L0_ffn_gate_w': 8.0,
     'L0_ffn_gate_bias': 8.0,
     'L0_ffn_w1': 8.0,
     'L0_ffn_w3': 8.0,
     'L0_ffn_w2': 8.0,
     'L0_ffn_sw1': 8.0,
     'L0_ffn_sw3': 8.0,
     'L0_ffn_sw2': 8.0,
     'L1_attn_w_attn': 8.0,
     'L1_attn_la_attn': 8.0,
     'L1_attn_w_proj': 6.441,
     'L1_attn_la_proj': 7.555,
     'L1_ffn_w_gate': 4.032,
     'L1_ffn_w_up': 3.803,
     'L1_ffn_w_down': 3.878}
    for name, (base, spread) in spreads.items():
        noise = np.random.default_rng([zlib.crc32(name.encode()), seed]).standard_normal(out[name].shape)
        drawn = base * np.exp(spread * noise) if base else spread * noise
        out[name] = jnp.asarray(drawn.astype(out[name].dtype))
    for name, factor in factors.items():
        out[name] = (out[name] * factor).astype(out[name].dtype)
    return out
```

```python
from contextlib import ExitStack

import concourse.bass as bass
from concourse import mybir

F32 = mybir.dt.float32
BF16 = mybir.dt.bfloat16
U32 = mybir.dt.uint32
I32 = mybir.dt.int32
ALU = mybir.AluOpType
ACT = mybir.ActivationFunctionType
AX = mybir.AxisListType

P = 128
D = 256
KD = D // P
H = 16
DH = D // H
HPB = P // DH
SLOT = 32
EPS = 1e-5
ROUND = 1.5 * 2.0 ** 23
MASKED = -1e30
BIG = 1e30


def head_at(pos):
    r, b, eo = pos // 4, pos // 2 % 2, pos % 2
    return HPB * b + 2 * r + eo


def build(nc, x_t, codebook_t, tok_w1, tok_b1, tok_w2, tok_b2,
          g_ln, w_qkv0, w_out0, gate_wt, gate_bias, w13, w2,
          w_qkv1, b_qk, b_v, la_attn_t, lb_attn, w_proj, b_proj, la_proj_t, lb_proj, kv_scale, kv_zero,
          w_gu, w_down, ident_in, causal_in, slot_in, rank_in, out):
    SEQ = x_t.shape[1]
    ROWS = codebook_t.shape[1]
    HID = tok_w1.shape[1]
    E = gate_wt.shape[1]
    EA = w13.shape[0]
    INTER = w2.shape[1]
    INNER = w_down.shape[0]
    RANK = la_attn_t.shape[0]
    KH, KI, KN = HID // P, INTER // P, INNER // P
    GS = 4
    GT = GS * P
    G = SEQ // GS
    TG = ROWS // 512

    table = nc.dram_tensor("token_table", (ROWS, D), F32).ap()

    with ExitStack() as ctx:
        def sb(name, shape, dt=F32, at=None):
            return (at or ctx).enter_context(nc.sbuf_tensor(name, shape, dt))

        def sem(name):
            return ctx.enter_context(nc.semaphore(name))

        PS = ctx.enter_context(nc.psum_tensor("banks", [P, 8, 512], F32))

        resid = sb("resid", [P, SEQ, D])
        ident = sb("ident", [P, P])
        ident_b = sb("ident_b", [P, P], BF16)
        causal = sb("causal", [P, P])
        causal_b = sb("causal_b", [P, 4, P], BF16)
        slot = sb("slot", [P, 2])
        ones = sb("ones", [P, P])
        minus_half = sb("minus_half", [P, GS])
        idx = sb("idx", [P, SEQ], I32)
        wqkv = [sb(f"wqkv{i}", [P, KD, 3 * D]) for i in range(2)]
        wout = [sb(f"wout{i}", [P, KD, D]) for i in range(2)]
        gln = sb("gln", [P, KD])
        bqk = sb("bqk", [P, 4])
        bq_scaled = sb("bq_scaled", [P, KD])
        bv = sb("bv", [P, D])
        bproj = sb("bproj", [P, D])
        kvs = sb("kvs", [P, 1])
        kvz = sb("kvz", [P, 1])
        kvinv = sb("kvinv", [P, 1])
        gw = sb("gw", [P, KD, E])
        gbias = sb("gbias", [P, E])
        rank = sb("rank", [P, E])
        w13_sb = sb("w13_sb", [P, EA, KD, 2 * INTER])
        w2_sb = sb("w2_sb", [P, EA, KI, D])
        wgu_q = sb("wgu_q", [P, KD, 2 * INNER], BF16)
        wdn_q = sb("wdn_q", [P, KN, D], BF16)
        wabs = sb("wabs", [P, 4])
        wmean = sb("wmean", [P, 4])
        wscale = sb("wscale", [P, 4])
        winv = sb("winv", [P, 4])

        with ExitStack() as t_:
            cb = sb("cb", [P, KD, ROWS], at=t_)
            tw1 = sb("tw1", [P, KD, HID], at=t_)
            tw2 = sb("tw2", [P, KH, D], at=t_)
            tb1 = sb("tb1", [P, KH], at=t_)
            tb2 = sb("tb2", [P, D], at=t_)
            thid = sb("thid", [P, KH, 512], at=t_)
            trow = sb("trow", [P, 4, D], at=t_)
            la1 = sb("la1", [RANK, D], at=t_)
            lb1 = sb("lb1", [RANK, 3 * D], at=t_)
            la2 = sb("la2", [RANK, D], at=t_)
            lb2 = sb("lb2", [RANK, D], at=t_)
            wst = sb("wst", [P, 2 * INNER], at=t_)
        with ExitStack() as a_:
            stats = sb("stats", [P, 6], at=a_)
            mv = sb("mv", [P, 4, 2], at=a_)
            varp = sb("varp", [P, 2], at=a_)
            rstd = sb("rstd", [P, 2], at=a_)
            xn = sb("xn", [P, D], at=a_)
            xT = sb("xT", [P, KD, P], at=a_)
            qT = sb("qT", [P, 2, KD, P], at=a_)
            kq = sb("kq", [P, KD, P], at=a_)
            kT = sb("kT", [P, 2, KD, 2, P], at=a_)
            vq = sb("vq", [P, D], at=a_)
            V = sb("V", [P, 2, H, SLOT], at=a_)
            prob = sb("prob", [P, 2, H, P], at=a_)
            probT = sb("probT", [P, H, P], at=a_)
            rmax = sb("rmax", [P, H], at=a_)
            rden = sb("rden", [P, H], at=a_)
            oraw = sb("oraw", [P, 4, P], at=a_)
            onrm = sb("onrm", [P, D], at=a_)
            oT = sb("oT", [P, KD, P], at=a_)
        with ExitStack() as m_:
            mstats = sb("mstats", [P, GS, 6], at=m_)
            mmv = sb("mmv", [P, GS, 2], at=m_)
            mvar = sb("mvar", [P, GS], at=m_)
            mrstd = sb("mrstd", [P, GS], at=m_)
            mxn = sb("mxn", [P, GS, D], at=m_)
            mxT = sb("mxT", [P, 2, KD, GT], at=m_)
            hT = sb("hT", [P, 2, KI, GT], at=m_)
            tnh = sb("tnh", [P, 2, GT], at=m_)
            act_ = sb("act_", [P, 2, GT], at=m_)
            gates = sb("gates", [P, 2, GS, EA], at=m_)
            r8 = [sb(f"r8_{i}", [P, GS, E], at=m_) for i in range(6)]
            r1 = [sb(f"r1_{i}", [P, GS], at=m_) for i in range(6)]
        with ExitStack() as f_:
            fstats = sb("fstats", [P, 6], at=f_)
            fmv = sb("fmv", [P, 2], at=f_)
            fvar = sb("fvar", [P, 2], at=f_)
            frstd = sb("frstd", [P, 2], at=f_)
            fxn = sb("fxn", [P, D], at=f_)
            fq = sb("fq", [P, D], at=f_)
            fqb = sb("fqb", [P, 2, D], BF16, at=f_)
            fxT = sb("fxT", [P, KD, P], BF16, at=f_)
            fs = sb("fs", [P, 2, 8], at=f_)
            ft = sb("ft", [P, INNER], at=f_)
            fp = sb("fp", [P, INNER], at=f_)
            fpq = sb("fpq", [P, INNER], at=f_)
            fpb = sb("fpb", [P, 2, INNER], BF16, at=f_)
            fpT = sb("fpT", [P, KN, P], BF16, at=f_)

        tok_in, idx_in, attn_in, exp_in, ffn_in = (sem(f"{n}_loaded") for n in ("tok", "idx", "attn", "experts", "ffn"))
        consts = sem("consts_ready")
        prep = sem("prep_step")
        lora_psum = sem("lora_psum")
        lora_added = sem("lora_added")
        wsum_psum = sem("wsum_psum")
        weights_ready = sem("weights_ready")
        wst_summed = sem("wst_summed")
        wst_quantized = sem("wst_quantized")
        t_hid_psum, t_hid, t_row_psum, t_row = (sem(n) for n in ("t_hid_psum", "t_hid", "t_row_psum", "t_row"))
        t_store = [sem(f"table_stored{b}") for b in range(4)]
        gathered = [sem(f"gathered{b}") for b in range(2)]
        names = ("stats aggr var rstd xn xT_psum xT qk_psum q k kchain v_psum v_ones v vchain s_psum rmax shifted prob pT_psum pT"
                 " o_psum oraw o2_psum rden onrm oT_psum oT y_psum resid biased").split()
        A = [{n: sem(f"a{i}_{n}") for n in names} for i in range(2)]
        M = {n: sem(f"m_{n}") for n in ("stats aggr var rstd xn xT_psum xT route_psum route_exp route_max router gates"
                                        " up_psum tanh half hT down_psum resid").split()}
        F = {n: sem(f"f_{n}") for n in ("stats aggr var rstd chain pchain pround fscale q q_psum xT up_psum tanh half prod scales pq pq_psum pT"
                                        " down_psum resid").split()}
        stored = sem("out_stored")

        def seen(eng, s, i, k=1, per=1, n=SEQ):
            if isinstance(i, int) and not 0 <= i < n:
                return
            eng.wait_ge(s, i * per + k)

        def has(i, n=SEQ):
            return not isinstance(i, int) or 0 <= i < n

        def row(t, i):
            return t[:, i] if isinstance(i, int) else t[:, bass.ds(i, 1)].rearrange("p a d -> p (a d)")

        def pair(i):
            return i // 2

        def spread(v, n):
            return v.unsqueeze(2).broadcast_to([P, v.shape[1], n])

        def skewed(eng, step, n, before, behind):
            first = behind
            last = (n - before - first) // 2 * 2 + first
            for s in range(-before, first):
                step(s, s % 2)
            with eng.Fori(0, (last - first) // 2, 1) as j:
                for b in range(2):
                    step(j * 2 + (first + b), (first + b) % 2)
            for s in range(last, n + behind):
                step(s, s % 2)

        block = ctx.enter_context(nc.Block())

        @block.sync
        def _(sp):
            def kt(a):
                return a.rearrange("(k p) n -> p k n", p=P)

            sp.dma_start(tw1[:], kt(tok_w1)).then_inc(tok_in, 16)
            sp.dma_start(cb[:], kt(codebook_t)).then_inc(tok_in, 16)
            sp.dma_start(tb1[:], tok_b1).then_inc(tok_in, 16)
            sp.dma_start(tw2[:], kt(tok_w2)).then_inc(tok_in, 16)
            sp.dma_start(tb2[:], tok_b2).then_inc(tok_in, 16)
            sp.dma_start(idx[:], x_t).then_inc(idx_in, 16)
            for dst, src in ((ident, ident_in), (causal, causal_in), (slot, slot_in), (gln, g_ln), (bqk, b_qk), (bv, b_v),
                             (bproj, b_proj), (kvs, kv_scale), (kvz, kv_zero), (gbias, gate_bias), (rank, rank_in),
                             (la1, la_attn_t), (lb1, lb_attn), (la2, la_proj_t), (lb2, lb_proj)):
                sp.dma_start(dst[:], src).then_inc(attn_in, 16)
            for dst, src in ((wqkv[0], w_qkv0), (wout[0], w_out0), (wqkv[1], w_qkv1), (wout[1], w_proj), (gw, gate_wt)):
                sp.dma_start(dst[:], kt(src)).then_inc(attn_in, 16)
            for n in range(2 * (KD + 1)):
                if 0 < n <= KD + 1:
                    sp.wait_ge(wst_summed, n)
                if n > KD + 1:
                    sp.wait_ge(wst_quantized, n - KD - 1)
                k = n % (KD + 1)
                if k < KD:
                    sp.dma_start(wst[:], w_gu[k * P:(k + 1) * P, :]).then_inc(ffn_in, 16)
                else:
                    sp.dma_start(wst[:].rearrange("p (k n) -> p k n", k=KN), kt(w_down)).then_inc(ffn_in, 16)
            for n in range(4 * TG):
                sp.wait_ge(t_row, n + 1)
                sp.dma_start(table[n * P:(n + 1) * P, :], trow[:, n % 4, :]).then_inc(t_store[n % 4], 16)
            for e in range(EA):
                sp.dma_start(w13_sb[:, e], kt(w13[e])).then_inc(exp_in, 16)
                sp.dma_start(w2_sb[:, e], kt(w2[e])).then_inc(exp_in, 16)
            with sp.Fori(0, SEQ, 1) as i:
                sp.wait_ge(F["resid"], i + 1)
                sp.dma_start(out[bass.ds(i, 1)].rearrange("a p d -> p (a d)"), row(resid, i)).then_inc(stored, 16)
            sp.wait_ge(stored, 16 * SEQ)

        ATTN_LOADS = 20 * 16

        @block.gpsimd
        def _(pool):
            pool.memset(minus_half[:], -0.5).then_inc(consts, 1)
            pool.memset(ones[:], 1.0).then_inc(consts, 1)
            pool.wait_ge(idx_in, 16)
            pool.wait_ge(consts, 1)
            for t in range(4):
                pool.wait_ge(t_store[t], 16 * TG)

            def gather(i):
                pool.indirect_dma_start(resid[:, i, :], None, table,
                                        bass.IndirectOffsetOnAxis(ap=idx[:, i:i + 1].bitcast(U32), axis=0)).then_inc(gathered[i % 2], 16)

            def attention(layer):
                a = A[layer]

                def step(s, b):
                    if layer == 0 and has(s + 4):
                        if has(s + 2):
                            pool.wait_ge(gathered[b], pair(s + 2) * 16 + 16)
                        gather(s + 4)
                    if has(s + 2):
                        seen(pool, a["var"], s + 2)
                        seen(pool, a["xn"], s)
                        pool.tensor_tensor(rstd[:, b:b + 1], varp[:, b:b + 1], minus_half[:, 0:1], ALU.pow).then_inc(a["rstd"], 1)
                    if layer == 1 and has(s):
                        seen(pool, a["xn"], s)
                        pool.tensor_tensor(row(resid, s), row(resid, s), bproj[:], ALU.add).then_inc(a["biased"], 1)

                if layer == 0:
                    for s in range(-4, SEQ):
                        step(s, s % 2)
                else:
                    skewed(pool, step, SEQ, 2, 0)

            attention(0)
            for g in range(G):
                pool.wait_ge(M["var"], g + 1)
                if g:
                    pool.wait_ge(M["xn"], GS * g)
                pool.tensor_tensor(mrstd[:], mvar[:], minus_half[:], ALU.pow).then_inc(M["rstd"], 1)
            attention(1)

            def ffn_step(s, b):
                if has(s):
                    seen(pool, F["var"], s)
                    pool.tensor_tensor(frstd[:, b:b + 1], fvar[:, b:b + 1], minus_half[:, 0:1], ALU.pow).then_inc(F["rstd"], 1)

            skewed(pool, ffn_step, SEQ, 0, 0)

        @block.tensor
        def _(pe):
            def prepare():
                pe.wait_ge(attn_in, ATTN_LOADS)
                for n, (la, lb, k, lo, hi) in enumerate(((la1, lb1, 0, 0, 512), (la1, lb1, 0, 512, 768),
                                                         (la1, lb1, 1, 0, 512), (la1, lb1, 1, 512, 768),
                                                         (la2, lb2, 0, 0, 256), (la2, lb2, 1, 0, 256))):
                    if n >= 3:
                        pe.wait_ge(lora_added, n - 2)
                    pe.matmul(PS[:, 4 + n % 3, 0:hi - lo], la[:, k * P:(k + 1) * P], lb[:, lo:hi], start=True, stop=True).then_inc(lora_psum, 1)
                pe.wait_ge(consts, 2)
                pe.wait_ge(wst_summed, 3)
                pe.matmul(PS[:, 7, 0:4], ones[:], wabs[:], start=True, stop=True).then_inc(wsum_psum, 1)

            pe.wait_ge(tok_in, 80)
            for t in range(TG):
                for m in range(KH):
                    n = t * KH + m
                    if n >= 2:
                        pe.wait_ge(t_hid, n - 1)
                    for k in range(KD):
                        mm = pe.matmul(PS[:, n % 2], tw1[:, k, m * P:(m + 1) * P], cb[:, k, t * 512:(t + 1) * 512],
                                       start=(k == 0), stop=(k == KD - 1))
                    mm.then_inc(t_hid_psum, 1)
                pe.wait_ge(t_hid, (t + 1) * KH)
                for r in range(4):
                    n = t * 4 + r
                    if n >= 2:
                        pe.wait_ge(t_row, n - 1)
                    for k in range(KH):
                        mm = pe.matmul(PS[:, 2 + n % 2, 0:D], thid[:, k, r * P:(r + 1) * P], tw2[:, k, :],
                                       start=(k == 0), stop=(k == KH - 1))
                    mm.then_inc(t_row_psum, 1)
                if t == 0:
                    prepare()

            def attention(layer):
                a = A[layer]
                pe.wait_ge(weights_ready, 1)
                if layer == 0:
                    pe.wait_ge(t_row, 4 * TG)
                else:
                    pe.wait_ge(M["resid"], G * EA * GS)

                def o_turn(s):
                    if has(s):
                        seen(pe, a["oraw"], s)
                        seen(pe, a["resid"], s - 1)
                        seen(pe, a["v"], s + 2)
                        for t in range(4):
                            mm = pe.transpose(PS[:, 7, t * P:(t + 1) * P], oraw[:, t, :], ident[:])
                        mm.then_inc(a["o2_psum"], 1)

                def scores(s, b):
                    if has(s):
                        seen(pe, a["q"], s)
                        seen(pe, a["k"], s)
                        seen(pe, a["shifted"], s - 1)
                        for r in range(4):
                            pe.matmul(PS[:, r, :], ident_b[:], causal_b[:].rearrange("p a k -> p (a k)"), start=True, stop=False,
                                      skip_group_check=True)
                        for kb in range(KD):
                            for r in range(4):
                                rows = slice(SLOT * r, SLOT * (r + 1))
                                mm = pe.matmul(PS[:, r, kb * 256:(kb + 1) * 256], qT[rows, b, kb, :],
                                               kT[rows, b, kb].rearrange("p e k -> p (e k)"), start=False, stop=(kb == 1),
                                               tile_position=(SLOT * r, 0), skip_group_check=True)
                        mm.then_inc(a["s_psum"], 1)

                def x_turn(s):
                    if has(s):
                        seen(pe, a["xn"], s)
                        seen(pe, a["q"], s - 1)
                        seen(pe, a["k"], s - 1)
                        for k in range(KD):
                            mm = pe.transpose(PS[:, 6, k * P:(k + 1) * P], xn[:, k * P:(k + 1) * P], ident[:])
                        mm.then_inc(a["xT_psum"], 1)

                def on_turn(s):
                    if has(s):
                        seen(pe, a["onrm"], s)
                        for k in range(KD):
                            mm = pe.transpose(PS[:, 7, k * P:(k + 1) * P], onrm[:, k * P:(k + 1) * P], ident[:])
                        mm.then_inc(a["oT_psum"], 1)

                def p_turn(s, b):
                    if has(s):
                        seen(pe, a["prob"], s)
                        for r in range(4):
                            if r < 2:
                                seen(pe, a["oraw"], s - 1)
                                seen(pe, a["pT"], s - 1, 4, 4)
                            else:
                                seen(pe, a["pT"], s, r - 1, 4)
                            for c in range(4):
                                mm = pe.transpose(PS[:, 4 + r % 2, c * P:(c + 1) * P], prob[:, b, 4 * r + c, :], ident[:])
                            mm.then_inc(a["pT_psum"], 1)

                def project(s):
                    if has(s):
                        seen(pe, a["xT"], s)
                        for n in range(4):
                            for k in range(KD):
                                mm = pe.matmul(PS[:, 6, n * P:(n + 1) * P], wqkv[layer][:, k, n * P:(n + 1) * P], xT[:, k, :],
                                               start=(k == 0), stop=(k == KD - 1))
                        mm.then_inc(a["qk_psum"], 1)
                        seen(pe, a["oT"], s - 3)
                        seen(pe, a["v"], s - 1)
                        for k in range(KD):
                            mm = pe.matmul(PS[:, 7, 0:D], xT[:, k, :], wqkv[layer][:, k, 2 * D:3 * D],
                                           start=(k == 0), stop=(k == KD - 1))
                        mm.then_inc(a["v_psum"], 1)

                def pv(s, b):
                    if has(s):
                        seen(pe, a["v"], s)
                        seen(pe, a["pT"], s, 4, 4)
                        for t in range(4):
                            for c in range(4):
                                mm = pe.matmul(PS[SLOT * c:SLOT * (c + 1), 4, t * P:(t + 1) * P], V[:, b, 4 * t + c, :],
                                               probT[:, 4 * t + c, :], start=True, stop=True, tile_position=(0, SLOT * c))
                        mm.then_inc(a["o_psum"], 1)

                def out_proj(s):
                    if has(s):
                        seen(pe, a["oT"], s)
                        seen(pe, a["v"], s + 3)
                        for k in range(KD):
                            mm = pe.matmul(PS[:, 7, 0:D], oT[:, k, :], wout[layer][:, k, :], start=(k == 0), stop=(k == KD - 1))
                        mm.then_inc(a["y_psum"], 1)

                def step(s, b):
                    o_turn(s - 2)
                    scores(s, b)
                    x_turn(s + 1)
                    on_turn(s - 2)
                    p_turn(s - 1, 1 - b)
                    project(s + 1)
                    pv(s - 1, 1 - b)
                    out_proj(s - 2)

                skewed(pe, step, SEQ, 1, 2)

            attention(0)

            pe.wait_ge(A[0]["resid"], SEQ)
            pe.wait_ge(exp_in, 2 * EA * 16)

            def xn_turn(g, b):
                if has(g, G):
                    seen(pe, M["xn"], g, GS, GS, G)
                    seen(pe, M["router"], g - 1, 1, 1, G)
                    for k in range(KD):
                        for t in range(GS):
                            mm = pe.transpose(PS[:, 6 + k, t * P:(t + 1) * P], mxn[:, t, k * P:(k + 1) * P], ident[:])
                        mm.then_inc(M["xT_psum"], 1)

            def route(g, b):
                if has(g, G):
                    seen(pe, M["xT"], g, KD, KD, G)
                    for t in range(GS):
                        for k in range(KD):
                            mm = pe.matmul(PS[:, 6, t * E:(t + 1) * E], mxT[:, b, k, t * P:(t + 1) * P], gw[:, k, :],
                                           start=(k == 0), stop=(k == KD - 1))
                    mm.then_inc(M["route_psum"], 1)

            def up(g, b, e):
                for h in range(KI):
                    if e:
                        seen(pe, M["hT"], g, (e - 1) * KI + h + 1, EA * KI, G)
                    else:
                        seen(pe, M["hT"], g - 1, (EA - 1) * KI + h + 1, EA * KI, G)
                    for u in range(2):
                        for k in range(KD):
                            mm = pe.matmul(PS[:, 2 * h + u], w13_sb[:, e, k, u * INTER + h * P:u * INTER + (h + 1) * P],
                                           mxT[:, b, k, :], start=(k == 0), stop=(k == KD - 1))
                    mm.then_inc(M["up_psum"], 1)

            def down(g, e):
                seen(pe, M["hT"], g, (e + 1) * KI, EA * KI, G)
                for t in range(GS):
                    if t % 2 == 0:
                        if e:
                            seen(pe, M["resid"], g, (e - 1) * GS + t + 2, EA * GS, G)
                        else:
                            seen(pe, M["resid"], g - 1, (EA - 1) * GS + t + 2, EA * GS, G)
                    for k in range(KI):
                        mm = pe.matmul(PS[:, 4 + t // 2, t % 2 * D:(t % 2 + 1) * D], hT[:, e % 2, k, t * P:(t + 1) * P],
                                       w2_sb[:, e, k, :], start=(k == 0), stop=(k == KI - 1), skip_group_check=True)
                    if t % 2:
                        mm.then_inc(M["down_psum"], 1)

            def expert_step(g, b):
                if has(g, G):
                    for e in range(EA):
                        up(g, b, e)
                        if e:
                            down(g, e - 1)
                        if e == EA - 2:
                            xn_turn(g + 1, 1 - b)
                        if e == EA - 1:
                            route(g + 1, 1 - b)
                    down(g, EA - 1)
                else:
                    xn_turn(g + 1, 1 - b)
                    route(g + 1, 1 - b)

            skewed(pe, expert_step, G, 1, 1)

            attention(1)

            pe.wait_ge(A[1]["resid"], SEQ)

            def q_turn(s, b):
                if has(s):
                    seen(pe, F["q"], s)
                    seen(pe, F["xT"], s - 1)
                    for k in range(KD):
                        mm = pe.transpose(PS[:, 4].bitcast(BF16)[:, k * P:(k + 1) * P], fqb[:, b, k * P:(k + 1) * P], ident_b[:])
                    mm.then_inc(F["q_psum"], 1)

            def ffn_up(s):
                if has(s):
                    seen(pe, F["xT"], s)
                    seen(pe, F["prod"], s - 1)
                    for n in range(2 * INNER // 512):
                        for k in range(KD):
                            mm = pe.matmul(PS[:, n], fxT[:, k, :], wgu_q[:, k, n * 512:(n + 1) * 512],
                                           start=(k == 0), stop=(k == KD - 1))
                    mm.then_inc(F["up_psum"], 1)

            def ffn_down(s, b):
                if has(s):
                    seen(pe, F["pq"], s)
                    seen(pe, F["pT"], s - 1)
                    for k in range(KN):
                        mm = pe.transpose(PS[:, 5].bitcast(BF16)[:, k * P:(k + 1) * P], fpb[:, b, k * P:(k + 1) * P], ident_b[:])
                    mm.then_inc(F["pq_psum"], 1)
                    seen(pe, F["pT"], s)
                    seen(pe, F["resid"], s - 1)
                    for k in range(KN):
                        mm = pe.matmul(PS[:, 6, 0:D], fpT[:, k, :], wdn_q[:, k, :], start=(k == 0), stop=(k == KN - 1))
                    mm.then_inc(F["down_psum"], 1)

            def ffn_step(s, b):
                ffn_up(s)
                ffn_down(s - 1, 1 - b)
                q_turn(s + 1, 1 - b)

            skewed(pe, ffn_step, SEQ, 1, 1)

        @block.scalar
        def _(act):
            act.wait_ge(tok_in, 80)
            for t in range(TG):
                for m in range(KH):
                    n = t * KH + m
                    act.wait_ge(t_hid_psum, n + 1)
                    if t:
                        act.wait_ge(t_row_psum, 4 * t)
                    nc.scalar.activation(thid[:, m, :], PS[:, n % 2], ACT.Gelu_apprx_tanh, bias=tb1[:, m:m + 1]).then_inc(t_hid, 1)

            def attention(layer):
                a = A[layer]

                def x_copy(s):
                    if has(s):
                        seen(act, a["xT_psum"], s)
                        nc.scalar.copy(xT[:].rearrange("p k n -> p (k n)"), PS[:, 6, 0:D]).then_inc(a["xT"], 1)

                def o_copy(s):
                    if has(s):
                        seen(act, a["oT_psum"], s)
                        seen(act, a["y_psum"], s - 1)
                        nc.scalar.copy(oT[:].rearrange("p k n -> p (k n)"), PS[:, 7, 0:D]).then_inc(a["oT"], 1)

                def p_copy(s):
                    if has(s):
                        seen(act, a["o_psum"], s - 1)
                        for r in range(4):
                            seen(act, a["pT_psum"], s, r + 1, 4)
                            nc.scalar.copy(probT[:, 4 * r:4 * r + 4, :].rearrange("p a n -> p (a n)"), PS[:, 4 + r % 2, :]).then_inc(a["pT"], 1)

                def q_copy(s, b):
                    if has(s):
                        seen(act, a["qk_psum"], s)
                        if layer == 0:
                            nc.scalar.mul(qT[:, b].rearrange("p k n -> p (k n)"), PS[:, 6, 0:D], DH ** -0.5).then_inc(a["q"], 1)
                        else:
                            for k in range(KD):
                                ins = nc.scalar.activation(qT[:, b, k, :], PS[:, 6, k * P:(k + 1) * P], ACT.Identity,
                                                           bias=bq_scaled[:, k:k + 1], scale=DH ** -0.5)
                            ins.then_inc(a["q"], 1)

                def exps(s, b):
                    if has(s):
                        seen(act, a["shifted"], s)
                        v = prob[:, b].rearrange("p a n -> p (a n)")
                        nc.scalar.activation(v, v, ACT.Exp).then_inc(a["prob"], 1)

                def raw_copy(s):
                    if has(s):
                        seen(act, a["o_psum"], s)
                        seen(act, a["o2_psum"], s - 1)
                        nc.scalar.copy(oraw[:].rearrange("p a n -> p (a n)"), PS[:, 4, :]).then_inc(a["oraw"], 1)

                def step(s, b):
                    x_copy(s + 1)
                    o_copy(s - 2)
                    p_copy(s - 1)
                    q_copy(s + 1, 1 - b)
                    exps(s, b)
                    raw_copy(s - 1)

                skewed(act, step, SEQ, 1, 2)

            act.wait_ge(weights_ready, 1)
            attention(0)

            act.wait_ge(A[0]["resid"], SEQ)

            def xT_copy(g, b):
                if has(g, G):
                    for k in range(KD):
                        seen(act, M["xT_psum"], g, k + 1, KD, G)
                        nc.scalar.copy(mxT[:, b, k, :], PS[:, 6 + k, :]).then_inc(M["xT"], 1)

            def route_exp(g, b):
                if has(g, G):
                    seen(act, M["route_max"], g, 1, 1, G)
                    v = r8[0][:].rearrange("p a e -> p (a e)")
                    nc.scalar.activation(v, v, ACT.Exp).then_inc(M["route_exp"], 1)

            def expert_step(g, b):
                if has(g, G):
                    for e in range(EA):
                        for h in range(KI):
                            n = e * KI + h
                            seen(act, M["up_psum"], g, n + 1, EA * KI, G)
                            if n >= 2:
                                seen(act, M["half"], g, n - 1, EA * KI, G)
                            else:
                                seen(act, M["half"], g - 1, EA * KI - 1 + n, EA * KI, G)
                            nc.scalar.activation(tnh[:, h, :], PS[:, 2 * h], ACT.Tanh, scale=0.5).then_inc(M["tanh"], 1)
                        if e == EA - 2:
                            xT_copy(g + 1, 1 - b)
                    route_exp(g + 1, 1 - b)
                else:
                    xT_copy(g + 1, 1 - b)
                    route_exp(g + 1, 1 - b)

            skewed(act, expert_step, G, 1, 1)

            act.wait_ge(M["resid"], G * EA * GS)
            attention(1)
            act.wait_ge(A[1]["resid"], SEQ)

            def fx_copy(s):
                if has(s):
                    seen(act, F["q_psum"], s)
                    seen(act, F["up_psum"], s - 1)
                    nc.scalar.copy(fxT[:].rearrange("p k n -> p (k n)"), PS[:, 4].bitcast(BF16)[:, 0:D]).then_inc(F["xT"], 1)

            def ftanh(s, b):
                if has(s):
                    seen(act, F["up_psum"], s)
                    seen(act, F["scales"], s)
                    seen(act, F["half"], s - 1)
                    nc.scalar.activation(ft[:], PS[:, 0:2].rearrange("p a n -> p (a n)"), ACT.Tanh, scale=fs[:, b, 4:5]).then_inc(F["tanh"], 1)

            def fp_copy(s):
                if has(s):
                    seen(act, F["pq_psum"], s)
                    seen(act, F["down_psum"], s - 1)
                    nc.scalar.copy(fpT[:].rearrange("p k n -> p (k n)"), PS[:, 5].bitcast(BF16)).then_inc(F["pT"], 1)

            def ffn_step(s, b):
                ftanh(s, b)
                fp_copy(s - 1)
                fx_copy(s + 1)

            skewed(act, ffn_step, SEQ, 1, 1)

        @block.vector
        def _(dve):
            done = [0]

            def after_me(ins):
                done[0] += 1
                ins.then_inc(prep, 1)
                dve.wait_ge(prep, done[0])

            dve.wait_ge(attn_in, ATTN_LOADS)
            dve.tensor_copy(ident_b[:], ident[:])
            for c in range(4):
                dve.tensor_copy(causal_b[:, c, :], causal[:])
            dve.tensor_scalar(bq_scaled[:], bqk[:, 0:KD], DH ** -0.5, None, ALU.mult)
            after_me(dve.reciprocal(kvinv[:], kvs[:]))
            v = wst[:].rearrange("p (u n) -> p u n", u=2)
            dve.wait_ge(ffn_in, 16)
            dve.tensor_reduce(wabs[:, 0:2], v, AX.X, ALU.add, apply_absolute_value=True).then_inc(wst_summed, 1)
            dve.wait_ge(ffn_in, 32)
            dve.tensor_reduce(wabs[:, 2:4], v, AX.X, ALU.add, apply_absolute_value=True).then_inc(wst_summed, 1)
            dve.wait_ge(wst_summed, 2)
            after_me(dve.tensor_tensor(wabs[:, 0:2], wabs[:, 0:2], wabs[:, 2:4], ALU.add))
            after_me(dve.memset(wabs[:, 3:4], 0.0))
            dve.wait_ge(ffn_in, 48)
            dve.tensor_reduce(wabs[:, 2:3], wst[:], AX.X, ALU.add, apply_absolute_value=True).then_inc(wst_summed, 1)

            def table_rows(t):
                dve.wait_ge(tok_in, 80)
                for n in range(4 * t, 4 * t + 4):
                    dve.wait_ge(t_row_psum, n + 1)
                    if n >= 4:
                        dve.wait_ge(t_store[n % 4], 16 * (n // 4))
                    dve.tensor_tensor(trow[:, n % 4, :], PS[:, 2 + n % 2, 0:D], tb2[:], ALU.add).then_inc(t_row, 1)

            table_rows(0)
            for k in range(KD):
                dve.tensor_scalar(wqkv[0][:, k, :], wqkv[0][:, k, :], gln[:, k:k + 1], None, ALU.mult)
            for n, (w, k, lo, hi) in enumerate(((wqkv[1], 0, 0, 512), (wqkv[1], 0, 512, 768), (wqkv[1], 1, 0, 512),
                                                (wqkv[1], 1, 512, 768), (wout[1], 0, 0, 256), (wout[1], 1, 0, 256))):
                dve.wait_ge(lora_psum, n + 1)
                dve.scalar_tensor_tensor(w[:, k, lo:hi], PS[:, 4 + n % 3, 0:hi - lo], 2.0, w[:, k, lo:hi], ALU.mult, ALU.add)\
                   .then_inc(lora_added, 1)
            dve.wait_ge(wsum_psum, 1)
            after_me(dve.tensor_scalar(wmean[:], PS[:, 7, 0:4], 1.0 / (D * INNER), EPS, ALU.mult, ALU.max))
            after_me(dve.reciprocal(wscale[:], wmean[:]))
            after_me(dve.reciprocal(winv[:], wscale[:]))

            def ternary(dst, src, which):
                after_me(dve.tensor_scalar(src, src, wscale[:, which:which + 1], ROUND, ALU.mult, ALU.add))
                after_me(dve.tensor_scalar(src, src, -ROUND, 1.0, ALU.add, ALU.min))
                return dve.tensor_scalar(dst, src, -1.0, None, ALU.max)

            for n in range(KD):
                dve.wait_ge(ffn_in, 64 + 16 * n)
                after_me(ternary(wgu_q[:, n, 0:INNER], wst[:, 0:INNER], 0))
                ternary(wgu_q[:, n, INNER:], wst[:, INNER:], 1).then_inc(wst_quantized, 1)
            dve.wait_ge(ffn_in, 96)
            ternary(wdn_q[:].rearrange("p k n -> p (k n)"), wst[:], 2).then_inc(weights_ready, 1)

            for t in range(1, TG):
                table_rows(t)

            def attention(layer):
                a = A[layer]
                if layer == 0:
                    for t in range(4):
                        dve.wait_ge(t_store[t], 16 * TG)
                dve.memset(V[:].rearrange("p b h n -> p (b h n)"), 1.0).then_inc(a["v_ones"], 1)
                dve.wait_ge(a["v_ones"], 1)

                def norm(s, b):
                    if has(s):
                        seen(dve, a["rstd"], s)
                        seen(dve, a["xT_psum"], s - 1)
                        dve.tensor_scalar(xn[:], row(resid, s), mv[:, b, 0:1], rstd[:, b:b + 1], ALU.subtract, ALU.mult).then_inc(a["xn"], 1)

                def o_norm(s):
                    if has(s):
                        seen(dve, a["o2_psum"], s)
                        o = PS[:, 7].rearrange("p (h n) -> p h n", n=SLOT)
                        dve.reciprocal(rden[:], o[:, :, DH]).then_inc(a["rden"], 1)
                        seen(dve, a["rden"], s)
                        seen(dve, a["oT_psum"], s - 1)
                        dve.tensor_tensor(onrm[:].rearrange("p (h n) -> p h n", n=DH), o[:, :, 0:DH],
                                          spread(rden[:], DH),
                                          ALU.mult).then_inc(a["onrm"], 1)

                def softmax(s, b):
                    if has(s):
                        seen(dve, a["s_psum"], s)
                        sc = PS[:, 0:4].rearrange("p r (c k) -> p (r c) k", k=P)
                        dve.tensor_reduce(rmax[:], sc, AX.X, ALU.max).then_inc(a["rmax"], 1)
                        seen(dve, a["rmax"], s)
                        seen(dve, a["pT_psum"], s - 2, 4, 4)
                        dve.tensor_tensor(prob[:, b], sc, spread(rmax[:], P),
                                          ALU.subtract).then_inc(a["shifted"], 1)

                def k_copy(s, b):
                    if has(s):
                        seen(dve, a["qk_psum"], s)
                        seen(dve, a["q"], s)
                        src = PS[:, 6, D:2 * D].rearrange("p (k n) -> p k n", k=KD)
                        if layer == 0:
                            for e in range(2):
                                ins = dve.tensor_scalar(kT[:, b, :, e, :], src, slot[:, e:e + 1], None, ALU.mult)
                            ins.then_inc(a["k"], 1)
                        else:
                            for k in range(KD):
                                ins = dve.tensor_scalar(kq[:, k, :], src[:, k, :], bqk[:, KD + k:KD + k + 1], kvinv[:, 0:1], ALU.add, ALU.mult)
                            ins.then_inc(a["kchain"], 1)
                            seen(dve, a["kchain"], s, 1, 4)
                            dve.tensor_scalar(kq[:], kq[:], kvz[:, 0:1], 0.0, ALU.add, ALU.max).then_inc(a["kchain"], 1)
                            seen(dve, a["kchain"], s, 2, 4)
                            dve.tensor_scalar(kq[:], kq[:], 255.0, ROUND, ALU.min, ALU.add).then_inc(a["kchain"], 1)
                            seen(dve, a["kchain"], s, 3, 4)
                            dve.tensor_scalar(kq[:], kq[:], -ROUND, kvz[:, 0:1], ALU.add, ALU.subtract).then_inc(a["kchain"], 1)
                            seen(dve, a["kchain"], s, 4, 4)
                            for e in range(2):
                                ins = dve.tensor_scalar(kT[:, b, :, e, :], kq[:], kvs[:, 0:1], slot[:, e:e + 1], ALU.mult, ALU.mult)
                            ins.then_inc(a["k"], 1)

                def v_copy(s, b):
                    if has(s):
                        seen(dve, a["v_psum"], s)
                        seen(dve, a["o_psum"], s - 2)
                        dst = V[:, b, :, 0:DH]
                        if layer == 0:
                            dve.tensor_copy(dst, PS[:, 7, 0:D].rearrange("p (h n) -> p h n", n=DH)).then_inc(a["v"], 1)
                        else:
                            dve.tensor_tensor(vq[:], PS[:, 7, 0:D], bv[:], ALU.add).then_inc(a["vchain"], 1)
                            seen(dve, a["vchain"], s, 1, 4)
                            dve.tensor_scalar(vq[:], vq[:], kvinv[:, 0:1], kvz[:, 0:1], ALU.mult, ALU.add).then_inc(a["vchain"], 1)
                            seen(dve, a["vchain"], s, 2, 4)
                            dve.tensor_scalar(vq[:], vq[:], 0.0, 255.0, ALU.max, ALU.min).then_inc(a["vchain"], 1)
                            seen(dve, a["vchain"], s, 3, 4)
                            dve.tensor_scalar(vq[:], vq[:], ROUND, -ROUND, ALU.add, ALU.add).then_inc(a["vchain"], 1)
                            seen(dve, a["vchain"], s, 4, 4)
                            dve.tensor_scalar(dst, vq[:].rearrange("p (h n) -> p h n", n=DH), kvz[:, 0:1], kvs[:, 0:1],
                                              ALU.subtract, ALU.mult).then_inc(a["v"], 1)

                def add(s):
                    seen(dve, a["stats"], s + 4)
                    if has(s):
                        seen(dve, a["y_psum"], s)
                        if layer == 1:
                            seen(dve, a["biased"], s)
                        dve.tensor_tensor(row(resid, s), row(resid, s), PS[:, 7, 0:D], ALU.add).then_inc(a["resid"], 1)

                def moments(s, b):
                    if has(s):
                        if layer == 0:
                            dve.wait_ge(gathered[b], pair(s) * 16 + 16)
                        dve.bn_stats(stats[:], row(resid, s)).then_inc(a["stats"], 1)

                def moments_end(s, b):
                    if has(s):
                        dve.bn_aggr(mv[:, b, :], stats[:]).then_inc(a["aggr"], 1)
                        seen(dve, a["aggr"], s)
                        if layer == 0:
                            dve.tensor_scalar(varp[:, b:b + 1], mv[:, b, 1:2], 1.0 + EPS, EPS * EPS, ALU.mult, ALU.add).then_inc(a["var"], 1)
                        else:
                            dve.tensor_scalar(varp[:, b:b + 1], mv[:, b, 1:2], EPS, None, ALU.add).then_inc(a["var"], 1)

                def step(s, b):
                    norm(s + 1, 1 - b)
                    o_norm(s - 2)
                    softmax(s, b)
                    k_copy(s + 1, 1 - b)
                    v_copy(s + 1, 1 - b)
                    moments(s + 2, b)
                    add(s - 2)
                    moments_end(s + 2, b)

                skewed(dve, step, SEQ, 2, 2)

            attention(0)

            dve.memset(gates[:].rearrange("p b t e -> p (b t e)"), 0.5).then_inc(M["gates"], 1)
            dve.wait_ge(M["gates"], 1)

            def moments(g):
                if has(g, G):
                    for t in range(GS):
                        ins = dve.bn_stats(mstats[:, t, :], row(resid, g * GS + t))
                    ins.then_inc(M["stats"], 1)

            def moments_end(g):
                if has(g, G):
                    for t in range(GS):
                        ins = dve.bn_aggr(mmv[:, t, :], mstats[:, t, :])
                    ins.then_inc(M["aggr"], 1)
                    seen(dve, M["aggr"], g, 1, 1, G)
                    dve.tensor_scalar(mvar[:], mmv[:, :, 1], EPS, None, ALU.add).then_inc(M["var"], 1)

            def norm(g):
                if has(g, G):
                    seen(dve, M["rstd"], g, 1, 1, G)
                    seen(dve, M["xT_psum"], g - 1, KD, KD, G)
                    for t in range(GS):
                        dve.tensor_scalar(mxn[:, t, :], row(resid, g * GS + t), mmv[:, t, 0:1], mrstd[:, t:t + 1],
                                          ALU.subtract, ALU.mult).then_inc(M["xn"], 1)

            ROUTER = 17

            def router(g, b):
                if not has(g, G):
                    return
                n = [0]

                def then(ins):
                    n[0] += 1
                    ins.then_inc(M["gates"], 1)
                    dve.wait_ge(M["gates"], g * ROUTER + n[0] + 1)

                def over(v):
                    return spread(v[:], E)

                def each(v):
                    return v[:].unsqueeze(1).broadcast_to([P, GS, E])

                seen(dve, M["route_psum"], g, 1, 1, G)
                lg = PS[:, 6, 0:GS * E].rearrange("p (t e) -> p t e", e=E)
                then(dve.tensor_reduce(r1[0][:], lg, AX.X, ALU.max))
                ins = dve.tensor_tensor(r8[0][:], lg, over(r1[0]), ALU.subtract)
                ins.then_inc(M["route_max"], 1)
                seen(dve, M["route_exp"], g, 1, 1, G)
                then(dve.tensor_reduce(r1[1][:], r8[0][:], AX.X, ALU.add))
                then(dve.reciprocal(r1[2][:], r1[1][:]))
                then(dve.tensor_tensor(r8[1][:], r8[0][:], over(r1[2]), ALU.mult))
                then(dve.tensor_tensor(r8[2][:], r8[1][:], each(gbias), ALU.add))
                for turn in range(2):
                    then(dve.tensor_reduce(r1[3][:], r8[2][:], AX.X, ALU.max))
                    then(dve.tensor_tensor(r8[3][:], r8[2][:], over(r1[3]), ALU.is_equal))
                    then(dve.tensor_tensor(r8[3][:], r8[3][:], each(rank), ALU.mult))
                    then(dve.tensor_reduce(r1[4][:], r8[3][:], AX.X, ALU.max))
                    if turn == 0:
                        then(dve.tensor_tensor(r8[4][:], r8[3][:], over(r1[4]), ALU.is_equal))
                        then(dve.scalar_tensor_tensor(r8[2][:], r8[4][:], -BIG, r8[2][:], ALU.mult, ALU.add))
                    else:
                        then(dve.tensor_tensor(r8[5][:], r8[3][:], over(r1[4]), ALU.is_equal))
                then(dve.tensor_tensor(r8[4][:], r8[4][:], r8[5][:], ALU.add))
                dve.scalar_tensor_tensor(gates[:, b, :, 0:E], r8[1][:], 0.5, r8[4][:], ALU.mult, ALU.mult).then_inc(M["router"], 1)
                assert n[0] == ROUTER, n[0]

            def expert_step(g, b):
                def add(e):
                    for t in range(GS):
                        if t % 2 == 0:
                            seen(dve, M["down_psum"], g, e * 2 + t // 2 + 1, EA * 2, G)
                        r = row(resid, g * GS + t)
                        dve.scalar_tensor_tensor(r, PS[:, 4 + t // 2, t % 2 * D:(t % 2 + 1) * D], gates[:, b, t, e:e + 1], r,
                                                 ALU.mult, ALU.add).then_inc(M["resid"], 1)

                if has(g, G):
                    seen(dve, M["router"], g, 1, 1, G)
                    for e in range(EA):
                        for h in range(KI):
                            n = e * KI + h
                            seen(dve, M["tanh"], g, n + 1, EA * KI, G)
                            if n == (EA - 4) * KI:
                                seen(dve, M["stats"], g + 1, 1, 1, G)
                            dve.scalar_tensor_tensor(act_[:, h, :], tnh[:, h, :], 1.0, PS[:, 2 * h], ALU.add, ALU.mult).then_inc(M["half"], 1)
                            seen(dve, M["half"], g, n + 1, EA * KI, G)
                            if h == 0:
                                if e >= 2:
                                    seen(dve, M["down_psum"], g, (e - 1) * 2, EA * 2, G)
                                else:
                                    seen(dve, M["down_psum"], g - 1, (EA + e - 1) * 2, EA * 2, G)
                            dve.tensor_tensor(hT[:, e % 2, h, :], act_[:, h, :], PS[:, 2 * h + 1], ALU.mult).then_inc(M["hT"], 1)
                        if e:
                            add(e - 1)
                        if e == EA - 5:
                            moments(g + 1)
                        if e == EA - 4:
                            moments_end(g + 1)
                        if e == EA - 3:
                            norm(g + 1)
                    router(g + 1, 1 - b)
                    add(EA - 1)
                else:
                    moments(g + 1)
                    seen(dve, M["stats"], g + 1, 1, 1, G)
                    moments_end(g + 1)
                    norm(g + 1)
                    router(g + 1, 1 - b)

            skewed(dve, expert_step, G, 1, 1)

            attention(1)

            CH = 8

            def ffn_moments(s, b):
                if has(s):
                    dve.bn_stats(fstats[:], row(resid, s)).then_inc(F["stats"], 1)

            def ffn_moments_end(s, b):
                if has(s):
                    dve.bn_aggr(fmv[:], fstats[:]).then_inc(F["aggr"], 1)
                    seen(dve, F["aggr"], s)
                    dve.tensor_scalar(fvar[:, b:b + 1], fmv[:, 1:2], EPS, None, ALU.add).then_inc(F["var"], 1)

            def ffn_quant(s, b):
                if not has(s):
                    return
                n = [0]

                def then(ins):
                    n[0] += 1
                    ins.then_inc(F["chain"], 1)
                    seen(dve, F["chain"], s, n[0], CH)

                seen(dve, F["rstd"], s)
                then(dve.tensor_scalar(fxn[:], row(resid, s), fmv[:, 0:1], frstd[:, b:b + 1], ALU.subtract, ALU.mult))
                then(dve.tensor_reduce(fs[:, b, 0:1], fxn[:], AX.X, ALU.max, apply_absolute_value=True))
                then(dve.tensor_scalar(fs[:, b, 1:2], fs[:, b, 0:1], EPS, 1.0 / 127.0, ALU.max, ALU.mult))
                then(dve.reciprocal(fs[:, b, 2:3], fs[:, b, 1:2]))
                then(dve.tensor_scalar(fq[:], fxn[:], fs[:, b, 2:3], 127.0, ALU.mult, ALU.min))
                then(dve.tensor_scalar(fq[:], fq[:], -128.0, ROUND, ALU.max, ALU.add))
                then(dve.tensor_scalar(fs[:, b, 3:4], fs[:, b, 1:2], winv[:, 1:2], 0.5, ALU.mult, ALU.mult))
                then(dve.tensor_scalar(fs[:, b, 4:5], fs[:, b, 1:2], winv[:, 0:1], 0.5, ALU.mult, ALU.mult))
                assert n[0] == CH
                dve.tensor_scalar(fqb[:, b, :], fq[:], -ROUND, None, ALU.add).then_inc(F["q"], 1)
                dve.tensor_scalar(fs[:, b, 5:6], fs[:, b, 4:5], fs[:, b, 3:4], 2.0, ALU.mult, ALU.mult).then_inc(F["scales"], 1)

            PR = 7

            def ffn_mid(s, b):
                seen(dve, F["stats"], s + 1)
                if not has(s):
                    ffn_moments_end(s + 1, 1 - b)
                    return
                n = [0]

                def then(ins):
                    n[0] += 1
                    ins.then_inc(F["prod"] if n[0] == 1 else F["pchain"], 1)
                    if n[0] == 1:
                        seen(dve, F["prod"], s)
                    else:
                        seen(dve, F["pchain"], s, n[0] - 1, PR - 1)

                seen(dve, F["tanh"], s)
                dve.scalar_tensor_tensor(fp[:], ft[:], 1.0, PS[:, 0:2].rearrange("p a n -> p (a n)"), ALU.add, ALU.mult).then_inc(F["half"], 1)
                ffn_moments_end(s + 1, 1 - b)
                seen(dve, F["half"], s)
                then(dve.tensor_tensor(fp[:], fp[:], PS[:, 2:4].rearrange("p a n -> p (a n)"), ALU.mult))
                then(dve.tensor_reduce(fs[:, b, 6:7], fp[:], AX.X, ALU.max, apply_absolute_value=True))
                then(dve.tensor_scalar(fs[:, b, 6:7], fs[:, b, 6:7], fs[:, b, 5:6], EPS, ALU.mult, ALU.max))
                then(dve.tensor_scalar(fs[:, b, 6:7], fs[:, b, 6:7], 1.0 / 127.0, None, ALU.mult))
                then(dve.reciprocal(fs[:, b, 7:8], fs[:, b, 6:7]))
                then(dve.tensor_scalar(fs[:, b, 7:8], fs[:, b, 7:8], fs[:, b, 5:6], None, ALU.mult))
                then(dve.tensor_scalar(fpq[:], fp[:], fs[:, b, 7:8], 127.0, ALU.mult, ALU.min))
                assert n[0] == PR
                dve.tensor_scalar(fpq[:], fpq[:], -128.0, ROUND, ALU.max, ALU.add).then_inc(F["pround"], 1)
                seen(dve, F["pround"], s)
                dve.tensor_scalar(fpb[:, b, :], fpq[:], -ROUND, None, ALU.add).then_inc(F["pq"], 1)

            def ffn_add(s, b):
                if has(s):
                    seen(dve, F["down_psum"], s)
                    dve.tensor_scalar(fs[:, b, 6:7], fs[:, b, 6:7], winv[:, 2:3], None, ALU.mult).then_inc(F["fscale"], 1)
                    seen(dve, F["fscale"], s)
                    dve.scalar_tensor_tensor(row(resid, s), PS[:, 6, 0:D], fs[:, b, 6:7], row(resid, s), ALU.mult, ALU.add).then_inc(F["resid"], 1)

            def ffn_step(s, b):
                ffn_moments(s + 1, 1 - b)
                ffn_mid(s, b)
                ffn_add(s - 1, 1 - b)
                ffn_quant(s + 1, 1 - b)

            skewed(dve, ffn_step, SEQ, 1, 1)


def _inputs(v):
    import numpy as np

    f = {k: np.asarray(a) for k, a in v.items()}
    pos = [head_at(p) * DH + d for p in range(H) for d in range(DH)]
    v_cols = [2 * D + c for c in pos]
    order = list(range(2 * D)) + v_cols

    def rows(a):
        return np.broadcast_to(np.asarray(a).reshape(1, -1), (P, np.asarray(a).size))

    def cols(a):
        return np.asarray(a).reshape(-1, P).T

    def experts(a, b):
        return np.concatenate([a.transpose(0, 2, 1), b.transpose(0, 2, 1)], axis=2)

    inter = f["L0_ffn_w1"].shape[1]
    sw1, sw3 = (f[n].reshape(-1, inter, D) for n in ("L0_ffn_sw1", "L0_ffn_sw3"))
    sw2 = f["L0_ffn_sw2"].reshape(D, -1, inter).transpose(1, 2, 0)
    n_exp = f["L0_ffn_gate_w"].shape[0]
    at = np.arange(P)
    return {
        "x_t": f["x"].T,
        "codebook_t": f["L0_tok_codebook"].T,
        "tok_w1": f["L0_tok_W1"],
        "tok_b1": cols(f["L0_tok_b1"]),
        "tok_w2": f["L0_tok_W2"],
        "tok_b2": rows(f["L0_tok_b2"]),
        "g_ln": cols(f["L0_attn_g_ln"]),
        "w_qkv0": np.concatenate([f["L0_attn_Wq"], f["L0_attn_Wkv"]], axis=1)[:, order],
        "w_out0": f["L0_attn_Wo"][pos],
        "gate_wt": f["L0_ffn_gate_w"].T,
        "gate_bias": rows(f["L0_ffn_gate_bias"]),
        "w13": np.concatenate([experts(f["L0_ffn_w1"], f["L0_ffn_w3"]), experts(sw1, sw3)]),
        "w2": np.concatenate([f["L0_ffn_w2"].transpose(0, 2, 1), sw2]),
        "w_qkv1": f["L1_attn_w_attn"][:, order],
        "b_qk": cols(f["L1_attn_b_attn"][:2 * D]),
        "b_v": rows(f["L1_attn_b_attn"][v_cols]),
        "la_attn_t": f["L1_attn_la_attn"].T,
        "lb_attn": f["L1_attn_lb_attn"][:, order],
        "w_proj": f["L1_attn_w_proj"][pos],
        "b_proj": rows(f["L1_attn_b_proj"]),
        "la_proj_t": f["L1_attn_la_proj"][pos].T,
        "lb_proj": f["L1_attn_lb_proj"],
        "kv_scale": rows(f["L1_attn_kv_scale"]),
        "kv_zero": rows(f["L1_attn_kv_zero_point"]),
        "w_gu": np.concatenate([f["L1_ffn_w_gate"].T, f["L1_ffn_w_up"].T], axis=1),
        "w_down": f["L1_ffn_w_down"].T,
        "ident_in": np.eye(P, dtype=np.float32),
        "causal_in": np.where(at[None, :] > at[:, None], np.float32(MASKED), np.float32(0)),
        "slot_in": np.stack([at % SLOT < DH, at % SLOT >= DH], axis=1).astype(np.float32),
        "rank_in": np.tile(np.arange(n_exp, 0, -1, dtype=np.float32), (P, 1)),
    }


def kernel(**inputs):
    import numpy as np
    from concourse import bacc
    from concourse.bass_utils import run_bass_kernel_spmd

    nc = bacc.Bacc("TRN2", target_bir_lowering=False, num_devices=1)
    arrays = {f"in_{n}": np.ascontiguousarray(a) for n, a in _inputs(inputs).items()}
    args = [nc.dram_tensor(n, a.shape, mybir.dt.from_np(a.dtype), kind="ExternalInput").ap() for n, a in arrays.items()]
    n_seq, length = inputs["x"].shape
    out = nc.dram_tensor("out_0", (n_seq, length, D), F32, kind="ExternalOutput").ap()
    build(nc, *args, out)
    r = run_bass_kernel_spmd(nc, [arrays], core_ids=[0])
    return r.results[0]["out_0"]
```

```python
from contextlib import ExitStack

import concourse.bass as bass
from concourse import mybir

F32 = mybir.dt.float32
BF16 = mybir.dt.bfloat16
U32 = mybir.dt.uint32
I32 = mybir.dt.int32
ALU = mybir.AluOpType
ACT = mybir.ActivationFunctionType
AX = mybir.AxisListType

P = 128
D = 256
KD = D // P
H = 16
DH = D // H
HPB = P // DH
SLOT = 32
EPS = 1e-5
ROUND = 1.5 * 2.0 ** 23
MASKED = -1e30
BIG = 1e30


def build(nc, x_t, codebook_t, tok_w1, tok_b1, tok_w2, tok_b2,
          g_ln, w_qkv0, w_out0, gate_wt, gate_bias, w13, w2,
          w_qkv1, b_qk, b_v, la_attn_t, lb_attn, w_proj, b_proj, la_proj_t, lb_proj, kv_scale, kv_zero,
          w_gu, w_down, ident_in, causal_in, own_in, rank_in, earlier_in, tile_no_in, out):
    SEQ = x_t.shape[1]
    ROWS = codebook_t.shape[1]
    HID = tok_w1.shape[1]
    E = gate_wt.shape[1]
    EA = w13.shape[0]
    INTER = w2.shape[1]
    INNER = w_down.shape[0]
    RANK = la_attn_t.shape[0]
    KH, KI, KN = HID // P, INTER // P, INNER // P
    GS = 4
    GT = GS * P
    G = SEQ // GS
    TG = ROWS // 512
    NS = EA - E
    TOP = 2
    NT = TOP * SEQ + E
    FILLS = 8

    table = nc.dram_tensor("token_table", (ROWS, D), F32).ap()
    placed_x = nc.dram_tensor("placed_x", (NT * P, D), F32).ap()
    placed_y = nc.dram_tensor("placed_y", (NT * P, D), F32).ap()

    with ExitStack() as ctx:
        def sb(name, shape, dt=F32, at=None):
            return (at or ctx).enter_context(nc.sbuf_tensor(name, shape, dt))

        def sem(name):
            return ctx.enter_context(nc.semaphore(name))

        PS = ctx.enter_context(nc.psum_tensor("banks", [P, 8, 512], F32))

        resid = sb("resid", [P, SEQ, D])
        ident = sb("ident", [P, P])
        ident_b = sb("ident_b", [P, P], BF16)
        causal = sb("causal", [P, P])
        causal_b = sb("causal_b", [P, 4, P], BF16)
        own = [sb(f"own{i}", [P, HPB]) for i in range(2)]
        ones = sb("ones", [P, P])
        minus_round = sb("minus_round", [P, 1])
        minus_half = sb("minus_half", [P, GS])
        idx = sb("idx", [P, SEQ], I32)
        wqkv = [sb(f"wqkv{i}", [P, KD, 3 * D]) for i in range(2)]
        wout = [sb(f"wout{i}", [P, KD, D]) for i in range(2)]
        gln = sb("gln", [P, KD])
        bqk = sb("bqk", [P, 4])
        bq_scaled = sb("bq_scaled", [P, KD])
        bv = sb("bv", [P, D])
        bproj = sb("bproj", [P, D])
        kvs = sb("kvs", [P, 1])
        kvz = sb("kvz", [P, 1])
        kvinv = sb("kvinv", [P, 1])
        gw = sb("gw", [P, KD, E])
        gbias = sb("gbias", [P, E])
        rank = sb("rank", [P, E])
        earlier = sb("earlier", [P, P])
        zeros = sb("zeros", [P, D])
        place = sb("place", [P, SEQ, TOP], I32)
        place_now = sb("place_now", [P, 2, TOP], I32)
        tile_expert = sb("tile_expert", [1, NT], I32)
        gate = sb("gate", [P, TOP, SEQ])
        yrow = sb("yrow", [P, 2, TOP, D])
        w13_sb = sb("w13_sb", [P, EA, KD, 2 * INTER])
        w2_sb = sb("w2_sb", [P, EA, KI, D])
        wgu_q = sb("wgu_q", [P, KD, 2 * INNER], BF16)
        wdn_q = sb("wdn_q", [P, KN, D], BF16)
        wabs = sb("wabs", [P, 4])
        wmean = sb("wmean", [P, 4])
        wscale = sb("wscale", [P, 4])
        winv = sb("winv", [P, 4])

        with ExitStack() as t_:
            cb = sb("cb", [P, KD, ROWS], at=t_)
            tw1 = sb("tw1", [P, KD, HID], at=t_)
            tw2 = sb("tw2", [P, KH, D], at=t_)
            tb1 = sb("tb1", [P, KH], at=t_)
            tb2 = sb("tb2", [P, D], at=t_)
            thid = sb("thid", [P, KH, 512], at=t_)
            trow = sb("trow", [P, 4, D], at=t_)
            la1 = sb("la1", [RANK, D], at=t_)
            lb1 = sb("lb1", [RANK, 3 * D], at=t_)
            la2 = sb("la2", [RANK, D], at=t_)
            lb2 = sb("lb2", [RANK, D], at=t_)
            wst = sb("wst", [P, 2 * INNER], at=t_)
        with ExitStack() as a_:
            stats = sb("stats", [P, 6], at=a_)
            mv = sb("mv", [P, 4, 2], at=a_)
            varp = sb("varp", [P, 2], at=a_)
            rstd = sb("rstd", [P, 2], at=a_)
            xn = sb("xn", [P, D], at=a_)
            xT = sb("xT", [P, KD, P], at=a_)
            qT = sb("qT", [P, 2, KD, P], at=a_)
            kv = sb("kv", [P, 2, 2 * D], at=a_)
            kT = sb("kT", [P, 2, KD, HPB, P], at=a_)
            V = sb("V", [P, 2, H, SLOT], at=a_)
            prob = sb("prob", [P, 2, H, P], at=a_)
            probT = sb("probT", [P, H, P], at=a_)
            rmax = sb("rmax", [P, H], at=a_)
            rden = sb("rden", [P, H], at=a_)
            oraw = sb("oraw", [P, 4, P], at=a_)
            onrm = sb("onrm", [P, D], at=a_)
            oT = sb("oT", [P, KD, P], at=a_)
        with ExitStack() as m_:
            mstats = sb("mstats", [P, GS, 6], at=m_)
            mmv = sb("mmv", [P, 2, GS, 2], at=m_)
            mvar = sb("mvar", [P, GS], at=m_)
            mrstd = sb("mrstd", [P, GS], at=m_)
            mxn = sb("mxn", [P, SEQ, D], at=m_)
            staged = sb("staged", [P, 2, GS, D], at=m_)
            mxT = sb("mxT", [P, 2, KD, GT], at=m_)
            with ExitStack() as s_:
                hT = sb("hT", [P, 2, KI, GT], at=s_)
                tnh = sb("tnh", [P, 2, GT], at=s_)
                act_ = sb("act_", [P, 2, GT], at=s_)
            with ExitStack() as r_:
                PAD = SEQ // 2
                score = sb("score", [P, SEQ, E], at=r_)
                biased = sb("biased", [P, SEQ, E], at=r_)
                tie = sb("tie", [P, SEQ, E], at=r_)
                chosen = [sb(f"chosen{i}", [P, SEQ, E], at=r_) for i in range(TOP)]
                selected = sb("selected", [P, SEQ, E], at=r_)
                per_token = sb("per_token", [P, SEQ], at=r_)
                counts = [sb(f"counts{i}", [P, PAD + SEQ, E], at=r_) for i in range(3)]
                tiles = [sb(f"tiles{i}", [P, E + E], at=r_) for i in range(3)]
                start = sb("start", [P, E], at=r_)
                place_f = sb("place_f", [P, SEQ, TOP], at=r_)
                tile_no = sb("tile_no", [P, NT], at=r_)
                beyond = sb("beyond", [P, NT, E - 1], at=r_)
                tile_expert_f = sb("tile_expert_f", [P, NT], at=r_)
            with ExitStack() as e_:
                ex = sb("ex", [P, 2, D], at=e_)
                exT = sb("exT", [P, 2, KD, P], at=e_)
                etanh = sb("etanh", [P, 2, INTER], at=e_)
                eact = sb("eact", [P, 2, INTER], at=e_)
                eh = sb("eh", [P, 2, INTER], at=e_)
                ehT = sb("ehT", [P, KI, P], at=e_)
                ey = sb("ey", [P, 2, D], at=e_)
        with ExitStack() as f_:
            fstats = sb("fstats", [P, 6], at=f_)
            fmv = sb("fmv", [P, 2, 2], at=f_)
            fvar = sb("fvar", [P, 2], at=f_)
            frstd = sb("frstd", [P, 2], at=f_)
            fxn = sb("fxn", [P, D], at=f_)
            fq = sb("fq", [P, 2, D], at=f_)
            fxT = sb("fxT", [P, KD, P], BF16, at=f_)
            fs = sb("fs", [P, 2, 6], at=f_)
            fm = sb("fm", [P, 2, 3], at=f_)
            ft = sb("ft", [P, INNER], at=f_)
            fh = sb("fh", [P, 2, INNER], at=f_)
            fu = sb("fu", [P, 2, INNER], at=f_)
            fp = sb("fp", [P, 2, INNER], at=f_)
            fpq = sb("fpq", [P, 2, INNER], at=f_)
            fpT = sb("fpT", [P, KN, P], BF16, at=f_)

        tok_in, idx_in, attn_in, exp_in, ffn_in = (sem(f"{n}_loaded") for n in ("tok", "idx", "attn", "experts", "ffn"))
        consts = sem("consts_ready")
        prep = sem("prep_step")
        lora_psum = sem("lora_psum")
        lora_added = sem("lora_added")
        wsum_psum = sem("wsum_psum")
        weights_ready = sem("weights_ready")
        wst_summed = sem("wst_summed")
        wst_quantized = sem("wst_quantized")
        t_hid_psum, t_hid, t_row_psum, t_row = (sem(n) for n in ("t_hid_psum", "t_hid", "t_row_psum", "t_row"))
        t_store = [sem(f"table_stored{b}") for b in range(4)]
        gathered = [sem(f"gathered{b}") for b in range(2)]
        names = ("stats aggr var rstd xn xT_psum xT qk_psum q k_read k keys v_psum v_read v_ones v chain s_psum rmax shifted prob pT_psum pT"
                 " o_psum oraw o2_psum rden onrm oT_psum oT y_psum resid biased").split()
        A = [{n: sem(f"a{i}_{n}") for n in names} for i in range(2)]
        M = {n: sem(f"m_{n}") for n in ("stats aggr var rstd xn xT_psum xT route_psum route_exp route_max kept chain selected"
                                        " prefix_psum routed").split()}
        S = {n: sem(f"s_{n}") for n in "staged xT_psum xT up_psum tanh half hT down_psum resid".split()}
        T = {n: sem(f"t_{n}") for n in "xT_psum xT up_psum tanh half h hT_psum hT down_psum y".split()}
        places_filled, scattered = sem("places_filled"), sem("scattered")
        tile_in = [sem(f"tile_loaded{b}") for b in range(2)]
        tile_out = [sem(f"tile_stored{b}") for b in range(2)]
        y_gathered = [sem(f"y_gathered{b}") for b in range(2)]
        place_set, y_added, y_added_all = sem("place_set"), sem("y_added_first"), sem("y_added_both")
        F = {n: sem(f"f_{n}") for n in ("stats aggr var rstd chain pchain fscale q q_psum xT up_psum tanh u half kept prod scales pq pq_psum pT"
                                        " down_psum resid").split()}
        stored = sem("out_stored")

        def seen(eng, s, i, k=1, per=1, n=SEQ):
            if isinstance(i, int) and not 0 <= i < n:
                return
            eng.wait_ge(s, i * per + k)

        def has(i, n=SEQ):
            return not isinstance(i, int) or 0 <= i < n

        def row(t, i):
            return t[:, i] if isinstance(i, int) else t[:, bass.ds(i, 1)].rearrange("p a d -> p (a d)")

        def pair(i):
            return i // 2

        def spread(v, n):
            return v.unsqueeze(2).broadcast_to([P, v.shape[1], n])

        def skewed(eng, step, n, before, behind):
            first = behind
            last = (n - before - first) // 2 * 2 + first
            for s in range(-before, first):
                step(s, s % 2)
            with eng.Fori(0, (last - first) // 2, 1) as j:
                for b in range(2):
                    step(j * 2 + (first + b), (first + b) % 2)
            for s in range(last, n + behind):
                step(s, s % 2)

        block = ctx.enter_context(nc.Block())

        def kt(a):
            return a.rearrange("(k p) n -> p k n", p=P)

        @block.sync
        def _(sp):
            sp.dma_start(tw1[:], kt(tok_w1)).then_inc(tok_in, 16)
            sp.dma_start(cb[:], kt(codebook_t)).then_inc(tok_in, 16)
            sp.dma_start(tb1[:], tok_b1).then_inc(tok_in, 16)
            sp.dma_start(tw2[:], kt(tok_w2)).then_inc(tok_in, 16)
            sp.dma_start(tb2[:], tok_b2).then_inc(tok_in, 16)
            sp.dma_start(idx[:], x_t).then_inc(idx_in, 16)
            for dst, src in ((ident, ident_in), (causal, causal_in), (own[0], own_in), (gln, g_ln), (bqk, b_qk), (bv, b_v),
                             (bproj, b_proj), (kvs, kv_scale), (kvz, kv_zero), (gbias, gate_bias), (rank, rank_in),
                             (earlier, earlier_in),
                             (la1, la_attn_t), (lb1, lb_attn), (la2, la_proj_t), (lb2, lb_proj)):
                sp.dma_start(dst[:], src).then_inc(attn_in, 16)
            for dst, src in ((wqkv[0], w_qkv0), (wout[0], w_out0), (wqkv[1], w_qkv1), (wout[1], w_proj), (gw, gate_wt)):
                sp.dma_start(dst[:], kt(src)).then_inc(attn_in, 16)
            for n in range(2 * (KD + 1)):
                if 0 < n <= KD + 1:
                    sp.wait_ge(wst_summed, n)
                if n > KD + 1:
                    sp.wait_ge(wst_quantized, n - KD - 1)
                k = n % (KD + 1)
                if k < KD:
                    sp.dma_start(wst[:], w_gu[k * P:(k + 1) * P, :]).then_inc(ffn_in, 16)
                else:
                    sp.dma_start(wst[:].rearrange("p (k n) -> p k n", k=KN), kt(w_down)).then_inc(ffn_in, 16)
            for n in range(4 * TG):
                sp.wait_ge(t_row, n + 1)
                sp.dma_start(table[n * P:(n + 1) * P, :], trow[:, n % 4, :]).then_inc(t_store[n % 4], 16)
            sp.wait_ge(A[0]["resid"], SEQ)
            sp.dma_start(tile_no[:], tile_no_in).then_inc(tile_in[0], 16)
            sp.wait_ge(scattered, 16 * TOP * SEQ)
            sp.wait_ge(S["resid"], G * NS * GS)

            def tile_rows(dram, j):
                if isinstance(j, int):
                    return dram[j * P:(j + 1) * P, :]
                return dram[bass.ds(j * P, P), :]

            def tile_step(j, b):
                if has(j + 5, NT):
                    seen(sp, T["xT_psum"], j + 3, 1, 1, NT)
                    sp.dma_start(ex[:, 1 - b, :], tile_rows(placed_x, j + 5)).then_inc(tile_in[1 - b], 16)
                if has(j, NT):
                    seen(sp, T["y"], j, 1, 1, NT)
                    sp.dma_start(tile_rows(placed_y, j), ey[:, b, :]).then_inc(tile_out[b], 16)

            skewed(sp, tile_step, NT, 5, 2)
            with sp.Fori(0, SEQ, 1) as i:
                sp.wait_ge(F["resid"], i + 1)
                sp.dma_start(out[bass.ds(i, 1)].rearrange("a p d -> p (a d)"), row(resid, i)).then_inc(stored, 16)
            sp.wait_ge(stored, 16 * SEQ)

        ATTN_LOADS = 21 * 16
        CH, PR = 6, 5

        @block.gpsimd
        def _(pool):
            pool.memset(minus_half[:], -0.5).then_inc(consts, 1)
            pool.memset(ones[:], 1.0).then_inc(consts, 1)
            pool.memset(minus_round[:], -ROUND).then_inc(consts, 1)
            pool.memset(zeros[:], 0.0).then_inc(consts, 1)
            pool.wait_ge(idx_in, 16)
            pool.wait_ge(consts, 1)
            for t in range(4):
                pool.wait_ge(t_store[t], 16 * TG)

            def gather(i):
                pool.indirect_dma_start(resid[:, i, :], None, table,
                                        bass.IndirectOffsetOnAxis(ap=idx[:, i:i + 1].bitcast(U32), axis=0)).then_inc(gathered[i % 2], 16)

            def attention(layer):
                a = A[layer]

                def step(s, b):
                    if layer == 0 and has(s + 5):
                        if has(s + 3):
                            pool.wait_ge(gathered[1 - b], pair(s + 3) * 16 + 16)
                        gather(s + 5)
                    if has(s + 3):
                        seen(pool, a["var"], s + 3)
                        seen(pool, a["xn"], s + 1)
                        pool.tensor_tensor(rstd[:, 1 - b:2 - b], varp[:, 1 - b:2 - b], minus_half[:, 0:1], ALU.pow).then_inc(a["rstd"], 1)
                    if layer == 1 and has(s + 5):
                        seen(pool, y_added_all, s + 3)
                        i = place[:, s + 5] if isinstance(s, int) else place[:, bass.ds(s + 5, 1)].rearrange("p a c -> p (a c)")
                        pool.tensor_copy(place_now[:, 1 - b, :], i).then_inc(place_set, 1)
                        seen(pool, place_set, s + 5)
                    if has(s + 2):
                        seen(pool, a["k"], s + 2)
                        seen(pool, a["s_psum"], s)
                        k = kv[:, b, 0:D].rearrange("p (k n) -> p k n", k=KD)
                        pool.tensor_tensor(kT[:, b], k.unsqueeze(2).broadcast_to([P, KD, HPB, P]),
                                           own[layer][:].unsqueeze(1).unsqueeze(3).broadcast_to([P, KD, HPB, P]),
                                           ALU.mult).then_inc(a["keys"], 1)
                    if layer == 1 and has(s + 1):
                        seen(pool, a["xn"], s + 1)
                        pool.tensor_tensor(row(resid, s + 1), row(resid, s + 1), bproj[:], ALU.add).then_inc(a["biased"], 1)

                    if layer == 1 and has(s + 5):
                        for c in range(TOP):
                            pool.indirect_dma_start(yrow[:, 1 - b, c, :], None, placed_y,
                                                    bass.IndirectOffsetOnAxis(ap=place_now[:, 1 - b, c:c + 1].bitcast(U32), axis=0))\
                                .then_inc(y_gathered[1 - b], 16)

                if layer == 0:
                    for s in range(-5, SEQ):
                        step(s, s % 2)
                else:
                    skewed(pool, step, SEQ, 5, 0)

            attention(0)
            for g in range(G):
                pool.wait_ge(M["var"], g + 1)
                if g:
                    pool.wait_ge(M["xn"], GS * g)
                pool.tensor_tensor(mrstd[:], mvar[:], minus_half[:], ALU.pow).then_inc(M["rstd"], 1)
            pool.wait_ge(M["routed"], 1)
            pool.wait_ge(M["kept"], G)
            pool.wait_ge(places_filled, 16 * FILLS)
            for s in range(SEQ):
                for c in range(TOP):
                    pool.indirect_dma_start(placed_x, bass.IndirectOffsetOnAxis(ap=place[:, s, c:c + 1].bitcast(U32), axis=0),
                                            mxn[:, s, :], None).then_inc(scattered, 16)
            for b in range(2):
                pool.wait_ge(tile_out[b], 16 * NT // 2)
            attention(1)

            def ffn_step(s, b):
                if has(s):
                    seen(pool, F["half"], s)
                    seen(pool, F["u"], s)
                    seen(pool, F["pq"], s - 2)
                    pool.tensor_tensor(fp[:, b, :], fh[:, b, :], fu[:, b, :], ALU.mult).then_inc(F["prod"], 1)
                if has(s + 3):
                    seen(pool, F["var"], s + 3)
                    seen(pool, F["chain"], s + 1, 1, CH)
                    pool.tensor_tensor(frstd[:, 1 - b:2 - b], fvar[:, 1 - b:2 - b], minus_half[:, 0:1], ALU.pow).then_inc(F["rstd"], 1)

            skewed(pool, ffn_step, SEQ, 3, 2)

        @block.tensor
        def _(pe):
            def prepare():
                pe.wait_ge(attn_in, ATTN_LOADS)
                for n, (la, lb, k, lo, hi) in enumerate(((la1, lb1, 0, 0, 512), (la1, lb1, 0, 512, 768),
                                                         (la1, lb1, 1, 0, 512), (la1, lb1, 1, 512, 768),
                                                         (la2, lb2, 0, 0, 256), (la2, lb2, 1, 0, 256))):
                    if n >= 3:
                        pe.wait_ge(lora_added, n - 2)
                    pe.matmul(PS[:, 4 + n % 3, 0:hi - lo], la[:, k * P:(k + 1) * P], lb[:, lo:hi], start=True, stop=True).then_inc(lora_psum, 1)
                pe.wait_ge(consts, 3)
                pe.wait_ge(wst_summed, 3)
                pe.matmul(PS[:, 7, 0:4], ones[:], wabs[:], start=True, stop=True).then_inc(wsum_psum, 1)

            pe.wait_ge(tok_in, 80)
            for t in range(TG):
                for m in range(KH):
                    n = t * KH + m
                    if n >= 2:
                        pe.wait_ge(t_hid, n - 1)
                    for k in range(KD):
                        mm = pe.matmul(PS[:, n % 2], tw1[:, k, m * P:(m + 1) * P], cb[:, k, t * 512:(t + 1) * 512],
                                       start=(k == 0), stop=(k == KD - 1))
                    mm.then_inc(t_hid_psum, 1)
                pe.wait_ge(t_hid, (t + 1) * KH)
                for r in range(4):
                    n = t * 4 + r
                    if n >= 2:
                        pe.wait_ge(t_row, n - 1)
                    for k in range(KH):
                        mm = pe.matmul(PS[:, 2 + n % 2, 0:D], thid[:, k, r * P:(r + 1) * P], tw2[:, k, :],
                                       start=(k == 0), stop=(k == KH - 1))
                    mm.then_inc(t_row_psum, 1)
                if t == 0:
                    prepare()

            def attention(layer):
                a = A[layer]
                pe.wait_ge(weights_ready, 1)
                if layer == 0:
                    pe.wait_ge(t_row, 4 * TG)
                else:
                    pe.wait_ge(T["y"], NT)

                k_read, v_read = (a["k"], a["v_read"]) if layer == 0 else (a["k_read"], a["v_read"])

                def o_turn(s):
                    if has(s):
                        seen(pe, a["oraw"], s)
                        seen(pe, a["resid"], s - 1)
                        seen(pe, v_read, s + 3)
                        for t in range(4):
                            mm = pe.transpose(PS[:, 7, t * P:(t + 1) * P], oraw[:, t, :], ident[:])
                        mm.then_inc(a["o2_psum"], 1)

                def scores(s, b, half):
                    if has(s):
                        if half == 0:
                            seen(pe, a["q"], s)
                            seen(pe, a["keys"], s)
                            seen(pe, a["shifted"], s - 1)
                        for n in (2 * half, 2 * half + 1):
                            pe.matmul(PS[:, n, :], ident_b[:], causal_b[:].rearrange("p a k -> p (a k)"), start=True, stop=False)
                            kb, h = n // 2, n % 2 * 4
                            mm = pe.matmul(PS[:, n, :], qT[:, b, kb, :], kT[:, b, kb, h:h + 4, :].rearrange("p h k -> p (h k)"),
                                           start=False, stop=True)
                        if half:
                            mm.then_inc(a["s_psum"], 1)

                def x_turn(s):
                    if has(s):
                        seen(pe, a["xn"], s)
                        seen(pe, a["q"], s - 1)
                        seen(pe, k_read, s - 1)
                        for k in range(KD):
                            mm = pe.transpose(PS[:, 6, k * P:(k + 1) * P], xn[:, k * P:(k + 1) * P], ident[:])
                        mm.then_inc(a["xT_psum"], 1)

                def on_turn(s):
                    if has(s):
                        seen(pe, a["onrm"], s)
                        for k in range(KD):
                            mm = pe.transpose(PS[:, 7, k * P:(k + 1) * P], onrm[:, k * P:(k + 1) * P], ident[:])
                        mm.then_inc(a["oT_psum"], 1)

                def p_turn(s, b):
                    if has(s):
                        seen(pe, a["prob"], s)
                        for r in range(4):
                            if r < 2:
                                seen(pe, a["oraw"], s - 1)
                                seen(pe, a["pT"], s - 1, 4, 4)
                            else:
                                seen(pe, a["pT"], s, r - 1, 4)
                            for c in range(4):
                                mm = pe.transpose(PS[:, 4 + r % 2, c * P:(c + 1) * P], prob[:, b, 4 * r + c, :], ident[:])
                            mm.then_inc(a["pT_psum"], 1)

                def project(s):
                    if has(s):
                        seen(pe, a["xT"], s)
                        for n in range(4):
                            for k in range(KD):
                                mm = pe.matmul(PS[:, 6, n * P:(n + 1) * P], wqkv[layer][:, k, n * P:(n + 1) * P], xT[:, k, :],
                                               start=(k == 0), stop=(k == KD - 1))
                        mm.then_inc(a["qk_psum"], 1)
                        seen(pe, a["oT"], s - 4)
                        seen(pe, v_read, s - 1)
                        for k in range(KD):
                            mm = pe.matmul(PS[:, 7, 0:D], xT[:, k, :], wqkv[layer][:, k, 2 * D:3 * D],
                                           start=(k == 0), stop=(k == KD - 1))
                        mm.then_inc(a["v_psum"], 1)

                def pv(s, b):
                    if has(s):
                        seen(pe, a["v"], s)
                        seen(pe, a["pT"], s, 4, 4)
                        for t in range(4):
                            for c in range(4):
                                mm = pe.matmul(PS[SLOT * c:SLOT * (c + 1), 4, t * P:(t + 1) * P], V[:, b, 4 * t + c, :],
                                               probT[:, 4 * t + c, :], start=True, stop=True, tile_position=(0, SLOT * c))
                        mm.then_inc(a["o_psum"], 1)

                def out_proj(s):
                    if has(s):
                        seen(pe, a["oT"], s)
                        seen(pe, v_read, s + 4)
                        for k in range(KD):
                            mm = pe.matmul(PS[:, 7, 0:D], oT[:, k, :], wout[layer][:, k, :], start=(k == 0), stop=(k == KD - 1))
                        mm.then_inc(a["y_psum"], 1)

                def step(s, b):
                    scores(s, b, 0)
                    o_turn(s - 2)
                    x_turn(s + 2)
                    scores(s, b, 1)
                    on_turn(s - 2)
                    project(s + 2)
                    p_turn(s - 1, 1 - b)
                    pv(s - 1, 1 - b)
                    out_proj(s - 2)

                skewed(pe, step, SEQ, 2, 2)

            attention(0)

            pe.wait_ge(A[0]["resid"], SEQ)
            pe.wait_ge(exp_in, 2 * EA * 16)

            def xn_turn(g, b, sems):
                if has(g, G):
                    if sems is M:
                        seen(pe, M["xn"], g, GS, GS, G)
                        bank = 4
                    else:
                        seen(pe, S["staged"], g, 1, 1, G)
                        bank = 6
                    seen(pe, sems["xT"], g - 1, KD, KD, G)
                    for k in range(KD):
                        for t in range(GS):
                            mm = pe.transpose(PS[:, bank + k, t * P:(t + 1) * P], staged[:, b, t, k * P:(k + 1) * P], ident[:])
                        mm.then_inc(sems["xT_psum"], 1)

            def route(g, b):
                if has(g, G):
                    seen(pe, M["xT"], g, KD, KD, G)
                    for t in range(GS):
                        at = (g * GS + t) * E
                        dst = PS[:, 7, at:at + E] if isinstance(g, int) else PS[:, 7, bass.ds(at, E)]
                        for k in range(KD):
                            mm = pe.matmul(dst, mxT[:, b, k, t * P:(t + 1) * P], gw[:, k, :],
                                           start=(k == 0), stop=(k == KD - 1))
                    mm.then_inc(M["route_psum"], 1)

            def route_step(g, b):
                xn_turn(g + 1, 1 - b, M)
                route(g, b)

            skewed(pe, route_step, G, 1, 0)

            def prefixes():
                pe.wait_ge(M["selected"], 1)
                sel = selected[:].rearrange("p s e -> p (s e)")
                pe.matmul(PS[:, 5, 0:SEQ * E], earlier[:], sel, start=True, stop=True)
                pe.matmul(PS[:, 5, SEQ * E:2 * SEQ * E], ones[:], sel, start=True, stop=True).then_inc(M["prefix_psum"], 1)

            def up(g, b, e):
                for h in range(KI):
                    if e:
                        seen(pe, S["hT"], g, (e - 1) * KI + h + 1, NS * KI, G)
                    else:
                        seen(pe, S["hT"], g - 1, (NS - 1) * KI + h + 1, NS * KI, G)
                    for u in range(2):
                        for k in range(KD):
                            mm = pe.matmul(PS[:, 2 * h + u], w13_sb[:, E + e, k, u * INTER + h * P:u * INTER + (h + 1) * P],
                                           mxT[:, b, k, :], start=(k == 0), stop=(k == KD - 1))
                    mm.then_inc(S["up_psum"], 1)

            def down(g, e):
                if not has(g, G):
                    return
                seen(pe, S["hT"], g, (e + 1) * KI, NS * KI, G)
                for t in range(GS):
                    if t % 2 == 0:
                        if e:
                            seen(pe, S["resid"], g, (e - 1) * GS + t + 2, NS * GS, G)
                        else:
                            seen(pe, S["resid"], g - 1, (NS - 1) * GS + t + 2, NS * GS, G)
                    for k in range(KI):
                        mm = pe.matmul(PS[:, 4 + t // 2, t % 2 * D:(t % 2 + 1) * D], hT[:, e % 2, k, t * P:(t + 1) * P],
                                       w2_sb[:, E + e, k, :], start=(k == 0), stop=(k == KI - 1), skip_group_check=True)
                    if t % 2:
                        mm.then_inc(S["down_psum"], 1)

            prefixes()

            def shared_step(g, b):
                if has(g, G):
                    seen(pe, S["xT"], g, KD, KD, G)
                    up(g, b, 0)
                down(g - 1, NS - 1)
                xn_turn(g + 1, 1 - b, S)
                if has(g, G):
                    for e in range(1, NS):
                        up(g, b, e)
                        down(g, e - 1)

            skewed(pe, shared_step, G, 1, 1)

            pe.wait_ge(S["resid"], G * NS * GS)

            def tile_turn(j, b):
                if has(j, NT):
                    pe.wait_ge(tile_in[b], pair(j) * 16 + (32 if b == 0 else 16))
                    seen(pe, T["xT"], j - 1, 1, 1, NT)
                    for k in range(KD):
                        mm = pe.transpose(PS[:, 2, k * P:(k + 1) * P], ex[:, b, k * P:(k + 1) * P], ident[:])
                    mm.then_inc(T["xT_psum"], 1)

            def hidden_turn(j, b):
                if has(j, NT):
                    seen(pe, T["h"], j, 1, 1, NT)
                    for k in range(KI):
                        mm = pe.transpose(PS[:, 3, k * P:(k + 1) * P], eh[:, b, k * P:(k + 1) * P], ident[:])
                    mm.then_inc(T["hT_psum"], 1)

            tile_experts = []

            def tile_up(j, b):
                if has(j, NT):
                    at = tile_expert[0:1, j:j + 1] if isinstance(j, int) else tile_expert[0:1, bass.ds(j, 1)]
                    e = pe.value_load(at, min_val=0, max_val=E - 1)
                    tile_experts.append(e)
                    seen(pe, T["xT"], j, 1, 1, NT)
                    for k in range(KD):
                        mm = pe.matmul(PS[:, b], exT[:, b, k, :], w13_sb[:, bass.ds(e, 1), k, :].rearrange("p a n -> p (a n)"),
                                       start=(k == 0), stop=(k == KD - 1))
                    mm.then_inc(T["up_psum"], 1)

            def tile_down(j, b):
                if has(j, NT):
                    at = tile_expert[0:1, j:j + 1] if isinstance(j, int) else tile_expert[0:1, bass.ds(j, 1)]
                    e = pe.value_load(at, min_val=0, max_val=E - 1)
                    seen(pe, T["hT"], j, 1, 1, NT)
                    seen(pe, T["y"], j - 2, 1, 1, NT)
                    for k in range(KI):
                        mm = pe.matmul(PS[:, 4 + b, 0:D], ehT[:, k, :], w2_sb[:, bass.ds(e, 1), k, :].rearrange("p a n -> p (a n)"),
                                       start=(k == 0), stop=(k == KI - 1))
                    mm.then_inc(T["down_psum"], 1)

            def tile_step(j, b):
                tile_turn(j + 3, 1 - b)
                hidden_turn(j, b)
                tile_up(j + 2, b)
                tile_down(j, b)

            pe.wait_ge(M["routed"], 1)
            skewed(pe, tile_step, NT, 3, 2)

            attention(1)

            pe.wait_ge(A[1]["resid"], SEQ)

            def q_turn(s, b):
                if has(s):
                    seen(pe, F["q"], s)
                    seen(pe, F["xT"], s - 1)
                    for k in range(KD):
                        mm = pe.transpose(PS[:, 4, k * P:(k + 1) * P], fq[:, b, k * P:(k + 1) * P], ident[:])
                    mm.then_inc(F["q_psum"], 1)

            def ffn_up(s):
                if has(s):
                    seen(pe, F["xT"], s)
                    seen(pe, F["half"], s - 1)
                    seen(pe, F["u"], s - 1)
                    for n in range(2 * INNER // 512):
                        for k in range(KD):
                            mm = pe.matmul(PS[:, n], fxT[:, k, :], wgu_q[:, k, n * 512:(n + 1) * 512],
                                           start=(k == 0), stop=(k == KD - 1))
                    mm.then_inc(F["up_psum"], 1)

            def p_turn(s, b):
                if has(s):
                    seen(pe, F["pq"], s)
                    seen(pe, F["pT"], s - 1)
                    for k in range(KN):
                        mm = pe.transpose(PS[:, 5 + k // 4, k % 4 * P:(k % 4 + 1) * P], fpq[:, b, k * P:(k + 1) * P], ident[:])
                    mm.then_inc(F["pq_psum"], 1)

            def ffn_down(s):
                if has(s):
                    seen(pe, F["pT"], s)
                    seen(pe, F["resid"], s - 1)
                    for k in range(KN):
                        mm = pe.matmul(PS[:, 7, 0:D], fpT[:, k, :], wdn_q[:, k, :], start=(k == 0), stop=(k == KN - 1))
                    mm.then_inc(F["down_psum"], 1)

            def ffn_step(s, b):
                ffn_up(s + 1)
                ffn_down(s - 2)
                q_turn(s + 2, b)
                p_turn(s - 1, 1 - b)

            skewed(pe, ffn_step, SEQ, 2, 2)

        @block.scalar
        def _(act):
            act.wait_ge(tok_in, 80)

            def more_loads():
                act.wait_ge(ffn_in, 2 * (KD + 1) * 16)
                for e in range(EA):
                    act.dma_start(w13_sb[:, e], kt(w13[e])).then_inc(exp_in, 16)
                    act.dma_start(w2_sb[:, e], kt(w2[e])).then_inc(exp_in, 16)
                n = NT // FILLS
                act.wait_ge(consts, 4)
                for c in range(FILLS):
                    act.dma_start(placed_x[c * n * P:(c + 1) * n * P, :].rearrange("(n p) d -> p n d", p=P),
                                  zeros[:].unsqueeze(1).broadcast_to([P, n, D])).then_inc(places_filled, 16)

            for t in range(TG):
                for m in range(KH):
                    n = t * KH + m
                    act.wait_ge(t_hid_psum, n + 1)
                    if t:
                        act.wait_ge(t_row_psum, 4 * t)
                    nc.scalar.activation(thid[:, m, :], PS[:, n % 2], ACT.Gelu_apprx_tanh, bias=tb1[:, m:m + 1]).then_inc(t_hid, 1)
                if t == 1:
                    more_loads()

            def attention(layer):
                a = A[layer]

                def x_copy(s):
                    if has(s):
                        seen(act, a["xT_psum"], s)
                        nc.scalar.copy(xT[:].rearrange("p k n -> p (k n)"), PS[:, 6, 0:D]).then_inc(a["xT"], 1)

                def o_copy(s):
                    if has(s):
                        seen(act, a["oT_psum"], s)
                        seen(act, a["y_psum"], s - 1)
                        nc.scalar.copy(oT[:].rearrange("p k n -> p (k n)"), PS[:, 7, 0:D]).then_inc(a["oT"], 1)

                def p_copy(s):
                    if has(s):
                        seen(act, a["o_psum"], s - 1)
                        for r in range(4):
                            seen(act, a["pT_psum"], s, r + 1, 4)
                            nc.scalar.copy(probT[:, 4 * r:4 * r + 4, :].rearrange("p a n -> p (a n)"), PS[:, 4 + r % 2, :]).then_inc(a["pT"], 1)

                def q_copy(s, b):
                    if has(s):
                        seen(act, a["qk_psum"], s)
                        if layer == 0:
                            nc.scalar.mul(qT[:, b].rearrange("p k n -> p (k n)"), PS[:, 6, 0:D], DH ** -0.5).then_inc(a["q"], 1)
                            seen(act, a["keys"], s - 2)
                            nc.scalar.copy(kv[:, b, 0:D], PS[:, 6, D:2 * D]).then_inc(a["k"], 1)
                        else:
                            for k in range(KD):
                                ins = nc.scalar.activation(qT[:, b, k, :], PS[:, 6, k * P:(k + 1) * P], ACT.Identity,
                                                           bias=bq_scaled[:, k:k + 1], scale=DH ** -0.5)
                            ins.then_inc(a["q"], 1)

                def exps(s, b):
                    if has(s):
                        seen(act, a["shifted"], s)
                        v = prob[:, b].rearrange("p a n -> p (a n)")
                        nc.scalar.activation(v, v, ACT.Exp).then_inc(a["prob"], 1)

                def raw_copy(s):
                    if has(s):
                        seen(act, a["o_psum"], s)
                        seen(act, a["o2_psum"], s - 1)
                        nc.scalar.copy(oraw[:].rearrange("p a n -> p (a n)"), PS[:, 4, :]).then_inc(a["oraw"], 1)

                def step(s, b):
                    x_copy(s + 2)
                    o_copy(s - 2)
                    q_copy(s + 2, b)
                    p_copy(s - 1)
                    raw_copy(s - 1)
                    exps(s, b)

                skewed(act, step, SEQ, 2, 2)

            act.wait_ge(weights_ready, 1)
            act.wait_ge(consts, 3)
            attention(0)

            act.wait_ge(A[0]["resid"], SEQ)

            def xT_copy(g, b, sems):
                if has(g, G):
                    bank = 4 if sems is M else 6
                    if sems is M:
                        seen(act, M["route_psum"], g - 2, 1, 1, G)
                    else:
                        seen(act, S["up_psum"], g - 2, NS * KI, NS * KI, G)
                    for k in range(KD):
                        seen(act, sems["xT_psum"], g, k + 1, KD, G)
                        nc.scalar.copy(mxT[:, b, k, :], PS[:, bank + k, :]).then_inc(sems["xT"], 1)

            def route_step(g, b):
                xT_copy(g, b, M)
                if has(g, G):
                    seen(act, M["xn"], g, GS, GS, G)
                    dst = mxn[:, g * GS:(g + 1) * GS] if isinstance(g, int) else mxn[:, bass.ds(g * GS, GS)]
                    nc.scalar.copy(dst.rearrange("p t d -> p (t d)"), staged[:, b].rearrange("p t d -> p (t d)")).then_inc(M["kept"], 1)

            skewed(act, route_step, G, 0, 2)

            act.wait_ge(M["route_max"], 1)
            v = score[:].rearrange("p a e -> p (a e)")
            nc.scalar.activation(v, v, ACT.Exp).then_inc(M["route_exp"], 1)

            def shared_step(g, b):
                if has(g, G):
                    for e in range(NS):
                        for h in range(KI):
                            n = e * KI + h
                            seen(act, S["up_psum"], g, n + 1, NS * KI, G)
                            if n >= 2:
                                seen(act, S["half"], g, n - 1, NS * KI, G)
                            else:
                                seen(act, S["half"], g - 1, NS * KI - 1 + n, NS * KI, G)
                            nc.scalar.activation(tnh[:, h, :], PS[:, 2 * h], ACT.Tanh, scale=0.5).then_inc(S["tanh"], 1)
                        if e == 0:
                            xT_copy(g + 1, 1 - b, S)
                else:
                    xT_copy(g + 1, 1 - b, S)

            act.wait_ge(M["routed"], 1)
            skewed(act, shared_step, G, 1, 1)

            def tile_copy(j, b):
                if has(j, NT):
                    seen(act, T["xT_psum"], j, 1, 1, NT)
                    seen(act, T["up_psum"], j - 2, 1, 1, NT)
                    nc.scalar.copy(exT[:, b].rearrange("p k n -> p (k n)"), PS[:, 2, 0:D]).then_inc(T["xT"], 1)

            def hidden_copy(j):
                if has(j, NT):
                    seen(act, T["hT_psum"], j, 1, 1, NT)
                    seen(act, T["down_psum"], j - 1, 1, 1, NT)
                    nc.scalar.copy(ehT[:].rearrange("p k n -> p (k n)"), PS[:, 3, 0:INTER]).then_inc(T["hT"], 1)

            def tile_tanh(j, b):
                if has(j, NT):
                    seen(act, T["up_psum"], j, 1, 1, NT)
                    seen(act, T["half"], j - 2, 1, 1, NT)
                    nc.scalar.activation(etanh[:, b, :], PS[:, b, 0:INTER], ACT.Tanh, scale=0.5).then_inc(T["tanh"], 1)

            def tile_step(j, b):
                tile_copy(j + 3, 1 - b)
                hidden_copy(j)
                tile_tanh(j + 2, b)

            act.wait_ge(S["resid"], G * NS * GS)
            skewed(act, tile_step, NT, 3, 2)

            act.wait_ge(T["y"], NT)
            attention(1)
            act.wait_ge(A[1]["resid"], SEQ)

            def fx_copy(s):
                if has(s):
                    seen(act, F["q_psum"], s)
                    seen(act, F["up_psum"], s - 1)
                    nc.scalar.activation(fxT[:].rearrange("p k n -> p (k n)"), PS[:, 4, 0:D], ACT.Identity, bias=minus_round[:, 0:1])\
                      .then_inc(F["xT"], 1)

            def ftanh(s, b):
                if has(s):
                    seen(act, F["up_psum"], s)
                    seen(act, F["scales"], s)
                    seen(act, F["half"], s - 1)
                    nc.scalar.activation(ft[:], PS[:, 0:2].rearrange("p a n -> p (a n)"), ACT.Tanh, scale=fs[:, b, 4:5]).then_inc(F["tanh"], 1)

            def fu_copy(s, b):
                if has(s):
                    seen(act, F["prod"], s - 2)
                    nc.scalar.copy(fu[:, b, :], PS[:, 2:4].rearrange("p a n -> p (a n)")).then_inc(F["u"], 1)

            def fp_copy(s):
                if has(s):
                    seen(act, F["pq_psum"], s)
                    seen(act, F["down_psum"], s - 1)
                    nc.scalar.activation(fpT[:].rearrange("p k n -> p (k n)"), PS[:, 5:7].rearrange("p a n -> p (a n)"), ACT.Identity,
                                         bias=minus_round[:, 0:1]).then_inc(F["pT"], 1)

            def ffn_step(s, b):
                ftanh(s + 1, 1 - b)
                fx_copy(s + 2)
                fu_copy(s + 1, 1 - b)
                fp_copy(s - 1)

            skewed(act, ffn_step, SEQ, 2, 2)

        @block.vector
        def _(dve):
            done = [0]

            def after_me(ins):
                done[0] += 1
                ins.then_inc(prep, 1)
                dve.wait_ge(prep, done[0])

            dve.wait_ge(attn_in, ATTN_LOADS)
            dve.tensor_copy(ident_b[:], ident[:])
            for c in range(4):
                dve.tensor_copy(causal_b[:, c, :], causal[:])
            dve.tensor_scalar(bq_scaled[:], bqk[:, 0:KD], DH ** -0.5, None, ALU.mult)
            after_me(dve.reciprocal(kvinv[:], kvs[:]))
            v = wst[:].rearrange("p (u n) -> p u n", u=2)
            dve.wait_ge(ffn_in, 16)
            dve.tensor_reduce(wabs[:, 0:2], v, AX.X, ALU.add, apply_absolute_value=True).then_inc(wst_summed, 1)
            dve.wait_ge(ffn_in, 32)
            dve.tensor_reduce(wabs[:, 2:4], v, AX.X, ALU.add, apply_absolute_value=True).then_inc(wst_summed, 1)
            dve.wait_ge(wst_summed, 2)
            after_me(dve.tensor_tensor(wabs[:, 0:2], wabs[:, 0:2], wabs[:, 2:4], ALU.add))
            after_me(dve.memset(wabs[:, 3:4], 0.0))
            dve.wait_ge(ffn_in, 48)
            dve.tensor_reduce(wabs[:, 2:3], wst[:], AX.X, ALU.add, apply_absolute_value=True).then_inc(wst_summed, 1)

            def table_rows(t):
                dve.wait_ge(tok_in, 80)
                for n in range(4 * t, 4 * t + 4):
                    dve.wait_ge(t_row_psum, n + 1)
                    if n >= 4:
                        dve.wait_ge(t_store[n % 4], 16 * (n // 4))
                    dve.tensor_tensor(trow[:, n % 4, :], PS[:, 2 + n % 2, 0:D], tb2[:], ALU.add).then_inc(t_row, 1)

            table_rows(0)
            dve.tensor_scalar(own[1][:], own[0][:], kvs[:, 0:1], None, ALU.mult)
            for k in range(KD):
                dve.tensor_scalar(wqkv[0][:, k, :], wqkv[0][:, k, :], gln[:, k:k + 1], None, ALU.mult)
            for n, (w, k, lo, hi) in enumerate(((wqkv[1], 0, 0, 512), (wqkv[1], 0, 512, 768), (wqkv[1], 1, 0, 512),
                                                (wqkv[1], 1, 512, 768), (wout[1], 0, 0, 256), (wout[1], 1, 0, 256))):
                dve.wait_ge(lora_psum, n + 1)
                dve.scalar_tensor_tensor(w[:, k, lo:hi], PS[:, 4 + n % 3, 0:hi - lo], 2.0, w[:, k, lo:hi], ALU.mult, ALU.add)\
                   .then_inc(lora_added, 1)
            dve.wait_ge(wsum_psum, 1)
            after_me(dve.tensor_scalar(wmean[:], PS[:, 7, 0:4], 1.0 / (D * INNER), EPS, ALU.mult, ALU.max))
            after_me(dve.reciprocal(wscale[:], wmean[:]))
            after_me(dve.reciprocal(winv[:], wscale[:]))

            def ternary(dst, src, which):
                after_me(dve.tensor_scalar(src, src, wscale[:, which:which + 1], ROUND, ALU.mult, ALU.add))
                after_me(dve.tensor_scalar(src, src, -ROUND, 1.0, ALU.add, ALU.min))
                return dve.tensor_scalar(dst, src, -1.0, None, ALU.max)

            for n in range(KD):
                dve.wait_ge(ffn_in, 64 + 16 * n)
                after_me(ternary(wgu_q[:, n, 0:INNER], wst[:, 0:INNER], 0))
                ternary(wgu_q[:, n, INNER:], wst[:, INNER:], 1).then_inc(wst_quantized, 1)
            dve.wait_ge(ffn_in, 96)
            ternary(wdn_q[:].rearrange("p k n -> p (k n)"), wst[:], 2).then_inc(weights_ready, 1)

            for t in range(1, TG):
                table_rows(t)

            def attention(layer):
                a = A[layer]
                if layer == 0:
                    for t in range(4):
                        dve.wait_ge(t_store[t], 16 * TG)
                dve.memset(V[:].rearrange("p b h n -> p (b h n)"), 1.0).then_inc(a["v_ones"], 1)
                dve.wait_ge(a["v_ones"], 1)

                def norm(s, b):
                    if has(s):
                        seen(dve, a["rstd"], s)
                        seen(dve, a["xT_psum"], s - 1)
                        dve.tensor_scalar(xn[:], row(resid, s), mv[:, b, 0:1], rstd[:, b:b + 1], ALU.subtract, ALU.mult).then_inc(a["xn"], 1)

                def o_norm(s):
                    seen(dve, a["stats"], s + 5)
                    if has(s):
                        seen(dve, a["o2_psum"], s)
                        o = PS[:, 7].rearrange("p (h n) -> p h n", n=SLOT)
                        dve.reciprocal(rden[:], o[:, :, DH]).then_inc(a["rden"], 1)
                        seen(dve, a["rden"], s)
                        seen(dve, a["oT_psum"], s - 1)
                        dve.tensor_tensor(onrm[:].rearrange("p (h n) -> p h n", n=DH), o[:, :, 0:DH],
                                          spread(rden[:], DH),
                                          ALU.mult).then_inc(a["onrm"], 1)

                def softmax(s, b):
                    if has(s):
                        seen(dve, a["s_psum"], s)
                        sc = PS[:, 0:4].rearrange("p r (c k) -> p (r c) k", k=P)
                        dve.tensor_reduce(rmax[:], sc, AX.X, ALU.max).then_inc(a["rmax"], 1)
                        seen(dve, a["rmax"], s)
                        seen(dve, a["pT_psum"], s - 2, 4, 4)
                        dve.tensor_tensor(prob[:, b], sc, spread(rmax[:], P),
                                          ALU.subtract).then_inc(a["shifted"], 1)

                def values(s, b):
                    if has(s) and layer == 0:
                        seen(dve, a["v_psum"], s)
                        dve.tensor_copy(kv[:, b, D:2 * D], PS[:, 7, 0:D]).then_inc(a["v_read"], 1)

                def fake_quant(s, b):
                    if has(s) and layer == 1:
                        t = kv[:, b, :]
                        seen(dve, a["qk_psum"], s)
                        seen(dve, a["q"], s)
                        seen(dve, a["keys"], s - 2)
                        for k in range(KD):
                            ins = dve.tensor_scalar(kv[:, b, k * P:(k + 1) * P], PS[:, 6, D + k * P:D + (k + 1) * P],
                                                    bqk[:, KD + k:KD + k + 1], None, ALU.add)
                        ins.then_inc(a["k_read"], 1)
                        seen(dve, a["v_psum"], s)
                        dve.tensor_tensor(kv[:, b, D:2 * D], PS[:, 7, 0:D], bv[:], ALU.add).then_inc(a["v_read"], 1)
                        seen(dve, a["k_read"], s)
                        seen(dve, a["v_read"], s)
                        dve.tensor_scalar(t, t, kvinv[:, 0:1], kvz[:, 0:1], ALU.mult, ALU.add).then_inc(a["chain"], 1)
                        seen(dve, a["chain"], s, 1, 4)
                        dve.tensor_scalar(t, t, 0.0, 255.0, ALU.max, ALU.min).then_inc(a["chain"], 1)
                        seen(dve, a["chain"], s, 2, 4)
                        dve.tensor_scalar(t, t, ROUND, -ROUND, ALU.add, ALU.add).then_inc(a["chain"], 1)
                        seen(dve, a["chain"], s, 3, 4)
                        dve.tensor_scalar(kv[:, b, 0:D], kv[:, b, 0:D], kvz[:, 0:1], None, ALU.subtract).then_inc(a["k"], 1)
                        dve.tensor_scalar(kv[:, b, D:2 * D], kv[:, b, D:2 * D], kvz[:, 0:1], kvs[:, 0:1],
                                          ALU.subtract, ALU.mult).then_inc(a["chain"], 1)

                def v_store(s, b):
                    if has(s):
                        seen(dve, a["o_psum"], s - 2)
                        if layer == 0:
                            seen(dve, a["v_read"], s)
                        else:
                            seen(dve, a["chain"], s, 4, 4)
                        dve.tensor_copy(V[:, b, :, 0:DH], kv[:, b, D:2 * D].rearrange("p (h n) -> p h n", n=DH)).then_inc(a["v"], 1)

                def add(s):
                    if has(s):
                        seen(dve, a["y_psum"], s)
                        if layer == 1:
                            seen(dve, a["biased"], s)
                        dve.tensor_tensor(row(resid, s), row(resid, s), PS[:, 7, 0:D], ALU.add).then_inc(a["resid"], 1)

                def routed_add(s, b, c):
                    if has(s) and layer == 1:
                        if c == 0:
                            dve.wait_ge(y_gathered[b], pair(s) * 32 + 32)
                        else:
                            seen(dve, y_added, s)
                        g = gate[:, c, s:s + 1] if isinstance(s, int) else gate[:, c, bass.ds(s, 1)]
                        dve.scalar_tensor_tensor(row(resid, s), yrow[:, b, c, :], g, row(resid, s), ALU.mult, ALU.add)\
                           .then_inc(y_added if c == 0 else y_added_all, 1)

                def moments(s, b):
                    if has(s):
                        if layer == 0:
                            dve.wait_ge(gathered[b], pair(s) * 16 + 16)
                        dve.bn_stats(stats[:], row(resid, s)).then_inc(a["stats"], 1)

                def moments_end(s, b):
                    if has(s):
                        dve.bn_aggr(mv[:, b, :], stats[:]).then_inc(a["aggr"], 1)
                        seen(dve, a["aggr"], s)
                        if layer == 0:
                            dve.tensor_scalar(varp[:, b:b + 1], mv[:, b, 1:2], 1.0 + EPS, EPS * EPS, ALU.mult, ALU.add).then_inc(a["var"], 1)
                        else:
                            dve.tensor_scalar(varp[:, b:b + 1], mv[:, b, 1:2], EPS, None, ALU.add).then_inc(a["var"], 1)

                def step(s, b):
                    if layer == 1:
                        seen(dve, y_added_all, s + 3)
                    norm(s + 2, b)
                    moments(s + 3, 1 - b)
                    o_norm(s - 2)
                    moments_end(s + 3, 1 - b)
                    softmax(s, b)
                    values(s + 2, b)
                    fake_quant(s + 2, b)
                    routed_add(s + 4, b, 0)
                    v_store(s + 1, 1 - b)
                    add(s - 2)
                    routed_add(s + 4, b, 1)

                skewed(dve, step, SEQ, 4, 2)

            attention(0)

            dve.wait_ge(A[0]["resid"], SEQ)

            def moments(g):
                if has(g, G):
                    for t in range(GS):
                        ins = dve.bn_stats(mstats[:, t, :], row(resid, g * GS + t))
                    ins.then_inc(M["stats"], 1)

            def moments_end(g, b):
                if has(g, G):
                    for t in range(GS):
                        ins = dve.bn_aggr(mmv[:, b, t, :], mstats[:, t, :])
                    ins.then_inc(M["aggr"], 1)
                    seen(dve, M["aggr"], g, 1, 1, G)
                    dve.tensor_scalar(mvar[:], mmv[:, b, :, 1], EPS, None, ALU.add).then_inc(M["var"], 1)

            def norm(g, b):
                seen(dve, M["stats"], g + 1, 1, 1, G)
                if has(g, G):
                    seen(dve, M["rstd"], g, 1, 1, G)
                    seen(dve, M["xn"], g - 1, GS, GS, G)
                    seen(dve, M["xT_psum"], g - 2, KD, KD, G)
                    seen(dve, M["kept"], g - 2, 1, 1, G)
                    for t in range(GS):
                        dve.tensor_scalar(staged[:, b, t, :], row(resid, g * GS + t), mmv[:, b, t, 0:1], mrstd[:, t:t + 1],
                                          ALU.subtract, ALU.mult).then_inc(M["xn"], 1)

            def route_step(g, b):
                moments(g + 1)
                norm(g, b)
                moments_end(g + 1, 1 - b)

            skewed(dve, route_step, G, 1, 2)

            n_chain = [0]

            def then(ins):
                n_chain[0] += 1
                ins.then_inc(M["chain"], 1)
                dve.wait_ge(M["chain"], n_chain[0])

            def over(v, n=E):
                return spread(v, n)

            def each(v, n):
                return v.unsqueeze(1).broadcast_to([P, n, v.shape[1]])

            def total(dst, src):
                then(dve.tensor_reduce(dst, src, AX.X, ALU.add))

            for i, v in enumerate(counts):
                ins = dve.memset(v[:, 0:PAD, :].rearrange("p s e -> p (s e)"), 0.0)
            for i, v in enumerate(tiles):
                ins = dve.memset(v[:, 0:E], 0.0)
            then(ins)
            dve.wait_ge(M["route_psum"], G)
            logits = PS[:, 7, 0:SEQ * E].rearrange("p (s e) -> p s e", e=E)
            then(dve.tensor_reduce(per_token[:], logits, AX.X, ALU.max))
            dve.tensor_tensor(score[:], logits, over(per_token[:]), ALU.subtract).then_inc(M["route_max"], 1)
            dve.wait_ge(M["route_exp"], 1)
            total(per_token[:], score[:])
            then(dve.reciprocal(per_token[:], per_token[:]))
            then(dve.tensor_tensor(score[:], score[:], over(per_token[:]), ALU.mult))
            then(dve.tensor_tensor(biased[:], score[:], each(gbias[:], SEQ), ALU.add))
            for turn in range(TOP):
                then(dve.tensor_reduce(per_token[:], biased[:], AX.X, ALU.max))
                then(dve.tensor_tensor(tie[:], biased[:], over(per_token[:]), ALU.is_equal))
                then(dve.tensor_tensor(tie[:], tie[:], each(rank[:], SEQ), ALU.mult))
                then(dve.tensor_reduce(per_token[:], tie[:], AX.X, ALU.max))
                then(dve.tensor_tensor(chosen[turn][:], tie[:], over(per_token[:]), ALU.is_equal))
                if turn == 0:
                    then(dve.scalar_tensor_tensor(biased[:], chosen[0][:], -BIG, biased[:], ALU.mult, ALU.add))
            dve.tensor_tensor(selected[:], chosen[0][:], chosen[1][:], ALU.add).then_inc(M["selected"], 1)
            for c in range(TOP):
                then(dve.tensor_tensor(tie[:], chosen[c][:], score[:], ALU.mult))
                total(gate[:, c, :], tie[:])
            g_all = gate[:].rearrange("p c s -> p (c s)")
            then(dve.tensor_scalar(g_all, g_all, 0.5, None, ALU.mult))
            dve.wait_ge(M["prefix_psum"], 1)
            within = PS[:, 5, 0:SEQ * E].rearrange("p (s e) -> p s e", e=E)
            then(dve.tensor_copy(counts[0][:, PAD:, :].rearrange("p s e -> p (s e)"), PS[:, 5, SEQ * E:2 * SEQ * E]))
            at, d, flip = 0, 1, 1
            while d < SEQ:
                then(dve.tensor_tensor(counts[flip][:, PAD:, :], counts[at][:, PAD:, :], counts[at][:, PAD - d:PAD + SEQ - d, :], ALU.add))
                at, flip, d = flip, 3 - flip, 2 * d
            upto = counts[at]
            then(dve.tensor_scalar(tiles[0][:, E:], upto[:, PAD + SEQ - 1, :], 1.0 / P, (P / 2 - 0.5) / P, ALU.mult, ALU.add))
            then(dve.tensor_scalar(tiles[0][:, E:], tiles[0][:, E:], ROUND, -ROUND, ALU.add, ALU.add))
            t_at, d, flip = 0, 1, 1
            while d < E:
                then(dve.tensor_tensor(tiles[flip][:, E:], tiles[t_at][:, E:], tiles[t_at][:, E - d:2 * E - d], ALU.add))
                t_at, flip, d = flip, 3 - flip, 2 * d
            ends = tiles[t_at]
            then(dve.tensor_tensor(start[:], ends[:, E:], tiles[0][:, E:], ALU.subtract))
            then(dve.tensor_scalar(start[:], start[:], float(P), None, ALU.mult))
            then(dve.tensor_tensor(biased[:], upto[:, PAD:, :], within, ALU.add))
            then(dve.tensor_tensor(biased[:], biased[:], counts[0][:, PAD:, :], ALU.subtract))
            then(dve.tensor_tensor(biased[:], biased[:], each(start[:], SEQ), ALU.add))
            for c in range(TOP):
                then(dve.tensor_tensor(tie[:], chosen[c][:], biased[:], ALU.mult))
                total(place_f[:, :, c], tie[:])
            then(dve.tensor_copy(place[:].rearrange("p s c -> p (s c)"), place_f[:].rearrange("p s c -> p (s c)")))
            dve.wait_ge(tile_in[0], 16)
            then(dve.tensor_tensor(beyond[:], over(tile_no[:], E - 1), each(ends[:, E:2 * E - 1], NT), ALU.is_ge))
            total(tile_expert_f[:], beyond[:])
            dve.tensor_copy(tile_expert[:], tile_expert_f[0:1, :]).then_inc(M["routed"], 1)

            def shared_add(g, e):
                if not has(g, G):
                    return
                for t in range(GS):
                    if t % 2 == 0:
                        seen(dve, S["down_psum"], g, e * 2 + t // 2 + 1, NS * 2, G)
                    r = row(resid, g * GS + t)
                    dve.scalar_tensor_tensor(r, PS[:, 4 + t // 2, t % 2 * D:(t % 2 + 1) * D], 0.5, r,
                                             ALU.mult, ALU.add).then_inc(S["resid"], 1)

            dve.wait_ge(M["kept"], G)

            def stage(g, b):
                if has(g, G):
                    if has(g - 2, G):
                        seen(dve, S["xT_psum"], g - 2, KD, KD, G)
                    src = mxn[:, g * GS:(g + 1) * GS] if isinstance(g, int) else mxn[:, bass.ds(g * GS, GS)]
                    dve.tensor_copy(staged[:, b].rearrange("p t d -> p (t d)"), src.rearrange("p t d -> p (t d)")).then_inc(S["staged"], 1)

            def shared_step(g, b):
                if has(g, G):
                    for e in range(NS):
                        for h in range(KI):
                            n = e * KI + h
                            seen(dve, S["tanh"], g, n + 1, NS * KI, G)
                            dve.scalar_tensor_tensor(act_[:, h, :], tnh[:, h, :], 1.0, PS[:, 2 * h], ALU.add, ALU.mult).then_inc(S["half"], 1)
                            seen(dve, S["half"], g, n + 1, NS * KI, G)
                            if h == 0:
                                seen(dve, S["down_psum"], g - 1, (e + 1) * 2, NS * 2, G)
                            dve.tensor_tensor(hT[:, e % 2, h, :], act_[:, h, :], PS[:, 2 * h + 1], ALU.mult).then_inc(S["hT"], 1)
                        if e:
                            shared_add(g, e - 1)
                        else:
                            shared_add(g - 1, NS - 1)
                else:
                    shared_add(g - 1, NS - 1)
                stage(g + 2, b)

            skewed(dve, shared_step, G, 2, 1)

            def tile_hidden(j, b):
                if has(j, NT):
                    seen(dve, T["tanh"], j, 1, 1, NT)
                    dve.scalar_tensor_tensor(eact[:, b, :], etanh[:, b, :], 1.0, PS[:, b, 0:INTER], ALU.add, ALU.mult).then_inc(T["half"], 1)
                    seen(dve, T["half"], j, 1, 1, NT)
                    seen(dve, T["hT_psum"], j - 2, 1, 1, NT)
                    dve.tensor_tensor(eh[:, b, :], eact[:, b, :], PS[:, b, INTER:2 * INTER], ALU.mult).then_inc(T["h"], 1)

            def tile_result(j, b):
                if has(j, NT):
                    seen(dve, T["down_psum"], j, 1, 1, NT)
                    if has(j - 2, NT):
                        dve.wait_ge(tile_out[b], pair(j) * 16)
                    dve.tensor_copy(ey[:, b, :], PS[:, 4 + b, 0:D]).then_inc(T["y"], 1)

            def tile_step(j, b):
                tile_hidden(j + 2, b)
                tile_result(j, b)

            skewed(dve, tile_step, NT, 3, 2)
            for b in range(2):
                dve.wait_ge(tile_out[b], 16 * NT // 2)

            attention(1)

            def ffn_moments(s, b):
                if has(s):
                    dve.bn_stats(fstats[:], row(resid, s)).then_inc(F["stats"], 1)

            def ffn_moments_end(s, b):
                if has(s):
                    dve.bn_aggr(fmv[:, b, :], fstats[:]).then_inc(F["aggr"], 1)
                    seen(dve, F["aggr"], s)
                    dve.tensor_scalar(fvar[:, b:b + 1], fmv[:, b, 1:2], EPS, None, ALU.add).then_inc(F["var"], 1)

            def ffn_quant(s, b):
                if not has(s):
                    return
                n = [0]

                def then(ins):
                    n[0] += 1
                    ins.then_inc(F["chain"], 1)
                    seen(dve, F["chain"], s, n[0], CH)

                seen(dve, F["rstd"], s)
                then(dve.tensor_scalar(fxn[:], row(resid, s), fmv[:, b, 0:1], frstd[:, b:b + 1], ALU.subtract, ALU.mult))
                then(dve.tensor_reduce(fs[:, b, 0:1], fxn[:], AX.X, ALU.max, apply_absolute_value=True))
                then(dve.tensor_scalar(fs[:, b, 1:2], fs[:, b, 0:1], EPS, 1.0 / 127.0, ALU.max, ALU.mult))
                then(dve.reciprocal(fs[:, b, 2:3], fs[:, b, 1:2]))
                seen(dve, F["q_psum"], s - 2)
                dve.tensor_scalar(fq[:, b, :], fxn[:], fs[:, b, 2:3], ROUND, ALU.mult, ALU.add).then_inc(F["q"], 1)
                then(dve.tensor_scalar(fs[:, b, 3:4], fs[:, b, 1:2], winv[:, 1:2], 0.5, ALU.mult, ALU.mult))
                then(dve.tensor_scalar(fs[:, b, 4:5], fs[:, b, 1:2], winv[:, 0:1], 0.5, ALU.mult, ALU.mult))
                assert n[0] == CH
                dve.tensor_scalar(fs[:, b, 5:6], fs[:, b, 4:5], fs[:, b, 3:4], 2.0, ALU.mult, ALU.mult).then_inc(F["scales"], 1)

            def ffn_half(s, b):
                seen(dve, F["stats"], s + 3)
                if has(s):
                    seen(dve, F["tanh"], s)
                    seen(dve, F["prod"], s - 2)
                    dve.scalar_tensor_tensor(fh[:, b, :], ft[:], 1.0, PS[:, 0:2].rearrange("p a n -> p (a n)"),
                                             ALU.add, ALU.mult).then_inc(F["half"], 1)
                    dve.tensor_copy(fm[:, b, 0:1], fs[:, b, 5:6]).then_inc(F["kept"], 1)

            def ffn_quant_hidden(s, b):
                if not has(s):
                    return
                n = [0]

                def then(ins):
                    n[0] += 1
                    ins.then_inc(F["pchain"], 1)
                    seen(dve, F["pchain"], s, n[0], PR)

                seen(dve, F["resid"], s - 2)
                seen(dve, F["kept"], s)
                seen(dve, F["prod"], s)
                then(dve.tensor_reduce(fm[:, b, 1:2], fp[:, b, :], AX.X, ALU.max, apply_absolute_value=True))
                then(dve.tensor_scalar(fm[:, b, 1:2], fm[:, b, 1:2], fm[:, b, 0:1], EPS, ALU.mult, ALU.max))
                then(dve.tensor_scalar(fm[:, b, 1:2], fm[:, b, 1:2], 1.0 / 127.0, None, ALU.mult))
                then(dve.reciprocal(fm[:, b, 2:3], fm[:, b, 1:2]))
                then(dve.tensor_scalar(fm[:, b, 2:3], fm[:, b, 2:3], fm[:, b, 0:1], None, ALU.mult))
                seen(dve, F["pq_psum"], s - 2)
                assert n[0] == PR
                dve.tensor_scalar(fpq[:, b, :], fp[:, b, :], fm[:, b, 2:3], ROUND, ALU.mult, ALU.add).then_inc(F["pq"], 1)

            def ffn_add(s, b):
                if has(s):
                    seen(dve, F["down_psum"], s)
                    dve.tensor_scalar(fm[:, b, 1:2], fm[:, b, 1:2], winv[:, 2:3], None, ALU.mult).then_inc(F["fscale"], 1)
                    seen(dve, F["fscale"], s)
                    dve.scalar_tensor_tensor(row(resid, s), PS[:, 7, 0:D], fm[:, b, 1:2], row(resid, s), ALU.mult, ALU.add).then_inc(F["resid"], 1)

            def ffn_step(s, b):
                ffn_half(s, b)
                ffn_quant(s + 2, b)
                ffn_moments_end(s + 3, 1 - b)
                ffn_quant_hidden(s - 1, 1 - b)
                ffn_add(s - 2, b)
                ffn_moments(s + 4, b)

            skewed(dve, ffn_step, SEQ, 4, 2)


def _inputs(v):
    import numpy as np

    f = {k: np.asarray(a) for k, a in v.items()}
    def rows(a):
        return np.broadcast_to(np.asarray(a).reshape(1, -1), (P, np.asarray(a).size))

    def cols(a):
        return np.asarray(a).reshape(-1, P).T

    def experts(a, b):
        return np.concatenate([a.transpose(0, 2, 1), b.transpose(0, 2, 1)], axis=2)

    inter = f["L0_ffn_w1"].shape[1]
    sw1, sw3 = (f[n].reshape(-1, inter, D) for n in ("L0_ffn_sw1", "L0_ffn_sw3"))
    sw2 = f["L0_ffn_sw2"].reshape(D, -1, inter).transpose(1, 2, 0)
    n_exp = f["L0_ffn_gate_w"].shape[0]
    at = np.arange(P)
    return {
        "x_t": f["x"].T,
        "codebook_t": f["L0_tok_codebook"].T,
        "tok_w1": f["L0_tok_W1"],
        "tok_b1": cols(f["L0_tok_b1"]),
        "tok_w2": f["L0_tok_W2"],
        "tok_b2": rows(f["L0_tok_b2"]),
        "g_ln": cols(f["L0_attn_g_ln"]),
        "w_qkv0": np.concatenate([f["L0_attn_Wq"], f["L0_attn_Wkv"]], axis=1),
        "w_out0": f["L0_attn_Wo"],
        "gate_wt": f["L0_ffn_gate_w"].T,
        "gate_bias": rows(f["L0_ffn_gate_bias"]),
        "w13": np.concatenate([experts(f["L0_ffn_w1"], f["L0_ffn_w3"]), experts(sw1, sw3)]),
        "w2": np.concatenate([f["L0_ffn_w2"].transpose(0, 2, 1), sw2]),
        "w_qkv1": f["L1_attn_w_attn"],
        "b_qk": cols(f["L1_attn_b_attn"][:2 * D]),
        "b_v": rows(f["L1_attn_b_attn"][2 * D:]),
        "la_attn_t": f["L1_attn_la_attn"].T,
        "lb_attn": f["L1_attn_lb_attn"],
        "w_proj": f["L1_attn_w_proj"],
        "b_proj": rows(f["L1_attn_b_proj"]),
        "la_proj_t": f["L1_attn_la_proj"].T,
        "lb_proj": f["L1_attn_lb_proj"],
        "kv_scale": rows(f["L1_attn_kv_scale"]),
        "kv_zero": rows(f["L1_attn_kv_zero_point"]),
        "w_gu": np.concatenate([f["L1_ffn_w_gate"].T, f["L1_ffn_w_up"].T], axis=1),
        "w_down": f["L1_ffn_w_down"].T,
        "ident_in": np.eye(P, dtype=np.float32),
        "causal_in": np.where(at[None, :] > at[:, None], np.float32(MASKED), np.float32(0)),
        "own_in": (at[:, None] // DH == np.arange(HPB)).astype(np.float32),
        "rank_in": np.tile(np.arange(n_exp, 0, -1, dtype=np.float32), (P, 1)),
        "earlier_in": (at[:, None] < at[None, :]).astype(np.float32),
        "tile_no_in": np.tile(np.arange(2 * f["x"].shape[0] + n_exp, dtype=np.float32), (P, 1)),
    }


def kernel(**inputs):
    import numpy as np
    from concourse import bacc
    from concourse.bass_utils import run_bass_kernel_spmd

    nc = bacc.Bacc("TRN2", target_bir_lowering=False, num_devices=1)
    arrays = {f"in_{n}": np.ascontiguousarray(a) for n, a in _inputs(inputs).items()}
    args = [nc.dram_tensor(n, a.shape, mybir.dt.from_np(a.dtype), kind="ExternalInput").ap() for n, a in arrays.items()]
    n_seq, length = inputs["x"].shape
    out = nc.dram_tensor("out_0", (n_seq, length, D), F32, kind="ExternalOutput").ap()
    build(nc, *args, out)
    r = run_bass_kernel_spmd(nc, [arrays], core_ids=[0])
    return r.results[0]["out_0"]
```

```python
from contextlib import ExitStack

import concourse.bass as bass
from concourse import mybir

F32 = mybir.dt.float32
F32R = mybir.dt.float32r
BF16 = mybir.dt.bfloat16
U32 = mybir.dt.uint32
I32 = mybir.dt.int32
ALU = mybir.AluOpType
ACT = mybir.ActivationFunctionType
AX = mybir.AxisListType

P = 128
D = 256
KD = D // P
H = 16
DH = D // H
HPB = P // DH
SLOT = 32
EPS = 1e-5
ROUND = 1.5 * 2.0 ** 23
MASKED = -1e30
BIG = 1e30


def build(nc, x_t, codebook_t, tok_w1, tok_b1, tok_w2, tok_b2,
          g_ln, w_qkv0, w_out0, gate_wt, gate_bias, w13, w2,
          w_qkv1, b_qk, b_v, la_attn_t, lb_attn, w_proj, b_proj, la_proj_t, lb_proj, kv_scale, kv_zero,
          w_gu, w_down, ident_in, causal_in, rank_in, earlier_in, tile_no_in, out):
    SEQ = x_t.shape[1]
    ROWS = codebook_t.shape[1]
    HID = tok_w1.shape[1]
    E = gate_wt.shape[1]
    EA = w13.shape[0]
    INTER = w2.shape[1]
    INNER = w_down.shape[0]
    RANK = la_attn_t.shape[0]
    KH, KI, KN = HID // P, INTER // P, INNER // P
    GS = 4
    GT = GS * P
    G = SEQ // GS
    TG = ROWS // 512
    NS = EA - E
    TOP = 2
    NT = TOP * SEQ + E
    FILLS = 8

    table = nc.dram_tensor("token_table", (ROWS, D), F32).ap()
    placed_x = nc.dram_tensor("placed_x", (NT * P, D), F32).ap()
    placed_y = nc.dram_tensor("placed_y", (NT * P, D), F32).ap()

    with ExitStack() as ctx:
        def sb(name, shape, dt=F32, at=None):
            return (at or ctx).enter_context(nc.sbuf_tensor(name, shape, dt))

        def sem(name):
            return ctx.enter_context(nc.semaphore(name))

        PS = ctx.enter_context(nc.psum_tensor("banks", [P, 8, 512], F32))

        resid = sb("resid", [P, SEQ, D])
        ident = sb("ident", [P, P])
        ident_b = sb("ident_b", [P, P], BF16)
        causal = sb("causal", [P, P])
        causal_b = sb("causal_b", [P, 4, P], BF16)
        ones = sb("ones", [P, P])
        minus_round = sb("minus_round", [P, 1])
        minus_half = sb("minus_half", [P, GS])
        idx = sb("idx", [P, SEQ], I32)
        wqkv = [sb(f"wqkv{i}", [P, KD, 3 * D]) for i in range(2)]
        wout = [sb(f"wout{i}", [P, KD, D]) for i in range(2)]
        gln = sb("gln", [P, KD])
        bqk = sb("bqk", [P, 4])
        bq_scaled = sb("bq_scaled", [P, KD])
        bv = sb("bv", [P, D])
        bproj = sb("bproj", [P, D])
        kvs = sb("kvs", [P, 1])
        kvz = sb("kvz", [P, 1])
        kvinv = sb("kvinv", [P, 1])
        gw = sb("gw", [P, KD, E])
        gbias = sb("gbias", [P, E])
        rank = sb("rank", [P, E])
        earlier = sb("earlier", [P, P])
        zeros = sb("zeros", [P, D])
        place = sb("place", [P, SEQ, TOP], I32)
        place_now = sb("place_now", [P, 2, TOP], I32)
        tile_expert = sb("tile_expert", [1, NT], I32)
        gate = sb("gate", [P, TOP, SEQ])
        yrow = sb("yrow", [P, 2, TOP, D])
        w13_sb = sb("w13_sb", [P, EA, KD, 2 * INTER])
        w2_sb = sb("w2_sb", [P, EA, KI, D])
        wgu_q = sb("wgu_q", [P, KD, 2 * INNER], BF16)
        wdn_q = sb("wdn_q", [P, KN, D], BF16)
        wabs = sb("wabs", [P, 4])
        wmean = sb("wmean", [P, 4])
        wscale = sb("wscale", [P, 4])
        winv = sb("winv", [P, 4])

        with ExitStack() as t_:
            cb = sb("cb", [P, KD, ROWS], at=t_)
            tw1 = sb("tw1", [P, KD, HID], at=t_)
            tw2 = sb("tw2", [P, KH, D], at=t_)
            tb1 = sb("tb1", [P, KH], at=t_)
            tb2 = sb("tb2", [P, D], at=t_)
            thid = sb("thid", [P, KH, 512], at=t_)
            trow = sb("trow", [P, 4, D], at=t_)
            la1 = sb("la1", [RANK, D], at=t_)
            lb1 = sb("lb1", [RANK, 3 * D], at=t_)
            la2 = sb("la2", [RANK, D], at=t_)
            lb2 = sb("lb2", [RANK, D], at=t_)
            wst = sb("wst", [P, 2 * INNER], at=t_)
        with ExitStack() as a_:
            stats = sb("stats", [P, 6], at=a_)
            mv = sb("mv", [P, 4, 2], at=a_)
            varp = sb("varp", [P, 2], at=a_)
            rstd = sb("rstd", [P, 2], at=a_)
            xn = sb("xn", [P, D], at=a_)
            xT = sb("xT", [P, KD, P], at=a_)
            qT = sb("qT", [P, 2, KD, P], at=a_)
            q_parts = sb("q_parts", [P, 2, 2, KD, P], F32R, at=a_)
            k_parts = sb("k_parts", [P, 2, KD, 2, P], F32R, at=a_)
            kv = sb("kv", [P, 2, 2 * D], at=a_)
            kT = sb("kT", [P, 2, KD, 2, HPB, P], F32R, at=a_)
            V = sb("V", [P, 2, H, SLOT], at=a_)
            prob = sb("prob", [P, 2, H, P], at=a_)
            rmax = sb("rmax", [P, H], at=a_)
            rden = sb("rden", [P, H], at=a_)
            oraw = sb("oraw", [P, 4, P], at=a_)
            onrm = sb("onrm", [P, D], at=a_)
            oT = sb("oT", [P, KD, P], at=a_)
        with ExitStack() as m_:
            mstats = sb("mstats", [P, GS, 6], at=m_)
            mmv = sb("mmv", [P, 2, GS, 2], at=m_)
            mvar = sb("mvar", [P, GS], at=m_)
            mrstd = sb("mrstd", [P, GS], at=m_)
            mxn = sb("mxn", [P, SEQ, D], at=m_)
            staged = sb("staged", [P, 2, GS, D], at=m_)
            mxT = sb("mxT", [P, 2, KD, GT], at=m_)
            with ExitStack() as s_:
                hT = sb("hT", [P, 2, KI, GT], at=s_)
                tnh = sb("tnh", [P, 2, GT], at=s_)
                act_ = sb("act_", [P, 2, GT], at=s_)
                PAD = SEQ // 2
                score = sb("score", [P, SEQ, E], at=s_)
                scratch = sb("scratch", [P, 2, SEQ, E], at=s_)
                biased, tie = scratch[:, 0], scratch[:, 1]
                chosen = [sb(f"chosen{i}", [P, SEQ, E], at=s_) for i in range(TOP)]
                selected = sb("selected", [P, SEQ, E], at=s_)
                per_token = sb("per_token", [P, SEQ], at=s_)
                counts = [sb(f"counts{i}", [P, PAD + SEQ, E], at=s_) for i in range(3)]
                tiles = [sb(f"tiles{i}", [P, E + E], at=s_) for i in range(3)]
                start = sb("start", [P, E], at=s_)
                place_f = sb("place_f", [P, SEQ, TOP], at=s_)
                tile_no = sb("tile_no", [P, NT], at=s_)
                beyond = scratch[:].rearrange("p a s e -> p (a s e)")[:, 0:NT * (E - 1)].rearrange("p (n e) -> p n e", e=E - 1)
                tile_expert_f = sb("tile_expert_f", [P, NT], at=s_)
            with ExitStack() as e_:
                ex = sb("ex", [P, 2, D], at=e_)
                exT = sb("exT", [P, 2, KD, P], at=e_)
                etanh = sb("etanh", [P, 2, INTER], at=e_)
                eact = sb("eact", [P, 2, INTER], at=e_)
                eh = sb("eh", [P, 2, INTER], at=e_)
                ehT = sb("ehT", [P, KI, P], at=e_)
                ey = sb("ey", [P, 2, D], at=e_)
        with ExitStack() as f_:
            fstats = sb("fstats", [P, 6], at=f_)
            fmv = sb("fmv", [P, 2, 2], at=f_)
            fvar = sb("fvar", [P, 2], at=f_)
            frstd = sb("frstd", [P, 2], at=f_)
            fxn = sb("fxn", [P, D], at=f_)
            fq = sb("fq", [P, 2, D], at=f_)
            fxT = sb("fxT", [P, KD, P], BF16, at=f_)
            fs = sb("fs", [P, 2, 5], at=f_)
            fm = sb("fm", [P, 2, 3], at=f_)
            ft = sb("ft", [P, INNER], at=f_)
            fh = sb("fh", [P, 2, INNER], at=f_)
            fu = sb("fu", [P, 2, INNER], at=f_)
            fp = sb("fp", [P, 2, INNER], at=f_)
            fpq = sb("fpq", [P, 2, INNER], at=f_)
            fpT = sb("fpT", [P, KN, P], BF16, at=f_)

        tok_first = sem("tok_first_loaded")
        tok_in, attn_in, exp_in, ffn_in = (sem(f"{n}_loaded") for n in ("tok", "attn", "experts", "ffn"))
        consts = sem("consts_ready")
        prep = sem("prep_step")
        prep_psum = sem("prep_psum")
        lora_added = sem("lora_added")
        weights_ready = sem("weights_ready")
        wst_summed = sem("wst_summed")
        wst_quantized = sem("wst_quantized")
        t_hid_psum, t_hid, t_row_psum, t_row = (sem(n) for n in ("t_hid_psum", "t_hid", "t_row_psum", "t_row"))
        t_store = [sem(f"table_stored{b}") for b in range(4)]
        gathered = [sem(f"gathered{b}") for b in range(2)]
        names = ("stats aggr var rstd xn xT_psum xT qk_psum q k_read k rounded split v_psum v_read v chain s_psum rmax shifted prob pT_psum pT"
                 " o_psum oraw o2_psum rden onrm oT_psum oT y_psum resid biased").split()
        A = [{n: sem(f"a{i}_{n}") for n in names if i or n not in ("k_read", "chain", "biased")} for i in range(2)]
        space_set = sem("space_set")
        keys_placed = [sem(f"keys_placed{b}") for b in range(2)]
        M = {n: sem(f"m_{n}") for n in ("stats aggr var rstd xn xT_psum xT route_psum route_exp route_max kept chain selected"
                                        " prefix_psum routed").split()}
        S = {n: sem(f"s_{n}") for n in "staged xT_psum xT up_psum tanh half hT down_psum resid".split()}
        T = {n: sem(f"t_{n}") for n in "xT_psum xT up_psum tanh half h hT_psum hT down_psum y".split()}
        prefix_read = sem("prefix_read")
        places_filled, scattered = sem("places_filled"), sem("scattered")
        tile_in = [sem(f"tile_loaded{b}") for b in range(2)]
        tile_out = [sem(f"tile_stored{b}") for b in range(2)]
        y_gathered = [sem(f"y_gathered{b}") for b in range(2)]
        place_set, y_added, y_added_all = sem("place_set"), sem("y_added_first"), sem("y_added_both")
        F = {n: sem(f"f_{n}") for n in ("stats aggr var rstd chain pchain fscale q q_psum xT up_psum tanh u half kept prod scales pq pq_psum pT"
                                        " down_psum resid").split()}
        stored = sem("out_stored")

        def seen(eng, s, i, k=1, per=1, n=SEQ):
            if isinstance(i, int) and not 0 <= i < n:
                return
            eng.wait_ge(s, i * per + k)

        def has(i, n=SEQ):
            return not isinstance(i, int) or 0 <= i < n

        def row(t, i):
            return t[:, i] if isinstance(i, int) else t[:, bass.ds(i, 1)].rearrange("p a d -> p (a d)")

        def pair(i):
            return i // 2

        def spread(v, n):
            return v.unsqueeze(2).broadcast_to([P, v.shape[1], n])

        def skewed(eng, step, n, before, behind):
            first = behind
            last = (n - before - first) // 2 * 2 + first
            for s in range(-before, first):
                step(s, s % 2)
            with eng.Fori(0, (last - first) // 2, 1) as j:
                for b in range(2):
                    step(j * 2 + (first + b), (first + b) % 2)
            for s in range(last, n + behind):
                step(s, s % 2)

        block = ctx.enter_context(nc.Block())

        def kt(a):
            return a.rearrange("(k p) n -> p k n", p=P)

        @block.sync
        def _(sp):
            cb_in = kt(codebook_t)
            sp.dma_start(tw1[:], kt(tok_w1)).then_inc(tok_first, 16)
            sp.dma_start(cb[:, :, 0:512], cb_in[:, :, 0:512]).then_inc(tok_first, 16)
            sp.dma_start(tb1[:], tok_b1).then_inc(tok_first, 16)
            sp.dma_start(tw2[:], kt(tok_w2)).then_inc(tok_in, 16)
            sp.dma_start(tb2[:], tok_b2).then_inc(tok_in, 16)
            sp.dma_start(cb[:, :, 512:], cb_in[:, :, 512:]).then_inc(tok_in, 16)
            sp.dma_start(idx[:], x_t).then_inc(attn_in, 16)
            for dst, src in ((ident, ident_in), (causal, causal_in), (gln, g_ln), (bqk, b_qk), (bv, b_v),
                             (bproj, b_proj), (kvs, kv_scale), (kvz, kv_zero), (gbias, gate_bias), (rank, rank_in),
                             (earlier, earlier_in),
                             (la1, la_attn_t), (lb1, lb_attn), (la2, la_proj_t), (lb2, lb_proj)):
                sp.dma_start(dst[:], src).then_inc(attn_in, 16)
            for dst, src in ((wqkv[0], w_qkv0), (wout[0], w_out0), (wqkv[1], w_qkv1), (wout[1], w_proj), (gw, gate_wt)):
                sp.dma_start(dst[:], kt(src)).then_inc(attn_in, 16)
            for n in range(4 * TG):
                sp.wait_ge(t_row, n + 1)
                sp.dma_start(table[n * P:(n + 1) * P, :], trow[:, n % 4, :]).then_inc(t_store[n % 4], 16)

            def place_keys(layer):
                def step(s, b):
                    seen(sp, A[layer]["split"], s)
                    for h in range(HPB if has(s) else 0):
                        own = slice(h * DH, (h + 1) * DH)
                        sp.dma_start(kT[own, b, :, :, h, :].bitcast(F32), k_parts[own, b].bitcast(F32)).then_inc(keys_placed[b], 16)

                skewed(sp, step, SEQ, 0, 2)

            place_keys(0)
            sp.wait_ge(A[0]["resid"], SEQ)
            sp.dma_start(tile_no[:], tile_no_in).then_inc(tile_in[0], 16)
            sp.wait_ge(scattered, 16 * TOP * SEQ)
            sp.wait_ge(S["resid"], G * NS * GS)

            def tile_rows(dram, j):
                if isinstance(j, int):
                    return dram[j * P:(j + 1) * P, :]
                return dram[bass.ds(j * P, P), :]

            def tile_step(j, b):
                if has(j + 5, NT):
                    seen(sp, T["xT_psum"], j + 3, 1, 1, NT)
                    sp.dma_start(ex[:, 1 - b, :], tile_rows(placed_x, j + 5)).then_inc(tile_in[1 - b], 16)
                if has(j, NT):
                    seen(sp, T["y"], j, 1, 1, NT)
                    sp.dma_start(tile_rows(placed_y, j), ey[:, b, :]).then_inc(tile_out[b], 16)

            skewed(sp, tile_step, NT, 5, 2)
            place_keys(1)
            with sp.Fori(0, SEQ, 1) as i:
                sp.wait_ge(F["resid"], i + 1)
                sp.dma_start(out[bass.ds(i, 1)].rearrange("a p d -> p (a d)"), row(resid, i)).then_inc(stored, 16)
            sp.wait_ge(stored, 16 * SEQ)

        ATTN_LOADS = 21 * 16
        CH, PR = 5, 4

        @block.gpsimd
        def _(pool):
            pool.memset(minus_half[:], -0.5).then_inc(consts, 1)
            pool.memset(ones[:], 1.0).then_inc(consts, 1)
            pool.memset(minus_round[:], -ROUND).then_inc(consts, 1)
            pool.memset(zeros[:], 0.0).then_inc(consts, 1)
            for n in range(2 * (KD + 1)):
                if 0 < n <= KD + 1:
                    pool.wait_ge(wst_summed, n)
                if n > KD + 1:
                    pool.wait_ge(wst_quantized, n - KD - 1)
                k = n % (KD + 1)
                if k < KD:
                    pool.dma_start(wst[:], w_gu[k * P:(k + 1) * P, :]).then_inc(ffn_in, 16)
                else:
                    pool.dma_start(wst[:].rearrange("p (k n) -> p k n", k=KN), kt(w_down)).then_inc(ffn_in, 16)
            pool.wait_ge(attn_in, ATTN_LOADS)
            pool.wait_ge(consts, 1)
            for t in range(4):
                pool.wait_ge(t_store[t], 16 * TG)

            def gather(i):
                pool.indirect_dma_start(resid[:, i, :], None, table,
                                        bass.IndirectOffsetOnAxis(ap=idx[:, i:i + 1].bitcast(U32), axis=0)).then_inc(gathered[i % 2], 16)

            def attention(layer):
                a = A[layer]

                def step(s, b):
                    if layer == 0 and has(s + 5):
                        if has(s + 3):
                            pool.wait_ge(gathered[1 - b], pair(s + 3) * 16 + 16)
                        gather(s + 5)
                    if has(s + 3):
                        seen(pool, a["var"], s + 3)
                        seen(pool, a["xn"], s + 1)
                        pool.tensor_tensor(rstd[:, 1 - b:2 - b], varp[:, 1 - b:2 - b], minus_half[:, 0:1], ALU.pow).then_inc(a["rstd"], 1)
                    if layer == 1 and has(s + 5):
                        seen(pool, y_added_all, s + 3)
                        i = place[:, s + 5] if isinstance(s, int) else place[:, bass.ds(s + 5, 1)].rearrange("p a c -> p (a c)")
                        pool.tensor_copy(place_now[:, 1 - b, :], i).then_inc(place_set, 1)
                        seen(pool, place_set, s + 5)
                    if has(s + 2):
                        if isinstance(s, int) and s == -2:
                            pool.wait_ge(space_set, layer + 1)
                        seen(pool, a["s_psum"], s)
                        seen(pool, a["rounded"], s + 2)
                        pool.tensor_tensor(q_parts[:, b, 1], qT[:, b], q_parts[:, b, 0].bitcast(F32), ALU.subtract)
                        k = kv[:, b, 0:D].rearrange("p (k n) -> p k n", k=KD)
                        pool.tensor_tensor(k_parts[:, b, :, 1, :], k, k_parts[:, b, :, 0, :].bitcast(F32), ALU.subtract).then_inc(a["split"], 1)
                    if layer == 1 and has(s + 1):
                        seen(pool, a["xn"], s + 1)
                        pool.tensor_tensor(row(resid, s + 1), row(resid, s + 1), bproj[:], ALU.add).then_inc(a["biased"], 1)

                    if layer == 1 and has(s + 5):
                        for c in range(TOP):
                            pool.indirect_dma_start(yrow[:, 1 - b, c, :], None, placed_y,
                                                    bass.IndirectOffsetOnAxis(ap=place_now[:, 1 - b, c:c + 1].bitcast(U32), axis=0))\
                                .then_inc(y_gathered[1 - b], 16)

                if layer == 0:
                    for s in range(-5, SEQ):
                        step(s, s % 2)
                else:
                    skewed(pool, step, SEQ, 5, 0)

            attention(0)
            for g in range(G):
                pool.wait_ge(M["var"], g + 1)
                if g:
                    pool.wait_ge(M["xn"], GS * g)
                pool.tensor_tensor(mrstd[:], mvar[:], minus_half[:], ALU.pow).then_inc(M["rstd"], 1)
            pool.wait_ge(M["routed"], 1)
            pool.wait_ge(M["kept"], G)
            pool.wait_ge(places_filled, 16 * FILLS)
            for s in range(SEQ):
                for c in range(TOP):
                    pool.indirect_dma_start(placed_x, bass.IndirectOffsetOnAxis(ap=place[:, s, c:c + 1].bitcast(U32), axis=0),
                                            mxn[:, s, :], None).then_inc(scattered, 16)
            for b in range(2):
                pool.wait_ge(tile_out[b], 16 * NT // 2)
            attention(1)

            def ffn_step(s, b):
                if has(s):
                    seen(pool, F["half"], s)
                    seen(pool, F["u"], s)
                    seen(pool, F["pq"], s - 2)
                    pool.tensor_tensor(fp[:, b, :], fh[:, b, :], fu[:, b, :], ALU.mult).then_inc(F["prod"], 1)
                if has(s - 1):
                    seen(pool, F["pchain"], s - 1, PR, PR)
                    seen(pool, F["pq_psum"], s - 3)
                if has(s + 3):
                    seen(pool, F["var"], s + 3)
                    seen(pool, F["chain"], s + 1, 1, CH)
                    pool.tensor_tensor(frstd[:, 1 - b:2 - b], fvar[:, 1 - b:2 - b], minus_half[:, 0:1], ALU.pow).then_inc(F["rstd"], 1)
                if has(s - 1):
                    pool.tensor_scalar(fpq[:, 1 - b, :], fp[:, 1 - b, :], fm[:, 1 - b, 2:3], ROUND, ALU.mult, ALU.add).then_inc(F["pq"], 1)

            skewed(pool, ffn_step, SEQ, 3, 3)

        @block.tensor
        def _(pe):
            def prepare():
                pe.wait_ge(attn_in, ATTN_LOADS)
                for n, (la, lb, k, lo, hi) in enumerate(((la1, lb1, 0, 0, 512), (la1, lb1, 0, 512, 768),
                                                         (la1, lb1, 1, 0, 512), (la1, lb1, 1, 512, 768),
                                                         (la2, lb2, 0, 0, 256), (la2, lb2, 1, 0, 256))):
                    if n >= 3:
                        pe.wait_ge(lora_added, n - 2)
                    pe.matmul(PS[:, 4 + n % 3, 0:hi - lo], la[:, k * P:(k + 1) * P], lb[:, lo:hi], start=True, stop=True).then_inc(prep_psum, 1)
            def weight_sums():
                pe.wait_ge(consts, 3)
                pe.wait_ge(wst_summed, 3)
                pe.matmul(PS[:, 7, 0:4], ones[:], wabs[:], start=True, stop=True).then_inc(prep_psum, 1)

            pe.wait_ge(tok_first, 48)
            for t in range(TG):
                if t == 1:
                    prepare()
                for m in range(KH):
                    n = t * KH + m
                    if n >= 2:
                        pe.wait_ge(t_hid, n - 1)
                    if t == 1 and m == 6:
                        weight_sums()
                    for k in range(KD):
                        mm = pe.matmul(PS[:, n % 2], tw1[:, k, m * P:(m + 1) * P], cb[:, k, t * 512:(t + 1) * 512],
                                       start=(k == 0), stop=(k == KD - 1))
                    mm.then_inc(t_hid_psum, 1)
                pe.wait_ge(t_hid, (t + 1) * KH)
                if t == 0:
                    pe.wait_ge(tok_in, 48)
                for r in range(4):
                    n = t * 4 + r
                    if n >= 2:
                        pe.wait_ge(t_row, n - 1)
                    for k in range(KH):
                        mm = pe.matmul(PS[:, 2 + n % 2, 0:D], thid[:, k, r * P:(r + 1) * P], tw2[:, k, :],
                                       start=(k == 0), stop=(k == KH - 1))
                    mm.then_inc(t_row_psum, 1)

            def attention(layer):
                a = A[layer]
                pe.wait_ge(weights_ready, 1)
                if layer == 0:
                    pe.wait_ge(t_row, 4 * TG)
                else:
                    pe.wait_ge(T["y"], NT)

                k_read, v_read = (a["k"], a["v_read"]) if layer == 0 else (a["k_read"], a["v_read"])

                def o_turn(s):
                    if has(s):
                        seen(pe, a["oraw"], s)
                        seen(pe, a["resid"], s - 1)
                        seen(pe, v_read, s + 3)
                        for t in range(4):
                            mm = pe.transpose(PS[:, 7, t * P:(t + 1) * P], oraw[:, t, :], ident[:])
                        mm.then_inc(a["o2_psum"], 1)

                def scores(s, b, banks):
                    if has(s):
                        if banks[0] == 0:
                            pe.wait_ge(keys_placed[b], pair(s) * 16 * HPB + (layer * SEQ // 2 + 1) * 16 * HPB)
                            seen(pe, a["shifted"], s - 1)
                        for n in banks:
                            pe.matmul(PS[:, n, :], ident_b[:], causal_b[:].rearrange("p a k -> p (a k)"), start=True, stop=False)
                            kb, h = n // 2, n % 2 * 4
                            for i, (q, k) in enumerate(((0, 0), (0, 1), (1, 0))):
                                mm = pe.matmul(PS[:, n, :], q_parts[:, b, q, kb, :], kT[:, b, kb, k, h:h + 4, :].rearrange("p h k -> p (h k)"),
                                               start=False, stop=(i == 2))
                        if banks[-1] == 3:
                            mm.then_inc(a["s_psum"], 1)

                def x_turn(s):
                    if has(s):
                        seen(pe, a["xn"], s)
                        seen(pe, a["q"], s - 1)
                        seen(pe, k_read, s - 1)
                        for k in range(KD):
                            mm = pe.transpose(PS[:, 6, k * P:(k + 1) * P], xn[:, k * P:(k + 1) * P], ident[:])
                        mm.then_inc(a["xT_psum"], 1)

                def on_turn(s):
                    if has(s):
                        seen(pe, a["onrm"], s)
                        for k in range(KD):
                            mm = pe.transpose(PS[:, 7, k * P:(k + 1) * P], onrm[:, k * P:(k + 1) * P], ident[:])
                        mm.then_inc(a["oT_psum"], 1)

                def p_turn(s, b, half):
                    if has(s):
                        if half == 0:
                            seen(pe, a["prob"], s)
                        for r in (2 * half, 2 * half + 1):
                            if r < 2:
                                seen(pe, a["oraw"], s - 1)
                                seen(pe, a["pT"], s - 1, 4, 4)
                            else:
                                seen(pe, a["pT"], s, r - 1, 4)
                            for c in range(4):
                                mm = pe.transpose(PS[:, 4 + r % 2, c * P:(c + 1) * P], prob[:, b, 4 * r + c, :], ident[:])
                            mm.then_inc(a["pT_psum"], 1)

                def project(s):
                    if has(s):
                        seen(pe, a["xT"], s)
                        for n in range(4):
                            for k in range(KD):
                                mm = pe.matmul(PS[:, 6, n * P:(n + 1) * P], wqkv[layer][:, k, n * P:(n + 1) * P], xT[:, k, :],
                                               start=(k == 0), stop=(k == KD - 1))
                        mm.then_inc(a["qk_psum"], 1)

                def project_values(s):
                    if has(s):
                        seen(pe, a["oT"], s - 4)
                        seen(pe, v_read, s - 1)
                        for k in range(KD):
                            mm = pe.matmul(PS[:, 7, 0:D], xT[:, k, :], wqkv[layer][:, k, 2 * D:3 * D],
                                           start=(k == 0), stop=(k == KD - 1))
                        mm.then_inc(a["v_psum"], 1)

                def pv(s, b):
                    if has(s):
                        seen(pe, a["v"], s)
                        seen(pe, a["pT"], s, 4, 4)
                        for t in range(4):
                            for c in range(4):
                                mm = pe.matmul(PS[SLOT * c:SLOT * (c + 1), 4, t * P:(t + 1) * P], V[:, b, 4 * t + c, :],
                                               prob[:, b, 4 * t + c, :], start=True, stop=True, tile_position=(0, SLOT * c))
                        mm.then_inc(a["o_psum"], 1)

                def out_proj(s):
                    if has(s):
                        seen(pe, a["oT"], s)
                        seen(pe, v_read, s + 4)
                        for k in range(KD):
                            mm = pe.matmul(PS[:, 7, 0:D], oT[:, k, :], wout[layer][:, k, :], start=(k == 0), stop=(k == KD - 1))
                        mm.then_inc(a["y_psum"], 1)

                def step(s, b):
                    scores(s, b, (0, 1, 2))
                    o_turn(s - 2)
                    x_turn(s + 2)
                    scores(s, b, (3,))
                    on_turn(s - 2)
                    project(s + 2)
                    project_values(s + 2)
                    p_turn(s - 1, 1 - b, 0)
                    p_turn(s - 1, 1 - b, 1)
                    out_proj(s - 2)
                    pv(s - 1, 1 - b)

                skewed(pe, step, SEQ, 2, 2)

            attention(0)

            pe.wait_ge(A[0]["resid"], SEQ)
            pe.wait_ge(exp_in, 2 * EA * 16)

            def xn_turn(g, b, sems):
                if has(g, G):
                    if sems is M:
                        seen(pe, M["xn"], g, GS, GS, G)
                    else:
                        seen(pe, S["staged"], g, 1, 1, G)
                    seen(pe, sems["xT"], g - 1, KD, KD, G)
                    for k in range(KD):
                        for t in range(GS):
                            mm = pe.transpose(PS[:, 6 + k, t * P:(t + 1) * P], staged[:, b, t, k * P:(k + 1) * P], ident[:])
                        mm.then_inc(sems["xT_psum"], 1)

            def route(g, b):
                if has(g, G):
                    seen(pe, M["xT"], g, KD, KD, G)
                    for t in range(GS):
                        at = (g * GS + t) * E
                        dst = PS[:, 5, at:at + E] if isinstance(g, int) else PS[:, 5, bass.ds(at, E)]
                        for k in range(KD):
                            mm = pe.matmul(dst, mxT[:, b, k, t * P:(t + 1) * P], gw[:, k, :],
                                           start=(k == 0), stop=(k == KD - 1))
                    mm.then_inc(M["route_psum"], 1)

            def route_step(g, b):
                xn_turn(g + 1, 1 - b, M)
                route(g, b)

            skewed(pe, route_step, G, 1, 0)

            def prefixes():
                pe.wait_ge(M["selected"], 1)
                sel = selected[:].rearrange("p s e -> p (s e)")
                pe.matmul(PS[:, 4, 0:SEQ * E], earlier[:], sel, start=True, stop=True)
                pe.matmul(PS[:, 4, SEQ * E:2 * SEQ * E], ones[:], sel, start=True, stop=True).then_inc(M["prefix_psum"], 1)

            def up(g, b, e):
                for h in range(KI):
                    if e:
                        seen(pe, S["hT"], g, (e - 1) * KI + h + 1, NS * KI, G)
                    else:
                        seen(pe, S["hT"], g - 1, (NS - 1) * KI + h + 1, NS * KI, G)
                    for u in range(2):
                        for k in range(KD):
                            mm = pe.matmul(PS[:, 2 * h + u], w13_sb[:, E + e, k, u * INTER + h * P:u * INTER + (h + 1) * P],
                                           mxT[:, b, k, :], start=(k == 0), stop=(k == KD - 1))
                    mm.then_inc(S["up_psum"], 1)

            def down(g, e):
                if not has(g, G):
                    return
                seen(pe, S["hT"], g, (e + 1) * KI, NS * KI, G)
                for t in range(GS):
                    if t % 2 == 0:
                        if e:
                            seen(pe, S["resid"], g, (e - 1) * GS + t + 2, NS * GS, G)
                        else:
                            seen(pe, S["resid"], g - 1, (NS - 1) * GS + t + 2, NS * GS, G)
                    for k in range(KI):
                        mm = pe.matmul(PS[:, 4 + t // 2, t % 2 * D:(t % 2 + 1) * D], hT[:, e % 2, k, t * P:(t + 1) * P],
                                       w2_sb[:, E + e, k, :], start=(k == 0), stop=(k == KI - 1), skip_group_check=True)
                    if t % 2:
                        mm.then_inc(S["down_psum"], 1)

            def shared_step(g, b):
                if has(g, G):
                    seen(pe, S["xT"], g, KD, KD, G)
                    up(g, b, 0)
                    if isinstance(g, int) and g == 0:
                        prefixes()
                down(g - 1, NS - 1)
                xn_turn(g + 1, 1 - b, S)
                if has(g, G):
                    for e in range(1, NS):
                        up(g, b, e)
                        if isinstance(g, int) and g == 0:
                            pe.wait_ge(prefix_read, 1)
                        down(g, e - 1)

            skewed(pe, shared_step, G, 1, 1)

            pe.wait_ge(S["resid"], G * NS * GS)

            def tile_turn(j, b):
                if has(j, NT):
                    pe.wait_ge(tile_in[b], pair(j) * 16 + (32 if b == 0 else 16))
                    seen(pe, T["xT"], j - 1, 1, 1, NT)
                    for k in range(KD):
                        mm = pe.transpose(PS[:, 2, k * P:(k + 1) * P], ex[:, b, k * P:(k + 1) * P], ident[:])
                    mm.then_inc(T["xT_psum"], 1)

            def hidden_turn(j, b):
                if has(j, NT):
                    seen(pe, T["h"], j, 1, 1, NT)
                    for k in range(KI):
                        mm = pe.transpose(PS[:, 3, k * P:(k + 1) * P], eh[:, b, k * P:(k + 1) * P], ident[:])
                    mm.then_inc(T["hT_psum"], 1)

            def tile_up(j, b):
                if has(j, NT):
                    at = tile_expert[0:1, j:j + 1] if isinstance(j, int) else tile_expert[0:1, bass.ds(j, 1)]
                    e = pe.value_load(at, min_val=0, max_val=E - 1)
                    seen(pe, T["xT"], j, 1, 1, NT)
                    for k in range(KD):
                        mm = pe.matmul(PS[:, b], exT[:, b, k, :], w13_sb[:, bass.ds(e, 1), k, :].rearrange("p a n -> p (a n)"),
                                       start=(k == 0), stop=(k == KD - 1))
                    mm.then_inc(T["up_psum"], 1)

            def tile_down(j, b):
                if has(j, NT):
                    at = tile_expert[0:1, j:j + 1] if isinstance(j, int) else tile_expert[0:1, bass.ds(j, 1)]
                    e = pe.value_load(at, min_val=0, max_val=E - 1)
                    seen(pe, T["hT"], j, 1, 1, NT)
                    seen(pe, T["y"], j - 2, 1, 1, NT)
                    for k in range(KI):
                        mm = pe.matmul(PS[:, 4 + b, 0:D], ehT[:, k, :], w2_sb[:, bass.ds(e, 1), k, :].rearrange("p a n -> p (a n)"),
                                       start=(k == 0), stop=(k == KI - 1))
                    mm.then_inc(T["down_psum"], 1)

            def tile_step(j, b):
                tile_turn(j + 3, 1 - b)
                hidden_turn(j, b)
                tile_up(j + 2, b)
                tile_down(j, b)

            pe.wait_ge(M["routed"], 1)
            skewed(pe, tile_step, NT, 3, 2)

            attention(1)

            pe.wait_ge(A[1]["resid"], SEQ)

            def q_turn(s, b):
                if has(s):
                    seen(pe, F["q"], s)
                    seen(pe, F["xT"], s - 1)
                    for k in range(KD):
                        mm = pe.transpose(PS[:, 4, k * P:(k + 1) * P], fq[:, b, k * P:(k + 1) * P], ident[:])
                    mm.then_inc(F["q_psum"], 1)

            def ffn_up(s):
                if has(s):
                    seen(pe, F["xT"], s)
                    seen(pe, F["half"], s - 1)
                    seen(pe, F["u"], s - 1)
                    for n in range(2 * INNER // 512):
                        for k in range(KD):
                            mm = pe.matmul(PS[:, n], fxT[:, k, :], wgu_q[:, k, n * 512:(n + 1) * 512],
                                           start=(k == 0), stop=(k == KD - 1))
                    mm.then_inc(F["up_psum"], 1)

            def p_turn(s, b):
                if has(s):
                    seen(pe, F["pq"], s)
                    seen(pe, F["pT"], s - 1)
                    for k in range(KN):
                        mm = pe.transpose(PS[:, 5 + k // 4, k % 4 * P:(k % 4 + 1) * P], fpq[:, b, k * P:(k + 1) * P], ident[:])
                    mm.then_inc(F["pq_psum"], 1)

            def ffn_down(s):
                if has(s):
                    seen(pe, F["pT"], s)
                    seen(pe, F["resid"], s - 1)
                    for k in range(KN):
                        mm = pe.matmul(PS[:, 7, 0:D], fpT[:, k, :], wdn_q[:, k, :], start=(k == 0), stop=(k == KN - 1))
                    mm.then_inc(F["down_psum"], 1)

            def ffn_step(s, b):
                ffn_up(s + 1)
                ffn_down(s - 2)
                q_turn(s + 2, b)
                p_turn(s - 1, 1 - b)

            skewed(pe, ffn_step, SEQ, 2, 2)

        @block.scalar
        def _(act):
            act.wait_ge(tok_first, 48)

            def expert_loads():
                for e in range(EA):
                    act.dma_start(w13_sb[:, e], kt(w13[e])).then_inc(exp_in, 16)
                    act.dma_start(w2_sb[:, e], kt(w2[e])).then_inc(exp_in, 16)

            def fill_places():
                n = NT // FILLS
                act.wait_ge(consts, 4)
                for c in range(FILLS):
                    act.dma_start(placed_x[c * n * P:(c + 1) * n * P, :].rearrange("(n p) d -> p n d", p=P),
                                  zeros[:].unsqueeze(1).broadcast_to([P, n, D])).then_inc(places_filled, 16)

            for t in range(TG):
                for m in range(KH):
                    n = t * KH + m
                    act.wait_ge(t_hid_psum, n + 1)
                    if t:
                        act.wait_ge(t_row_psum, 4 * t)
                    nc.scalar.activation(thid[:, m, :], PS[:, n % 2], ACT.Gelu_apprx_tanh, bias=tb1[:, m:m + 1]).then_inc(t_hid, 1)
                if t == 0:
                    expert_loads()
                if t == 1:
                    fill_places()

            def attention(layer):
                a = A[layer]

                def x_copy(s):
                    if has(s):
                        seen(act, a["xT_psum"], s)
                        nc.scalar.copy(xT[:].rearrange("p k n -> p (k n)"), PS[:, 6, 0:D]).then_inc(a["xT"], 1)

                def o_copy(s):
                    if has(s):
                        seen(act, a["oT_psum"], s)
                        seen(act, a["y_psum"], s - 1)
                        nc.scalar.copy(oT[:].rearrange("p k n -> p (k n)"), PS[:, 7, 0:D]).then_inc(a["oT"], 1)

                def p_copy(s, b):
                    if has(s):
                        for r in range(4):
                            seen(act, a["pT_psum"], s, r + 1, 4)
                            nc.scalar.copy(prob[:, b, 4 * r:4 * r + 4, :].rearrange("p a n -> p (a n)"), PS[:, 4 + r % 2, :]).then_inc(a["pT"], 1)

                def q_copy(s, b):
                    if has(s):
                        seen(act, a["qk_psum"], s)
                        if layer == 0:
                            nc.scalar.mul(qT[:, b].rearrange("p k n -> p (k n)"), PS[:, 6, 0:D], DH ** -0.5).then_inc(a["q"], 1)
                            seen(act, a["split"], s - 2)
                            nc.scalar.copy(kv[:, b, 0:D], PS[:, 6, D:2 * D]).then_inc(a["k"], 1)
                        else:
                            for k in range(KD):
                                ins = nc.scalar.activation(qT[:, b, k, :], PS[:, 6, k * P:(k + 1) * P], ACT.Identity,
                                                           bias=bq_scaled[:, k:k + 1], scale=DH ** -0.5)
                            ins.then_inc(a["q"], 1)

                def round_parts(s, b):
                    if has(s):
                        seen(act, a["q"], s)
                        seen(act, a["k"], s)
                        seen(act, a["s_psum"], s - 2)
                        nc.scalar.copy(q_parts[:, b, 0], qT[:, b])
                        nc.scalar.copy(k_parts[:, b, :, 0, :], kv[:, b, 0:D].rearrange("p (k n) -> p k n", k=KD)).then_inc(a["rounded"], 1)

                def exps(s, b):
                    if has(s):
                        seen(act, a["shifted"], s)
                        v = prob[:, b].rearrange("p a n -> p (a n)")
                        nc.scalar.activation(v, v, ACT.Exp).then_inc(a["prob"], 1)

                def raw_copy(s):
                    if has(s):
                        seen(act, a["o_psum"], s)
                        seen(act, a["o2_psum"], s - 1)
                        nc.scalar.copy(oraw[:].rearrange("p a n -> p (a n)"), PS[:, 4, :]).then_inc(a["oraw"], 1)

                def step(s, b):
                    x_copy(s + 2)
                    o_copy(s - 2)
                    q_copy(s + 2, b)
                    p_copy(s - 1, 1 - b)
                    raw_copy(s - 1)
                    exps(s, b)
                    round_parts(s + 2, b)

                skewed(act, step, SEQ, 2, 2)

            act.wait_ge(weights_ready, 1)
            act.wait_ge(consts, 3)
            attention(0)

            act.wait_ge(A[0]["resid"], SEQ)

            def xT_copy(g, b, sems):
                if has(g, G):
                    if sems is M:
                        seen(act, M["route_psum"], g - 2, 1, 1, G)
                    else:
                        seen(act, S["up_psum"], g - 2, NS * KI, NS * KI, G)
                    for k in range(KD):
                        seen(act, sems["xT_psum"], g, k + 1, KD, G)
                        nc.scalar.copy(mxT[:, b, k, :], PS[:, 6 + k, :]).then_inc(sems["xT"], 1)

            def route_step(g, b):
                xT_copy(g, b, M)
                if has(g, G):
                    seen(act, M["xn"], g, GS, GS, G)
                    dst = mxn[:, g * GS:(g + 1) * GS] if isinstance(g, int) else mxn[:, bass.ds(g * GS, GS)]
                    nc.scalar.copy(dst.rearrange("p t d -> p (t d)"), staged[:, b].rearrange("p t d -> p (t d)")).then_inc(M["kept"], 1)

            skewed(act, route_step, G, 0, 2)

            def shared_step(g, b):
                if has(g, G):
                    for e in range(NS):
                        for h in range(KI):
                            n = e * KI + h
                            seen(act, S["up_psum"], g, n + 1, NS * KI, G)
                            if n >= 2:
                                seen(act, S["half"], g, n - 1, NS * KI, G)
                            else:
                                seen(act, S["half"], g - 1, NS * KI - 1 + n, NS * KI, G)
                            nc.scalar.activation(tnh[:, h, :], PS[:, 2 * h], ACT.Tanh, scale=0.5).then_inc(S["tanh"], 1)
                        if e == 0:
                            xT_copy(g + 1, 1 - b, S)
                else:
                    xT_copy(g + 1, 1 - b, S)

            act.wait_ge(M["route_psum"], G)
            shared_step(-1, 1)
            act.wait_ge(M["route_max"], 1)
            v = score[:].rearrange("p a e -> p (a e)")
            nc.scalar.activation(v, v, ACT.Exp).then_inc(M["route_exp"], 1)
            skewed(act, shared_step, G, 0, 1)

            def tile_copy(j, b):
                if has(j, NT):
                    seen(act, T["xT_psum"], j, 1, 1, NT)
                    seen(act, T["up_psum"], j - 2, 1, 1, NT)
                    nc.scalar.copy(exT[:, b].rearrange("p k n -> p (k n)"), PS[:, 2, 0:D]).then_inc(T["xT"], 1)

            def hidden_copy(j):
                if has(j, NT):
                    seen(act, T["hT_psum"], j, 1, 1, NT)
                    seen(act, T["down_psum"], j - 1, 1, 1, NT)
                    nc.scalar.copy(ehT[:].rearrange("p k n -> p (k n)"), PS[:, 3, 0:INTER]).then_inc(T["hT"], 1)

            def tile_tanh(j, b):
                if has(j, NT):
                    seen(act, T["up_psum"], j, 1, 1, NT)
                    seen(act, T["half"], j - 2, 1, 1, NT)
                    nc.scalar.activation(etanh[:, b, :], PS[:, b, 0:INTER], ACT.Tanh, scale=0.5).then_inc(T["tanh"], 1)

            def tile_step(j, b):
                tile_copy(j + 3, 1 - b)
                hidden_copy(j)
                tile_tanh(j + 2, b)

            act.wait_ge(S["resid"], G * NS * GS)
            skewed(act, tile_step, NT, 3, 2)

            act.wait_ge(T["y"], NT)
            attention(1)
            act.wait_ge(A[1]["resid"], SEQ)

            def fx_copy(s):
                if has(s):
                    seen(act, F["q_psum"], s)
                    seen(act, F["up_psum"], s - 1)
                    nc.scalar.activation(fxT[:].rearrange("p k n -> p (k n)"), PS[:, 4, 0:D], ACT.Identity, bias=minus_round[:, 0:1])\
                      .then_inc(F["xT"], 1)

            def ftanh(s, b):
                if has(s):
                    seen(act, F["up_psum"], s)
                    seen(act, F["scales"], s)
                    seen(act, F["half"], s - 1)
                    nc.scalar.activation(ft[:], PS[:, 0:2].rearrange("p a n -> p (a n)"), ACT.Tanh, scale=fs[:, b, 3:4]).then_inc(F["tanh"], 1)

            def fu_copy(s, b):
                if has(s):
                    seen(act, F["prod"], s - 2)
                    nc.scalar.copy(fu[:, b, :], PS[:, 2:4].rearrange("p a n -> p (a n)")).then_inc(F["u"], 1)

            def fp_copy(s):
                if has(s):
                    seen(act, F["pq_psum"], s)
                    seen(act, F["down_psum"], s - 1)
                    nc.scalar.activation(fpT[:].rearrange("p k n -> p (k n)"), PS[:, 5:7].rearrange("p a n -> p (a n)"), ACT.Identity,
                                         bias=minus_round[:, 0:1]).then_inc(F["pT"], 1)

            def ffn_step(s, b):
                ftanh(s + 1, 1 - b)
                fx_copy(s + 2)
                fu_copy(s + 1, 1 - b)
                fp_copy(s - 1)

            skewed(act, ffn_step, SEQ, 2, 2)

        @block.vector
        def _(dve):
            done = [0]

            def after_me(ins):
                done[0] += 1
                ins.then_inc(prep, 1)
                dve.wait_ge(prep, done[0])

            dve.wait_ge(attn_in, ATTN_LOADS)
            dve.tensor_copy(ident_b[:], ident[:])
            for c in range(4):
                dve.tensor_copy(causal_b[:, c, :], causal[:])
            dve.tensor_scalar(bq_scaled[:], bqk[:, 0:KD], DH ** -0.5, None, ALU.mult)
            after_me(dve.reciprocal(kvinv[:], kvs[:]))
            v = wst[:].rearrange("p (u n) -> p u n", u=2)
            dve.wait_ge(ffn_in, 16)
            dve.tensor_reduce(wabs[:, 0:2], v, AX.X, ALU.add, apply_absolute_value=True).then_inc(wst_summed, 1)

            def table_rows(t):
                dve.wait_ge(tok_in, 48)
                for n in range(4 * t, 4 * t + 4):
                    dve.wait_ge(t_row_psum, n + 1)
                    if n >= 4:
                        dve.wait_ge(t_store[n % 4], 16 * (n // 4))
                    dve.tensor_tensor(trow[:, n % 4, :], PS[:, 2 + n % 2, 0:D], tb2[:], ALU.add).then_inc(t_row, 1)

            table_rows(0)
            for k in range(KD):
                dve.tensor_scalar(wqkv[0][:, k, :], wqkv[0][:, k, :], gln[:, k:k + 1], None, ALU.mult)
            for n, (w, k, lo, hi) in enumerate(((wqkv[1], 0, 0, 512), (wqkv[1], 0, 512, 768), (wqkv[1], 1, 0, 512),
                                                (wqkv[1], 1, 512, 768), (wout[1], 0, 0, 256), (wout[1], 1, 0, 256))):
                dve.wait_ge(prep_psum, n + 1)
                dve.scalar_tensor_tensor(w[:, k, lo:hi], PS[:, 4 + n % 3, 0:hi - lo], 2.0, w[:, k, lo:hi], ALU.mult, ALU.add)\
                   .then_inc(lora_added, 1)
            dve.wait_ge(ffn_in, 32)
            dve.tensor_reduce(wabs[:, 2:4], v, AX.X, ALU.add, apply_absolute_value=True).then_inc(wst_summed, 1)
            dve.wait_ge(wst_summed, 2)
            after_me(dve.tensor_tensor(wabs[:, 0:2], wabs[:, 0:2], wabs[:, 2:4], ALU.add))
            after_me(dve.memset(wabs[:, 3:4], 0.0))
            dve.wait_ge(ffn_in, 48)
            dve.tensor_reduce(wabs[:, 2:3], wst[:], AX.X, ALU.add, apply_absolute_value=True).then_inc(wst_summed, 1)
            dve.wait_ge(prep_psum, 7)
            after_me(dve.tensor_scalar(wmean[:], PS[:, 7, 0:4], 1.0 / (D * INNER), EPS, ALU.mult, ALU.max))
            after_me(dve.reciprocal(wscale[:], wmean[:]))
            after_me(dve.reciprocal(winv[:], wscale[:]))
            after_me(dve.tensor_scalar(winv[:, 3:4], winv[:, 0:1], winv[:, 1:2], 0.5, ALU.mult, ALU.mult))

            def ternary(dst, src, which):
                after_me(dve.tensor_scalar(src, src, wscale[:, which:which + 1], ROUND, ALU.mult, ALU.add))
                after_me(dve.tensor_scalar(src, src, -ROUND, 1.0, ALU.add, ALU.min))
                return dve.tensor_scalar(dst, src, -1.0, None, ALU.max)

            for n in range(KD):
                if n:
                    table_rows(1)
                dve.wait_ge(ffn_in, 64 + 16 * n)
                after_me(ternary(wgu_q[:, n, 0:INNER], wst[:, 0:INNER], 0))
                ternary(wgu_q[:, n, INNER:], wst[:, INNER:], 1).then_inc(wst_quantized, 1)
            table_rows(2)
            dve.wait_ge(ffn_in, 96)
            ternary(wdn_q[:].rearrange("p k n -> p (k n)"), wst[:], 2).then_inc(weights_ready, 1)

            for t in range(3, TG):
                table_rows(t)

            def attention(layer):
                a = A[layer]
                if layer == 0:
                    for t in range(4):
                        dve.wait_ge(t_store[t], 16 * TG)
                dve.memset(kT[:].bitcast(F32).rearrange("p b k r h n -> p (b k r h n)"), 0.0)
                dve.memset(V[:].rearrange("p b h n -> p (b h n)"), 1.0).then_inc(space_set, 1)
                dve.wait_ge(space_set, layer + 1)

                def norm(s, b):
                    if has(s):
                        seen(dve, a["rstd"], s)
                        seen(dve, a["xT_psum"], s - 1)
                        dve.tensor_scalar(xn[:], row(resid, s), mv[:, b, 0:1], rstd[:, b:b + 1], ALU.subtract, ALU.mult).then_inc(a["xn"], 1)

                def o_norm(s):
                    seen(dve, a["stats"], s + 5)
                    if has(s):
                        seen(dve, a["o2_psum"], s)
                        o = PS[:, 7].rearrange("p (h n) -> p h n", n=SLOT)
                        dve.reciprocal(rden[:], o[:, :, DH]).then_inc(a["rden"], 1)
                        seen(dve, a["rden"], s)
                        seen(dve, a["oT_psum"], s - 1)
                        dve.tensor_tensor(onrm[:].rearrange("p (h n) -> p h n", n=DH), o[:, :, 0:DH],
                                          spread(rden[:], DH),
                                          ALU.mult).then_inc(a["onrm"], 1)

                def largest(s, b):
                    if has(s):
                        seen(dve, a["s_psum"], s)
                        sc = PS[:, 0:4].rearrange("p r (c k) -> p (r c) k", k=P)
                        dve.tensor_reduce(rmax[:], sc, AX.X, ALU.max).then_inc(a["rmax"], 1)

                def shift(s, b):
                    if has(s):
                        sc = PS[:, 0:4].rearrange("p r (c k) -> p (r c) k", k=P)
                        seen(dve, a["rmax"], s)
                        seen(dve, a["o_psum"], s - 2)
                        dve.tensor_tensor(prob[:, b], sc, spread(rmax[:], P),
                                          ALU.subtract).then_inc(a["shifted"], 1)

                def values(s, b):
                    if has(s) and layer == 0:
                        seen(dve, a["v_psum"], s)
                        dve.tensor_copy(kv[:, b, D:2 * D], PS[:, 7, 0:D]).then_inc(a["v_read"], 1)

                def fake_quant(s, b):
                    if has(s) and layer == 1:
                        t = kv[:, b, :]
                        seen(dve, a["qk_psum"], s)
                        seen(dve, a["q"], s)
                        seen(dve, a["split"], s - 2)
                        for k in range(KD):
                            ins = dve.tensor_scalar(kv[:, b, k * P:(k + 1) * P], PS[:, 6, D + k * P:D + (k + 1) * P],
                                                    bqk[:, KD + k:KD + k + 1], None, ALU.add)
                        ins.then_inc(a["k_read"], 1)
                        seen(dve, a["v_psum"], s)
                        dve.tensor_tensor(kv[:, b, D:2 * D], PS[:, 7, 0:D], bv[:], ALU.add).then_inc(a["v_read"], 1)

                def fake_quant_end(s, b):
                    if has(s) and layer == 1:
                        t = kv[:, b, :]
                        seen(dve, a["k_read"], s)
                        seen(dve, a["v_read"], s)
                        dve.tensor_scalar(t, t, kvinv[:, 0:1], kvz[:, 0:1], ALU.mult, ALU.add).then_inc(a["chain"], 1)
                        seen(dve, a["chain"], s, 1, 3)
                        dve.tensor_scalar(t, t, 0.0, 255.0, ALU.max, ALU.min).then_inc(a["chain"], 1)
                        seen(dve, a["chain"], s, 2, 3)
                        dve.tensor_scalar(t, t, ROUND, -ROUND, ALU.add, ALU.add).then_inc(a["chain"], 1)
                        seen(dve, a["chain"], s, 3, 3)
                        dve.tensor_scalar(t, t, kvz[:, 0:1], kvs[:, 0:1], ALU.subtract, ALU.mult).then_inc(a["k"], 1)

                def v_store(s, b):
                    if has(s):
                        seen(dve, a["o_psum"], s - 2)
                        if layer == 0:
                            seen(dve, a["v_read"], s)
                        else:
                            seen(dve, a["k"], s)
                        dve.tensor_copy(V[:, b, :, 0:DH], kv[:, b, D:2 * D].rearrange("p (h n) -> p h n", n=DH)).then_inc(a["v"], 1)

                def add(s):
                    if has(s):
                        seen(dve, a["y_psum"], s)
                        if layer == 1:
                            seen(dve, a["biased"], s)
                        dve.tensor_tensor(row(resid, s), row(resid, s), PS[:, 7, 0:D], ALU.add).then_inc(a["resid"], 1)

                def routed_add(s, b, c):
                    if has(s) and layer == 1:
                        if c == 0:
                            dve.wait_ge(y_gathered[b], pair(s) * 32 + 32)
                        else:
                            seen(dve, y_added, s)
                        g = gate[:, c, s:s + 1] if isinstance(s, int) else gate[:, c, bass.ds(s, 1)]
                        dve.scalar_tensor_tensor(row(resid, s), yrow[:, b, c, :], g, row(resid, s), ALU.mult, ALU.add)\
                           .then_inc(y_added if c == 0 else y_added_all, 1)

                def moments(s, b):
                    if has(s):
                        if layer == 0:
                            dve.wait_ge(gathered[b], pair(s) * 16 + 16)
                        dve.bn_stats(stats[:], row(resid, s)).then_inc(a["stats"], 1)

                def moments_end(s, b):
                    if has(s):
                        dve.bn_aggr(mv[:, b, :], stats[:]).then_inc(a["aggr"], 1)
                        seen(dve, a["aggr"], s)
                        if layer == 0:
                            dve.tensor_scalar(varp[:, b:b + 1], mv[:, b, 1:2], 1.0 + EPS, EPS * EPS, ALU.mult, ALU.add).then_inc(a["var"], 1)
                        else:
                            dve.tensor_scalar(varp[:, b:b + 1], mv[:, b, 1:2], EPS, None, ALU.add).then_inc(a["var"], 1)

                def step(s, b):
                    if layer == 1:
                        seen(dve, y_added_all, s + 3)
                    norm(s + 2, b)
                    moments(s + 3, 1 - b)
                    o_norm(s - 2)
                    moments_end(s + 3, 1 - b)
                    largest(s, b)
                    values(s + 2, b)
                    fake_quant(s + 2, b)
                    shift(s, b)
                    fake_quant_end(s + 2, b)
                    routed_add(s + 4, b, 0)
                    v_store(s + 1, 1 - b)
                    add(s - 2)
                    routed_add(s + 4, b, 1)

                skewed(dve, step, SEQ, 4, 2)

            attention(0)

            dve.wait_ge(A[0]["resid"], SEQ)

            def moments(g):
                if has(g, G):
                    for t in range(GS):
                        ins = dve.bn_stats(mstats[:, t, :], row(resid, g * GS + t))
                    ins.then_inc(M["stats"], 1)

            def moments_end(g, b):
                if has(g, G):
                    for t in range(GS):
                        ins = dve.bn_aggr(mmv[:, b, t, :], mstats[:, t, :])
                    ins.then_inc(M["aggr"], 1)
                    seen(dve, M["aggr"], g, 1, 1, G)
                    dve.tensor_scalar(mvar[:], mmv[:, b, :, 1], EPS, None, ALU.add).then_inc(M["var"], 1)

            def norm(g, b):
                seen(dve, M["stats"], g + 1, 1, 1, G)
                if has(g, G):
                    seen(dve, M["rstd"], g, 1, 1, G)
                    seen(dve, M["xn"], g - 1, GS, GS, G)
                    seen(dve, M["xT_psum"], g - 2, KD, KD, G)
                    seen(dve, M["kept"], g - 2, 1, 1, G)
                    for t in range(GS):
                        dve.tensor_scalar(staged[:, b, t, :], row(resid, g * GS + t), mmv[:, b, t, 0:1], mrstd[:, t:t + 1],
                                          ALU.subtract, ALU.mult).then_inc(M["xn"], 1)

            def route_step(g, b):
                moments(g + 1)
                norm(g, b)
                moments_end(g + 1, 1 - b)

            skewed(dve, route_step, G, 1, 2)

            n_chain = [0]

            def then(ins):
                n_chain[0] += 1
                ins.then_inc(M["chain"], 1)
                dve.wait_ge(M["chain"], n_chain[0])

            def over(v, n=E):
                return spread(v, n)

            def each(v, n):
                return v.unsqueeze(1).broadcast_to([P, n, v.shape[1]])

            def total(dst, src):
                then(dve.tensor_reduce(dst, src, AX.X, ALU.add))

            for i, v in enumerate(counts):
                ins = dve.memset(v[:, 0:PAD, :].rearrange("p s e -> p (s e)"), 0.0)
            for i, v in enumerate(tiles):
                ins = dve.memset(v[:, 0:E], 0.0)
            then(ins)
            logits = PS[:, 5, 0:SEQ * E].rearrange("p (s e) -> p s e", e=E)
            def choose():
                dve.wait_ge(M["route_psum"], G)
                then(dve.tensor_reduce(per_token[:], logits, AX.X, ALU.max))
                dve.tensor_tensor(score[:], logits, over(per_token[:]), ALU.subtract).then_inc(M["route_max"], 1)
                dve.wait_ge(M["route_exp"], 1)
                total(per_token[:], score[:])
                then(dve.reciprocal(per_token[:], per_token[:]))
                then(dve.tensor_tensor(score[:], score[:], over(per_token[:]), ALU.mult))
                then(dve.tensor_tensor(biased, score[:], each(gbias[:], SEQ), ALU.add))
                for turn in range(TOP):
                    then(dve.tensor_reduce(per_token[:], biased, AX.X, ALU.max))
                    then(dve.tensor_tensor(tie, biased, over(per_token[:]), ALU.is_equal))
                    then(dve.tensor_tensor(tie, tie, each(rank[:], SEQ), ALU.mult))
                    then(dve.tensor_reduce(per_token[:], tie, AX.X, ALU.max))
                    then(dve.tensor_tensor(chosen[turn][:], tie, over(per_token[:]), ALU.is_equal))
                    if turn == 0:
                        then(dve.scalar_tensor_tensor(biased, chosen[0][:], -BIG, biased, ALU.mult, ALU.add))
                dve.tensor_tensor(selected[:], chosen[0][:], chosen[1][:], ALU.add).then_inc(M["selected"], 1)

            def count():
                for c in range(TOP):
                    then(dve.tensor_tensor(tie, chosen[c][:], score[:], ALU.mult))
                    total(gate[:, c, :], tie)
                g_all = gate[:].rearrange("p c s -> p (c s)")
                then(dve.tensor_scalar(g_all, g_all, 0.5, None, ALU.mult))
                dve.wait_ge(M["prefix_psum"], 1)
                then(dve.tensor_copy(selected[:].rearrange("p s e -> p (s e)"), PS[:, 4, 0:SEQ * E]))
                dve.tensor_copy(counts[0][:, PAD:, :].rearrange("p s e -> p (s e)"), PS[:, 4, SEQ * E:2 * SEQ * E]).then_inc(prefix_read, 1)
                dve.wait_ge(prefix_read, 1)
                at, d, flip = 0, 1, 1
                while d < SEQ:
                    then(dve.tensor_tensor(counts[flip][:, PAD:, :], counts[at][:, PAD:, :], counts[at][:, PAD - d:PAD + SEQ - d, :], ALU.add))
                    at, flip, d = flip, 3 - flip, 2 * d
                return counts[at]

            def set_places(upto):
                then(dve.tensor_scalar(tiles[0][:, E:], upto[:, PAD + SEQ - 1, :], 1.0 / P, (P / 2 - 0.5) / P, ALU.mult, ALU.add))
                then(dve.tensor_scalar(tiles[0][:, E:], tiles[0][:, E:], ROUND, -ROUND, ALU.add, ALU.add))
                t_at, d, flip = 0, 1, 1
                while d < E:
                    then(dve.tensor_tensor(tiles[flip][:, E:], tiles[t_at][:, E:], tiles[t_at][:, E - d:2 * E - d], ALU.add))
                    t_at, flip, d = flip, 3 - flip, 2 * d
                ends = tiles[t_at]
                then(dve.tensor_tensor(start[:], ends[:, E:], tiles[0][:, E:], ALU.subtract))
                then(dve.tensor_scalar(start[:], start[:], float(P), None, ALU.mult))
                then(dve.tensor_tensor(biased, upto[:, PAD:, :], selected[:], ALU.add))
                then(dve.tensor_tensor(biased, biased, counts[0][:, PAD:, :], ALU.subtract))
                then(dve.tensor_tensor(biased, biased, each(start[:], SEQ), ALU.add))
                for c in range(TOP):
                    then(dve.tensor_tensor(tie, chosen[c][:], biased, ALU.mult))
                    total(place_f[:, :, c], tie)
                then(dve.tensor_copy(place[:].rearrange("p s c -> p (s c)"), place_f[:].rearrange("p s c -> p (s c)")))
                dve.wait_ge(tile_in[0], 16)
                then(dve.tensor_tensor(beyond, over(tile_no[:], E - 1), each(ends[:, E:2 * E - 1], NT), ALU.is_ge))
                total(tile_expert_f[:], beyond)
                dve.tensor_copy(tile_expert[:], tile_expert_f[0:1, :]).then_inc(M["routed"], 1)

            def shared_add(g, e):
                if not has(g, G):
                    return
                for t in range(GS):
                    if t % 2 == 0:
                        seen(dve, S["down_psum"], g, e * 2 + t // 2 + 1, NS * 2, G)
                    r = row(resid, g * GS + t)
                    dve.scalar_tensor_tensor(r, PS[:, 4 + t // 2, t % 2 * D:(t % 2 + 1) * D], 0.5, r,
                                             ALU.mult, ALU.add).then_inc(S["resid"], 1)

            dve.wait_ge(M["kept"], G)

            def stage(g, b):
                if has(g, G):
                    if has(g - 2, G):
                        seen(dve, S["xT_psum"], g - 2, KD, KD, G)
                    src = mxn[:, g * GS:(g + 1) * GS] if isinstance(g, int) else mxn[:, bass.ds(g * GS, GS)]
                    dve.tensor_copy(staged[:, b].rearrange("p t d -> p (t d)"), src.rearrange("p t d -> p (t d)")).then_inc(S["staged"], 1)

            def shared_step(g, b):
                first = isinstance(g, int) and g == 0
                if first:
                    choose()
                if has(g, G):
                    for e in range(NS):
                        if first and e:
                            upto = count()
                        for h in range(KI):
                            n = e * KI + h
                            seen(dve, S["tanh"], g, n + 1, NS * KI, G)
                            dve.scalar_tensor_tensor(act_[:, h, :], tnh[:, h, :], 1.0, PS[:, 2 * h], ALU.add, ALU.mult).then_inc(S["half"], 1)
                            seen(dve, S["half"], g, n + 1, NS * KI, G)
                            if h == 0:
                                seen(dve, S["down_psum"], g - 1, (e + 1) * 2, NS * 2, G)
                            dve.tensor_tensor(hT[:, e % 2, h, :], act_[:, h, :], PS[:, 2 * h + 1], ALU.mult).then_inc(S["hT"], 1)
                        if e:
                            shared_add(g, e - 1)
                        else:
                            shared_add(g - 1, NS - 1)
                else:
                    shared_add(g - 1, NS - 1)
                stage(g + 2, b)
                if first:
                    set_places(upto)

            skewed(dve, shared_step, G, 2, 1)

            def tile_hidden(j, b):
                if has(j, NT):
                    seen(dve, T["tanh"], j, 1, 1, NT)
                    dve.scalar_tensor_tensor(eact[:, b, :], etanh[:, b, :], 1.0, PS[:, b, 0:INTER], ALU.add, ALU.mult).then_inc(T["half"], 1)
                    seen(dve, T["half"], j, 1, 1, NT)
                    seen(dve, T["hT_psum"], j - 2, 1, 1, NT)
                    dve.tensor_tensor(eh[:, b, :], eact[:, b, :], PS[:, b, INTER:2 * INTER], ALU.mult).then_inc(T["h"], 1)

            def tile_result(j, b):
                if has(j, NT):
                    seen(dve, T["down_psum"], j, 1, 1, NT)
                    if has(j - 2, NT):
                        dve.wait_ge(tile_out[b], pair(j) * 16)
                    dve.tensor_copy(ey[:, b, :], PS[:, 4 + b, 0:D]).then_inc(T["y"], 1)

            def tile_step(j, b):
                tile_hidden(j + 2, b)
                tile_result(j, b)

            skewed(dve, tile_step, NT, 3, 2)
            for b in range(2):
                dve.wait_ge(tile_out[b], 16 * NT // 2)

            attention(1)

            def ffn_moments(s, b):
                if has(s):
                    dve.bn_stats(fstats[:], row(resid, s)).then_inc(F["stats"], 1)

            def ffn_moments_end(s, b):
                if has(s):
                    dve.bn_aggr(fmv[:, b, :], fstats[:]).then_inc(F["aggr"], 1)
                    seen(dve, F["aggr"], s)
                    dve.tensor_scalar(fvar[:, b:b + 1], fmv[:, b, 1:2], EPS, None, ALU.add).then_inc(F["var"], 1)

            def ffn_quant(s, b):
                if not has(s):
                    return
                n = [0]

                def then(ins):
                    n[0] += 1
                    ins.then_inc(F["chain"], 1)
                    seen(dve, F["chain"], s, n[0], CH)

                seen(dve, F["rstd"], s)
                then(dve.tensor_scalar(fxn[:], row(resid, s), fmv[:, b, 0:1], frstd[:, b:b + 1], ALU.subtract, ALU.mult))
                then(dve.tensor_reduce(fs[:, b, 0:1], fxn[:], AX.X, ALU.max, apply_absolute_value=True))
                then(dve.tensor_scalar(fs[:, b, 1:2], fs[:, b, 0:1], EPS, 1.0 / 127.0, ALU.max, ALU.mult))
                then(dve.reciprocal(fs[:, b, 2:3], fs[:, b, 1:2]))
                seen(dve, F["q_psum"], s - 2)
                dve.tensor_scalar(fq[:, b, :], fxn[:], fs[:, b, 2:3], ROUND, ALU.mult, ALU.add).then_inc(F["q"], 1)
                then(dve.tensor_scalar(fs[:, b, 3:4], fs[:, b, 1:2], winv[:, 0:1], 0.5, ALU.mult, ALU.mult))
                assert n[0] == CH
                dve.tensor_scalar(fs[:, b, 4:5], fs[:, b, 1:2], fs[:, b, 1:2], winv[:, 3:4], ALU.mult, ALU.mult).then_inc(F["scales"], 1)

            def ffn_half(s, b):
                seen(dve, F["stats"], s + 3)
                if has(s):
                    seen(dve, F["tanh"], s)
                    seen(dve, F["prod"], s - 2)
                    dve.scalar_tensor_tensor(fh[:, b, :], ft[:], 1.0, PS[:, 0:2].rearrange("p a n -> p (a n)"),
                                             ALU.add, ALU.mult).then_inc(F["half"], 1)
                    dve.tensor_copy(fm[:, b, 0:1], fs[:, b, 4:5]).then_inc(F["kept"], 1)

            def ffn_quant_hidden(s, b):
                if not has(s):
                    return
                n = [0]

                def then(ins):
                    n[0] += 1
                    ins.then_inc(F["pchain"], 1)
                    seen(dve, F["pchain"], s, n[0], PR)

                seen(dve, F["resid"], s - 2)
                seen(dve, F["pq"], s - 2)
                seen(dve, F["kept"], s)
                seen(dve, F["prod"], s)
                then(dve.tensor_reduce(fm[:, b, 1:2], fp[:, b, :], AX.X, ALU.max, apply_absolute_value=True))
                then(dve.tensor_scalar(fm[:, b, 1:2], fm[:, b, 1:2], fm[:, b, 0:1], EPS, ALU.mult, ALU.max))
                then(dve.reciprocal(fm[:, b, 2:3], fm[:, b, 1:2]))
                then(dve.tensor_scalar(fm[:, b, 2:3], fm[:, b, 2:3], fm[:, b, 0:1], 127.0, ALU.mult, ALU.mult))
                assert n[0] == PR

            def ffn_add(s, b):
                if has(s):
                    seen(dve, F["down_psum"], s)
                    dve.tensor_scalar(fm[:, b, 1:2], fm[:, b, 1:2], winv[:, 2:3], 1.0 / 127.0, ALU.mult, ALU.mult).then_inc(F["fscale"], 1)
                    seen(dve, F["fscale"], s)
                    dve.scalar_tensor_tensor(row(resid, s), PS[:, 7, 0:D], fm[:, b, 1:2], row(resid, s), ALU.mult, ALU.add).then_inc(F["resid"], 1)

            def ffn_step(s, b):
                ffn_half(s, b)
                ffn_quant(s + 2, b)
                ffn_moments_end(s + 3, 1 - b)
                ffn_moments(s + 4, b)
                ffn_quant_hidden(s - 1, 1 - b)
                ffn_add(s - 2, b)

            skewed(dve, ffn_step, SEQ, 4, 2)


def _inputs(v):
    import numpy as np

    f = {k: np.asarray(a) for k, a in v.items()}
    def rows(a):
        return np.broadcast_to(np.asarray(a).reshape(1, -1), (P, np.asarray(a).size))

    def cols(a):
        return np.asarray(a).reshape(-1, P).T

    def experts(a, b):
        return np.concatenate([a.transpose(0, 2, 1), b.transpose(0, 2, 1)], axis=2)

    inter = f["L0_ffn_w1"].shape[1]
    sw1, sw3 = (f[n].reshape(-1, inter, D) for n in ("L0_ffn_sw1", "L0_ffn_sw3"))
    sw2 = f["L0_ffn_sw2"].reshape(D, -1, inter).transpose(1, 2, 0)
    n_exp = f["L0_ffn_gate_w"].shape[0]
    at = np.arange(P)
    return {
        "x_t": f["x"].T,
        "codebook_t": f["L0_tok_codebook"].T,
        "tok_w1": f["L0_tok_W1"],
        "tok_b1": cols(f["L0_tok_b1"]),
        "tok_w2": f["L0_tok_W2"],
        "tok_b2": rows(f["L0_tok_b2"]),
        "g_ln": cols(f["L0_attn_g_ln"]),
        "w_qkv0": np.concatenate([f["L0_attn_Wq"], f["L0_attn_Wkv"]], axis=1),
        "w_out0": f["L0_attn_Wo"],
        "gate_wt": f["L0_ffn_gate_w"].T,
        "gate_bias": rows(f["L0_ffn_gate_bias"]),
        "w13": np.concatenate([experts(f["L0_ffn_w1"], f["L0_ffn_w3"]), experts(sw1, sw3)]),
        "w2": np.concatenate([f["L0_ffn_w2"].transpose(0, 2, 1), sw2]),
        "w_qkv1": f["L1_attn_w_attn"],
        "b_qk": cols(f["L1_attn_b_attn"][:2 * D]),
        "b_v": rows(f["L1_attn_b_attn"][2 * D:]),
        "la_attn_t": f["L1_attn_la_attn"].T,
        "lb_attn": f["L1_attn_lb_attn"],
        "w_proj": f["L1_attn_w_proj"],
        "b_proj": rows(f["L1_attn_b_proj"]),
        "la_proj_t": f["L1_attn_la_proj"].T,
        "lb_proj": f["L1_attn_lb_proj"],
        "kv_scale": rows(f["L1_attn_kv_scale"]),
        "kv_zero": rows(f["L1_attn_kv_zero_point"]),
        "w_gu": np.concatenate([f["L1_ffn_w_gate"].T, f["L1_ffn_w_up"].T], axis=1),
        "w_down": f["L1_ffn_w_down"].T,
        "ident_in": np.eye(P, dtype=np.float32),
        "causal_in": np.where(at[None, :] > at[:, None], np.float32(MASKED), np.float32(0)),
        "rank_in": np.tile(np.arange(n_exp, 0, -1, dtype=np.float32), (P, 1)),
        "earlier_in": (at[:, None] < at[None, :]).astype(np.float32),
        "tile_no_in": np.tile(np.arange(2 * f["x"].shape[0] + n_exp, dtype=np.float32), (P, 1)),
    }


def kernel(**inputs):
    import numpy as np
    from concourse import bacc
    from concourse.bass_utils import run_bass_kernel_spmd

    nc = bacc.Bacc("TRN2", target_bir_lowering=False, num_devices=1)
    arrays = {f"in_{n}": np.ascontiguousarray(a) for n, a in _inputs(inputs).items()}
    args = [nc.dram_tensor(n, a.shape, mybir.dt.from_np(a.dtype), kind="ExternalInput").ap() for n, a in arrays.items()]
    n_seq, length = inputs["x"].shape
    out = nc.dram_tensor("out_0", (n_seq, length, D), F32, kind="ExternalOutput").ap()
    build(nc, *args, out)
    r = run_bass_kernel_spmd(nc, [arrays], core_ids=[0])
    return r.results[0]["out_0"]
```
